# Optimizing a Trainium2 kernel written in Bass

```python
import numpy as np
import jax
import jax.numpy as jnp

def _softmax(x, axis=-1):
    return jax.nn.softmax(x, axis=axis)

def _gelu(x):
    return jax.nn.gelu(x, approximate=True)

def _silu(x):
    return jax.nn.silu(x)

def _sigmoid(x):
    return jax.nn.sigmoid(x)

def _layernorm(x, axis=-1, eps=1e-05):
    m = jnp.mean(x, axis=axis, keepdims=True)
    v = jnp.var(x, axis=axis, keepdims=True)
    return (x - m) / jnp.sqrt(v + eps)

def _scatter_add(tgt, idx, src, axis=0):
    return tgt.at[idx].add(src)

def _segment_sum(src, seg, n):
    return jax.ops.segment_sum(src, seg, n)
kernel_name = 'mk_flamingo_gated_d4_seqx_r4_c91007'

def setup_inputs(seed: int=0):
    np.random.seed(seed)
    _w = jnp.asarray

    def _rec_inputs():
        import jax
        import jax.numpy as jnp
        _rk = jax.random.key(seed)
        x = 7.22e-05 + 1 * jax.random.normal(jax.random.fold_in(_rk, 1), (8, 112, 256), jnp.float32)
        _lenS = 112 - jax.random.randint(jax.random.fold_in(_rk, 7), (8,), 0, max(1, 112 // 4) + 1, jnp.int32)
        _lenS2 = 375 - jax.random.randint(jax.random.fold_in(_rk, 8), (8,), 0, max(1, 375 // 4) + 1, jnp.int32)
        _ctx_1024P = jax.random.normal(jax.random.fold_in(_rk, 11), (8, 16, 256), jnp.float32)
        _ctx_1024c = jax.random.dirichlet(jax.random.fold_in(_rk, 511), 0.3 * jnp.ones((16,), jnp.float32), (8, 375))
        _ctx_1024t = jnp.einsum('bsk,bkd->bsd', _ctx_1024c, _ctx_1024P)
        _ctx_1024t = _ctx_1024t * jax.lax.rsqrt(jnp.mean(jnp.square(_ctx_1024t)) + 1e-12) * 0.953939
        ctx_1024 = 2.81802e-05 + 1.00001 * (_ctx_1024t + 0.3 * jax.random.normal(jax.random.fold_in(_rk, 611), (8, 375, 256), jnp.float32))
        _validS = jnp.arange(112)[None, :] < _lenS[:, None]
        _validS2 = jnp.arange(375)[None, :] < _lenS2[:, None]
        _causal = jnp.tril(jnp.ones((112, 112), dtype=bool))
        mask_1xSxS2_ik0 = jnp.where(jnp.broadcast_to(_validS2[0:1, None, :], (1, 112, 375)), 0, 1).astype(jnp.int32)
        mask_BxSxS2_ik1 = jnp.where(jnp.broadcast_to(_validS2[:, None, :], (8, 112, 375)), 1, 0).astype(jnp.int32)
        _g = jax.random.normal(jax.random.fold_in(_rk, 9001), (2, 4), jnp.float32)
        _g = jnp.sign(_g) * jnp.maximum(jnp.abs(_g), 1.0) + (_g == 0) * 1.0
        g_xattn = _g[0]
        g_ffn = _g[1]
        return (x, ctx_1024, mask_1xSxS2_ik0, mask_BxSxS2_ik1, g_xattn, g_ffn)
    x, ctx_1024, mask_1xSxS2_ik0, mask_BxSxS2_ik1, g_xattn, g_ffn = _rec_inputs()

    def _L0_xattn_setup():
        import jax, jax.numpy as jnp
        import numpy as np
        B, NT, NM, C, H, FF = (8, 256, 512, 256, 8, 1024)

        def _ln(x, g, b):
            m = x.mean(-1, keepdims=True)
            v = jnp.mean((x - m) ** 2, axis=-1, keepdims=True)
            return (x - m) / jnp.sqrt(v + 1e-05) * g + b
        key = jax.random.key(seed)
        ks = jax.random.split(key, 8)
        w = lambda k, shape, s=0.02: jax.random.normal(k, shape, dtype=jnp.float32) * s
        return {'tgt': jax.random.normal(ks[0], (B, NT, C), dtype=jnp.float32), 'memory': jax.random.normal(ks[1], (B, NM, C), dtype=jnp.float32), 'qkv_w': w(ks[2], (3 * C, C)), 'qkv_b': jnp.zeros((3 * C,), jnp.float32), 'sa_out_w': w(ks[3], (C, C)), 'sa_out_b': jnp.zeros((C,), jnp.float32), 'in_proj_w': w(ks[4], (3 * C, C)), 'in_proj_b': jnp.zeros((3 * C,), jnp.float32), 'mha_out_w': w(ks[5], (C, C)), 'mha_out_b': jnp.zeros((C,), jnp.float32), 'lin1_w': w(ks[6], (FF, C)), 'lin1_b': jnp.zeros((FF,), jnp.float32), 'lin2_w': w(ks[7], (C, FF)), 'lin2_b': jnp.zeros((C,), jnp.float32), 'ln1_g': jnp.ones((C,), jnp.float32), 'ln1_b': jnp.zeros((C,), jnp.float32), 'ln2_g': jnp.ones((C,), jnp.float32), 'ln2_b': jnp.zeros((C,), jnp.float32), 'ln3_g': jnp.ones((C,), jnp.float32), 'ln3_b': jnp.zeros((C,), jnp.float32)}
    _L0_xattn_all = _L0_xattn_setup()
    _L0_xattn_in = {k: v for k, v in _L0_xattn_all.items() if k in ('qkv_w', 'qkv_b', 'sa_out_w', 'sa_out_b', 'in_proj_w', 'in_proj_b', 'mha_out_w', 'mha_out_b', 'lin1_w', 'lin1_b', 'lin2_w', 'lin2_b', 'ln1_g', 'ln1_b', 'ln2_g', 'ln2_b', 'ln3_g', 'ln3_b')}
    del _L0_xattn_all

    def _L0_ffn_setup():
        import jax, jax.numpy as jnp
        import numpy as np
        DIM = 256

        def _reference_tuple_inner(x, W_r, W_k, W_v, mu_r, mu_k):
            B, T, C = x.shape
            x_prev = jnp.concatenate([jnp.zeros((B, 1, C), x.dtype), x[:, :-1, :]], axis=1)
            xr = mu_r * x + (1.0 - mu_r) * x_prev
            xk = mu_k * x + (1.0 - mu_k) * x_prev
            r = jax.nn.sigmoid(jnp.einsum('btc,dc->btd', xr, W_r))
            k = jnp.einsum('btc,dc->btd', xk, W_k)
            k_act = jnp.square(jax.nn.relu(k))
            out = r * jnp.einsum('btc,dc->btd', k_act, W_v)
            new_state = x[:, -1, :]
            return (out, new_state)
        key = jax.random.key(seed)
        ks = jax.random.split(key, 6)
        B, T, C = (8, 512, DIM)
        x = jax.random.normal(ks[0], (B, T, C), dtype=jnp.float32)
        s = 1.0 / np.sqrt(C)
        W_r = jax.random.uniform(ks[1], (C, C), jnp.float32, -s, s)
        W_k = jax.random.uniform(ks[2], (C, C), jnp.float32, -s, s)
        W_v = jax.random.uniform(ks[3], (C, C), jnp.float32, -s, s)
        mu_r = jax.random.uniform(ks[4], (C,), jnp.float32)
        mu_k = jax.random.uniform(ks[5], (C,), jnp.float32)
        return {'x': x, 'W_r': W_r, 'W_k': W_k, 'W_v': W_v, 'mu_r': mu_r, 'mu_k': mu_k}
    _L0_ffn_all = _L0_ffn_setup()
    _L0_ffn_in = {k: v for k, v in _L0_ffn_all.items() if k in ('W_r', 'W_k', 'W_v', 'mu_r', 'mu_k')}
    del _L0_ffn_all

    def _L1_xattn_setup():
        import jax, jax.numpy as jnp
        import numpy as np
        from math import sqrt
        B, S, E, D, O = (8, 512, 256, 128, 256)
        key = jax.random.key(seed)
        ks = jax.random.split(key, 12)
        inp = {'query': jax.random.normal(ks[0], (B, S, E), jnp.float32), 'key': jax.random.normal(ks[1], (B, S, E), jnp.float32), 'value': jax.random.normal(ks[2], (B, S, E), jnp.float32), 'mask': jnp.tril(jnp.ones((S, S), jnp.int32))[None, :, :], 'Wq': jax.random.normal(ks[3], (E, D), jnp.float32) / sqrt(E), 'bq': jnp.zeros((D,), jnp.float32), 'Wk': jax.random.normal(ks[4], (E, D), jnp.float32) / sqrt(E), 'bk': jnp.zeros((D,), jnp.float32), 'Wv': jax.random.normal(ks[5], (E, D), jnp.float32) / sqrt(E), 'bv': jnp.zeros((D,), jnp.float32), 'Wo': jax.random.normal(ks[6], (D, O), jnp.float32) / sqrt(D), 'bo': jnp.zeros((O,), jnp.float32)}
        return inp
    _L1_xattn_all = _L1_xattn_setup()
    _L1_xattn_in = {k: v for k, v in _L1_xattn_all.items() if k in ('Wq', 'bq', 'Wk', 'bk', 'Wv', 'bv', 'Wo', 'bo')}
    del _L1_xattn_all

    def _L1_ffn_setup():
        import jax, jax.numpy as jnp
        import numpy as np
        B, S, D = (4, 1024, 256)
        E, F_EXP = (16, 512)
        F_C = 2.0
        F_SH = 512
        key = jax.random.key(seed)
        ks = jax.random.split(key, 8)
        s = 0.02
        return {'hidden_states': jax.random.normal(ks[0], (B, S, D), jnp.float32), 'gate_w': jax.random.normal(ks[1], (E, D), jnp.float32) * s, 'Wg': jax.random.normal(ks[2], (E, F_EXP, D), jnp.float32) * s, 'Wu': jax.random.normal(ks[3], (E, F_EXP, D), jnp.float32) * s, 'Wd': jax.random.normal(ks[4], (E, D, F_EXP), jnp.float32) * s, 'Ws_g': jax.random.normal(ks[5], (F_SH, D), jnp.float32) * s, 'Ws_u': jax.random.normal(ks[6], (F_SH, D), jnp.float32) * s, 'Ws_d': jax.random.normal(ks[7], (D, F_SH), jnp.float32) * s}
    _L1_ffn_all = _L1_ffn_setup()
    _L1_ffn_in = {k: v for k, v in _L1_ffn_all.items() if k in ('gate_w', 'Wg', 'Wu', 'Wd', 'Ws_g', 'Ws_u', 'Ws_d')}
    del _L1_ffn_all

    def _L2_xattn_setup():
        import jax, jax.numpy as jnp
        import numpy as np
        N_HEADS = 16
        D_MODEL = 256
        D_K = D_MODEL // N_HEADS
        B, S = (4, 512)
        NEG_INF = -1000000000.0

        def _proj(x, W, b):
            y = jnp.einsum('bsd,ed->bse', x, W) + b
            Bx, Sx, _ = y.shape
            return y.reshape(Bx, Sx, N_HEADS, D_K).transpose(0, 2, 1, 3)
        key = jax.random.key(seed)
        ks = jax.random.split(key, 12)
        scale = 1.0 / np.sqrt(D_MODEL)
        inp = {'query': jax.random.normal(ks[0], (B, S, D_MODEL), jnp.float32), 'key': jax.random.normal(ks[1], (B, S, D_MODEL), jnp.float32), 'value': jax.random.normal(ks[2], (B, S, D_MODEL), jnp.float32), 'mask': jax.random.randint(ks[3], (B, S, S), 0, 2, jnp.int32), 'Wq': jax.random.normal(ks[4], (D_MODEL, D_MODEL), jnp.float32) * scale, 'bq': jnp.zeros((D_MODEL,), jnp.float32), 'Wk': jax.random.normal(ks[5], (D_MODEL, D_MODEL), jnp.float32) * scale, 'bk': jnp.zeros((D_MODEL,), jnp.float32), 'Wv': jax.random.normal(ks[6], (D_MODEL, D_MODEL), jnp.float32) * scale, 'bv': jnp.zeros((D_MODEL,), jnp.float32), 'Wo': jax.random.normal(ks[7], (D_MODEL, D_MODEL), jnp.float32) * scale, 'bo': jnp.zeros((D_MODEL,), jnp.float32)}
        return inp
    _L2_xattn_all = _L2_xattn_setup()
    _L2_xattn_in = {k: v for k, v in _L2_xattn_all.items() if k in ('Wq', 'bq', 'Wk', 'bk', 'Wv', 'bv', 'Wo', 'bo')}
    del _L2_xattn_all

    def _L2_ffn_setup():
        import jax, jax.numpy as jnp
        import numpy as np
        B, S, D, H, L, E, K = (4, 256, 256, 16, 2, 8, 2)
        DFF = 4 * D

        def _ln(x, w, b):
            m = x.mean(-1, keepdims=True)
            v = x.var(-1, keepdims=True)
            return (x - m) / jnp.sqrt(v + 1e-05) * w + b

        def _attn(x, wq, wk, wv, wo, bq, bk, bv, bo):
            Bb, T, C = x.shape
            hd = C // H
            q = (x @ wq + bq).reshape(Bb, T, H, hd).transpose(0, 2, 1, 3)
            k = (x @ wk + bk).reshape(Bb, T, H, hd).transpose(0, 2, 1, 3)
            v = (x @ wv + bv).reshape(Bb, T, H, hd).transpose(0, 2, 1, 3)
            att = jnp.einsum('bhqd,bhkd->bhqk', q, k) * hd ** (-0.5)
            causal = jnp.tril(jnp.ones((T, T), bool))
            att = jnp.where(causal, att, -jnp.inf)
            att = jax.nn.softmax(att, axis=-1)
            y = jnp.einsum('bhqk,bhkd->bhqd', att, v).transpose(0, 2, 1, 3).reshape(Bb, T, C)
            return y @ wo + bo

        def _ffn(h, w1, b1, w2, b2):
            return jax.nn.gelu(h @ w1 + b1, approximate=False) @ w2 + b2

        def _combine_weights(logits):
            vals, idx = jax.lax.top_k(logits, K)
            w = jax.nn.softmax(vals, axis=-1)
            onehot = (idx[..., None] == jnp.arange(E)).astype(w.dtype)
            return jnp.sum(w[..., None] * onehot, axis=-2)

        def _token_moe(h, gw, gb, w1, b1, w2, b2):
            cw = _combine_weights(h @ gw + gb)
            out = jnp.zeros_like(h)
            for e in range(E):
                out = out + _ffn(h, w1[e], b1[e], w2[e], b2[e]) * cw[..., e:e + 1]
            return out

        def _seq_moe(h, gw, gb, w1, b1, w2, b2):
            cw = _combine_weights(h.mean(axis=1) @ gw + gb)
            out = jnp.zeros_like(h)
            for e in range(E):
                out = out + _ffn(h, w1[e], b1[e], w2[e], b2[e]) * cw[:, e, None, None]
            return out
        key = jax.random.key(seed)
        ks = jax.random.split(key, 9)
        n = lambda k, shp: jax.random.normal(k, shp, dtype=jnp.float32) * 0.02
        return {'x': jax.random.normal(ks[0], (B, S, D), dtype=jnp.float32), 'ln1_w': jnp.ones((L, D), jnp.float32), 'ln1_b': jnp.zeros((L, D), jnp.float32), 'ln2_w': jnp.ones((L, D), jnp.float32), 'ln2_b': jnp.zeros((L, D), jnp.float32), 'wq': n(ks[1], (L, D, D)), 'wk': n(ks[2], (L, D, D)), 'wv': n(ks[3], (L, D, D)), 'wo': n(ks[4], (L, D, D)), 'bq': jnp.zeros((L, D), jnp.float32), 'bk': jnp.zeros((L, D), jnp.float32), 'bv': jnp.zeros((L, D), jnp.float32), 'bo': jnp.zeros((L, D), jnp.float32), 'gate_w': n(ks[5], (L, D, E)), 'gate_b': jnp.zeros((L, E), jnp.float32), 'e_w1': n(ks[6], (L, E, D, DFF)), 'e_b1': jnp.zeros((L, E, DFF), jnp.float32), 'e_w2': n(ks[7], (L, E, DFF, D)), 'e_b2': jnp.zeros((L, E, D), jnp.float32)}
    _L2_ffn_all = _L2_ffn_setup()
    _L2_ffn_in = {k: v for k, v in _L2_ffn_all.items() if k in ('ln1_w', 'ln1_b', 'ln2_w', 'ln2_b', 'wq', 'wk', 'wv', 'wo', 'bq', 'bk', 'bv', 'bo', 'gate_w', 'gate_b', 'e_w1', 'e_b1', 'e_w2', 'e_b2')}
    del _L2_ffn_all

    def _L3_xattn_setup():
        import jax, jax.numpy as jnp
        import numpy as np
        HIDDEN = 256
        HEADS = 16
        HEAD_DIM = 64
        key = jax.random.key(seed)
        ks = jax.random.split(key, 7)
        B, Q, K = (2, 512, 1024)
        s = 1.0 / np.sqrt(HIDDEN)
        return {'query': jax.random.normal(ks[0], (B, Q, HIDDEN), dtype=jnp.float32), 'key': jax.random.normal(ks[1], (B, K, HIDDEN), dtype=jnp.float32), 'value': jax.random.normal(ks[2], (B, K, HIDDEN), dtype=jnp.float32), 'w_q': jax.random.normal(ks[3], (HIDDEN, HEADS * HEAD_DIM), dtype=jnp.float32) * s, 'w_k': jax.random.normal(ks[4], (HIDDEN, HEADS * HEAD_DIM), dtype=jnp.float32) * s, 'w_v': jax.random.normal(ks[5], (HIDDEN, HEADS * HEAD_DIM), dtype=jnp.float32) * s, 'w_o': jax.random.normal(ks[6], (HEADS * HEAD_DIM, HIDDEN), dtype=jnp.float32) * s}
    _L3_xattn_all = _L3_xattn_setup()
    _L3_xattn_in = {k: v for k, v in _L3_xattn_all.items() if k in ('w_q', 'w_k', 'w_v', 'w_o')}
    del _L3_xattn_all

    def _L3_ffn_setup():
        import jax, jax.numpy as jnp
        import numpy as np
        EPS = 1e-05

        def act_quant(x):
            scale = 127.0 / jnp.clip(jnp.max(jnp.abs(x), axis=-1, keepdims=True), EPS, None)
            q = jnp.clip(jnp.round(x * scale), -128.0, 127.0) / scale
            return x + jax.lax.stop_gradient(q - x)

        def weight_quant(w):
            scale = 1.0 / jnp.clip(jnp.mean(jnp.abs(w)), EPS, None)
            q = jnp.clip(jnp.round(w * scale), -1.0, 1.0) / scale
            return w + jax.lax.stop_gradient(q - w)

        def bitlinear(x, w):
            return act_quant(x) @ weight_quant(w).T
        key = jax.random.key(seed)
        k1, k2, k3, k4 = jax.random.split(key, 4)
        H, I = (256, 1024)
        B, S = (4, 1024)
        init = 0.02
        x = jax.random.normal(k1, (B, S, H), dtype=jnp.float32)
        w_gate = jax.random.normal(k2, (I, H), dtype=jnp.float32) * init
        w_up = jax.random.normal(k3, (I, H), dtype=jnp.float32) * init
        w_down = jax.random.normal(k4, (H, I), dtype=jnp.float32) * init
        return {'x': x, 'w_gate': w_gate, 'w_up': w_up, 'w_down': w_down}
    _L3_ffn_all = _L3_ffn_setup()
    _L3_ffn_in = {k: v for k, v in _L3_ffn_all.items() if k in ('w_gate', 'w_up', 'w_down')}
    del _L3_ffn_all
    return {'x': x, 'ctx_1024': ctx_1024, 'mask_1xSxS2_ik0': mask_1xSxS2_ik0, 'mask_BxSxS2_ik1': mask_BxSxS2_ik1, 'g_xattn': g_xattn, 'g_ffn': g_ffn, 'L0_xattn_qkv_w': _L0_xattn_in['qkv_w'], 'L0_xattn_qkv_b': _L0_xattn_in['qkv_b'], 'L0_xattn_sa_out_w': _L0_xattn_in['sa_out_w'], 'L0_xattn_sa_out_b': _L0_xattn_in['sa_out_b'], 'L0_xattn_in_proj_w': _L0_xattn_in['in_proj_w'], 'L0_xattn_in_proj_b': _L0_xattn_in['in_proj_b'], 'L0_xattn_mha_out_w': _L0_xattn_in['mha_out_w'], 'L0_xattn_mha_out_b': _L0_xattn_in['mha_out_b'], 'L0_xattn_lin1_w': _L0_xattn_in['lin1_w'], 'L0_xattn_lin1_b': _L0_xattn_in['lin1_b'], 'L0_xattn_lin2_w': _L0_xattn_in['lin2_w'], 'L0_xattn_lin2_b': _L0_xattn_in['lin2_b'], 'L0_xattn_ln1_g': _L0_xattn_in['ln1_g'], 'L0_xattn_ln1_b': _L0_xattn_in['ln1_b'], 'L0_xattn_ln2_g': _L0_xattn_in['ln2_g'], 'L0_xattn_ln2_b': _L0_xattn_in['ln2_b'], 'L0_xattn_ln3_g': _L0_xattn_in['ln3_g'], 'L0_xattn_ln3_b': _L0_xattn_in['ln3_b'], 'L0_ffn_W_r': _L0_ffn_in['W_r'], 'L0_ffn_W_k': _L0_ffn_in['W_k'], 'L0_ffn_W_v': _L0_ffn_in['W_v'], 'L0_ffn_mu_r': _L0_ffn_in['mu_r'], 'L0_ffn_mu_k': _L0_ffn_in['mu_k'], 'L1_xattn_Wq': _L1_xattn_in['Wq'], 'L1_xattn_bq': _L1_xattn_in['bq'], 'L1_xattn_Wk': _L1_xattn_in['Wk'], 'L1_xattn_bk': _L1_xattn_in['bk'], 'L1_xattn_Wv': _L1_xattn_in['Wv'], 'L1_xattn_bv': _L1_xattn_in['bv'], 'L1_xattn_Wo': _L1_xattn_in['Wo'], 'L1_xattn_bo': _L1_xattn_in['bo'], 'L1_ffn_gate_w': _L1_ffn_in['gate_w'], 'L1_ffn_Wg': _L1_ffn_in['Wg'], 'L1_ffn_Wu': _L1_ffn_in['Wu'], 'L1_ffn_Wd': _L1_ffn_in['Wd'], 'L1_ffn_Ws_g': _L1_ffn_in['Ws_g'], 'L1_ffn_Ws_u': _L1_ffn_in['Ws_u'], 'L1_ffn_Ws_d': _L1_ffn_in['Ws_d'], 'L2_xattn_Wq': _L2_xattn_in['Wq'], 'L2_xattn_bq': _L2_xattn_in['bq'], 'L2_xattn_Wk': _L2_xattn_in['Wk'], 'L2_xattn_bk': _L2_xattn_in['bk'], 'L2_xattn_Wv': _L2_xattn_in['Wv'], 'L2_xattn_bv': _L2_xattn_in['bv'], 'L2_xattn_Wo': _L2_xattn_in['Wo'], 'L2_xattn_bo': _L2_xattn_in['bo'], 'L2_ffn_ln1_w': _L2_ffn_in['ln1_w'], 'L2_ffn_ln1_b': _L2_ffn_in['ln1_b'], 'L2_ffn_ln2_w': _L2_ffn_in['ln2_w'], 'L2_ffn_ln2_b': _L2_ffn_in['ln2_b'], 'L2_ffn_wq': _L2_ffn_in['wq'], 'L2_ffn_wk': _L2_ffn_in['wk'], 'L2_ffn_wv': _L2_ffn_in['wv'], 'L2_ffn_wo': _L2_ffn_in['wo'], 'L2_ffn_bq': _L2_ffn_in['bq'], 'L2_ffn_bk': _L2_ffn_in['bk'], 'L2_ffn_bv': _L2_ffn_in['bv'], 'L2_ffn_bo': _L2_ffn_in['bo'], 'L2_ffn_gate_w': _L2_ffn_in['gate_w'], 'L2_ffn_gate_b': _L2_ffn_in['gate_b'], 'L2_ffn_e_w1': _L2_ffn_in['e_w1'], 'L2_ffn_e_b1': _L2_ffn_in['e_b1'], 'L2_ffn_e_w2': _L2_ffn_in['e_w2'], 'L2_ffn_e_b2': _L2_ffn_in['e_b2'], 'L3_xattn_w_q': _L3_xattn_in['w_q'], 'L3_xattn_w_k': _L3_xattn_in['w_k'], 'L3_xattn_w_v': _L3_xattn_in['w_v'], 'L3_xattn_w_o': _L3_xattn_in['w_o'], 'L3_ffn_w_gate': _L3_ffn_in['w_gate'], 'L3_ffn_w_up': _L3_ffn_in['w_up'], 'L3_ffn_w_down': _L3_ffn_in['w_down']}

def reference(x, ctx_1024, mask_1xSxS2_ik0, mask_BxSxS2_ik1, g_xattn, g_ffn, L0_xattn_qkv_w, L0_xattn_qkv_b, L0_xattn_sa_out_w, L0_xattn_sa_out_b, L0_xattn_in_proj_w, L0_xattn_in_proj_b, L0_xattn_mha_out_w, L0_xattn_mha_out_b, L0_xattn_lin1_w, L0_xattn_lin1_b, L0_xattn_lin2_w, L0_xattn_lin2_b, L0_xattn_ln1_g, L0_xattn_ln1_b, L0_xattn_ln2_g, L0_xattn_ln2_b, L0_xattn_ln3_g, L0_xattn_ln3_b, L0_ffn_W_r, L0_ffn_W_k, L0_ffn_W_v, L0_ffn_mu_r, L0_ffn_mu_k, L1_xattn_Wq, L1_xattn_bq, L1_xattn_Wk, L1_xattn_bk, L1_xattn_Wv, L1_xattn_bv, L1_xattn_Wo, L1_xattn_bo, L1_ffn_gate_w, L1_ffn_Wg, L1_ffn_Wu, L1_ffn_Wd, L1_ffn_Ws_g, L1_ffn_Ws_u, L1_ffn_Ws_d, L2_xattn_Wq, L2_xattn_bq, L2_xattn_Wk, L2_xattn_bk, L2_xattn_Wv, L2_xattn_bv, L2_xattn_Wo, L2_xattn_bo, L2_ffn_ln1_w, L2_ffn_ln1_b, L2_ffn_ln2_w, L2_ffn_ln2_b, L2_ffn_wq, L2_ffn_wk, L2_ffn_wv, L2_ffn_wo, L2_ffn_bq, L2_ffn_bk, L2_ffn_bv, L2_ffn_bo, L2_ffn_gate_w, L2_ffn_gate_b, L2_ffn_e_w1, L2_ffn_e_b1, L2_ffn_e_w2, L2_ffn_e_b2, L3_xattn_w_q, L3_xattn_w_k, L3_xattn_w_v, L3_xattn_w_o, L3_ffn_w_gate, L3_ffn_w_up, L3_ffn_w_down):
    import jax
    import jax.numpy as jnp

    def _L0_xattn_ref(tgt, memory, qkv_w, qkv_b, sa_out_w, sa_out_b, in_proj_w, in_proj_b, mha_out_w, mha_out_b, lin1_w, lin1_b, lin2_w, lin2_b, ln1_g, ln1_b, ln2_g, ln2_b, ln3_g, ln3_b):
        import jax, jax.numpy as jnp
        import numpy as np
        B, NT, NM, C, H, FF = (8, 256, 512, 256, 8, 1024)

        def _ln(x, g, b):
            m = x.mean(-1, keepdims=True)
            v = jnp.mean((x - m) ** 2, axis=-1, keepdims=True)
            return (x - m) / jnp.sqrt(v + 1e-05) * g + b
        Bx, N, Cx = tgt.shape
        qkv = tgt @ qkv_w.T + qkv_b
        q, k, v = jnp.split(qkv, 3, axis=-1)
        scores = jnp.einsum('bnc,bmc->bnm', q, k) * jnp.sqrt(jnp.float32(Cx))
        diag = jnp.eye(N, dtype=bool)
        scores = jnp.where(diag[None, :, :], scores, -jnp.inf)
        attn = jax.nn.softmax(scores, axis=-1)
        sa = jnp.einsum('bnm,bmc->bnc', attn, v) @ sa_out_w.T + sa_out_b
        x = _ln(tgt + sa, ln1_g, ln1_b)
        d = Cx // H
        wq, wk, wv = jnp.split(in_proj_w, 3, axis=0)
        bq, bk, bv = jnp.split(in_proj_b, 3, axis=0)
        qh = (x @ wq.T + bq).reshape(Bx, N, H, d).transpose(0, 2, 1, 3)
        kh = (memory @ wk.T + bk).reshape(Bx, -1, H, d).transpose(0, 2, 1, 3)
        vh = (memory @ wv.T + bv).reshape(Bx, -1, H, d).transpose(0, 2, 1, 3)
        a = jax.nn.softmax(jnp.einsum('bhnd,bhmd->bhnm', qh, kh) / jnp.sqrt(jnp.float32(d)), axis=-1)
        ca = jnp.einsum('bhnm,bhmd->bhnd', a, vh).transpose(0, 2, 1, 3).reshape(Bx, N, Cx)
        ca = ca @ mha_out_w.T + mha_out_b
        x = _ln(x + ca, ln2_g, ln2_b)
        ff = jax.nn.relu(x @ lin1_w.T + lin1_b) @ lin2_w.T + lin2_b
        return _ln(x + ff, ln3_g, ln3_b)

    def _L0_ffn_ref(x, W_r, W_k, W_v, mu_r, mu_k):
        import jax, jax.numpy as jnp
        import numpy as np
        DIM = 256

        def _reference_tuple_inner(x, W_r, W_k, W_v, mu_r, mu_k):
            B, T, C = x.shape
            x_prev = jnp.concatenate([jnp.zeros((B, 1, C), x.dtype), x[:, :-1, :]], axis=1)
            xr = mu_r * x + (1.0 - mu_r) * x_prev
            xk = mu_k * x + (1.0 - mu_k) * x_prev
            r = jax.nn.sigmoid(jnp.einsum('btc,dc->btd', xr, W_r))
            k = jnp.einsum('btc,dc->btd', xk, W_k)
            k_act = jnp.square(jax.nn.relu(k))
            out = r * jnp.einsum('btc,dc->btd', k_act, W_v)
            new_state = x[:, -1, :]
            return (out, new_state)
        return _reference_tuple_inner(x, W_r, W_k, W_v, mu_r, mu_k)[0]

    def _L1_xattn_ref(query, key, value, mask, Wq, bq, Wk, bk, Wv, bv, Wo, bo):
        import jax, jax.numpy as jnp
        import numpy as np
        from math import sqrt
        B, S, E, D, O = (8, 512, 256, 128, 256)
        q = jnp.einsum('bse,ed->bsd', query, Wq) + bq
        k = jnp.einsum('bse,ed->bsd', key, Wk) + bk
        v = jnp.einsum('bse,ed->bsd', value, Wv) + bv
        scale = 1.0 / sqrt(q.shape[-1])
        scores = jnp.einsum('bqd,bkd->bqk', q, k) * scale
        scores = jnp.where(mask == 0, -jnp.inf, scores)
        weights = jax.nn.softmax(scores, axis=-1)
        weights = jnp.nan_to_num(weights)
        out = jnp.einsum('bqk,bkd->bqd', weights, v)
        return jnp.einsum('bqd,do->bqo', out, Wo) + bo

    def _L1_ffn_ref(hidden_states, gate_w, Wg, Wu, Wd, Ws_g, Ws_u, Ws_d):
        import jax, jax.numpy as jnp
        import numpy as np
        B, S, D = (4, 1024, 256)
        E, F_EXP = (16, 512)
        F_C = 2.0
        F_SH = 512
        b, s, d = hidden_states.shape
        e = gate_w.shape[0]
        cap = int(s * F_C / e)
        logits = jnp.einsum('bsd,ed->bse', hidden_states, gate_w)
        scores = jax.nn.softmax(logits, axis=-1).transpose(0, 2, 1)
        topk_w, topk_idx = jax.lax.top_k(scores, cap)
        x_tok = jnp.take_along_axis(hidden_states[:, None, :, :], topk_idx[..., None], axis=2)
        g = jnp.einsum('becd,efd->becf', x_tok, Wg)
        u = jnp.einsum('becd,efd->becf', x_tok, Wu)
        h = jax.nn.gelu(g, approximate=False) * u
        eo = jnp.einsum('becf,edf->becd', h, Wd) * topk_w[..., None]
        offs = (jnp.arange(b) * s)[:, None, None]
        flat_idx = (topk_idx + offs).reshape(-1)
        flat = jnp.zeros((b * s, d), hidden_states.dtype)
        flat = flat.at[flat_idx].add(eo.reshape(-1, d))
        out = flat.reshape(b, s, d)
        gs = jnp.einsum('bsd,fd->bsf', hidden_states, Ws_g)
        us = jnp.einsum('bsd,fd->bsf', hidden_states, Ws_u)
        shared = jnp.einsum('bsf,df->bsd', jax.nn.gelu(gs, approximate=False) * us, Ws_d)
        return out + shared

    def _L2_xattn_ref(query, key, value, mask, Wq, bq, Wk, bk, Wv, bv, Wo, bo):
        import jax, jax.numpy as jnp
        import numpy as np
        N_HEADS = 16
        D_MODEL = 256
        D_K = D_MODEL // N_HEADS
        B, S = (4, 512)
        NEG_INF = -1000000000.0

        def _proj(x, W, b):
            y = jnp.einsum('bsd,ed->bse', x, W) + b
            Bx, Sx, _ = y.shape
            return y.reshape(Bx, Sx, N_HEADS, D_K).transpose(0, 2, 1, 3)
        q = _proj(query, Wq, bq)
        k = _proj(key, Wk, bk)
        v = _proj(value, Wv, bv)
        scores = jnp.einsum('bhqd,bhkd->bhqk', q, k) / jnp.sqrt(jnp.float32(D_K))
        m = mask[:, None, :, :]
        scores = jnp.where(m == 0, jnp.float32(NEG_INF), scores)
        p_attn = jax.nn.softmax(scores, axis=-1)
        x = jnp.einsum('bhqk,bhkd->bhqd', p_attn, v)
        x = x.transpose(0, 2, 1, 3).reshape(query.shape[0], -1, D_MODEL)
        return jnp.einsum('bsd,ed->bse', x, Wo) + bo

    def _L2_ffn_ref(x, ln1_w, ln1_b, ln2_w, ln2_b, wq, wk, wv, wo, bq, bk, bv, bo, gate_w, gate_b, e_w1, e_b1, e_w2, e_b2):
        import jax, jax.numpy as jnp
        import numpy as np
        B, S, D, H, L, E, K = (4, 256, 256, 16, 2, 8, 2)
        DFF = 4 * D

        def _ln(x, w, b):
            m = x.mean(-1, keepdims=True)
            v = x.var(-1, keepdims=True)
            return (x - m) / jnp.sqrt(v + 1e-05) * w + b

        def _attn(x, wq, wk, wv, wo, bq, bk, bv, bo):
            Bb, T, C = x.shape
            hd = C // H
            q = (x @ wq + bq).reshape(Bb, T, H, hd).transpose(0, 2, 1, 3)
            k = (x @ wk + bk).reshape(Bb, T, H, hd).transpose(0, 2, 1, 3)
            v = (x @ wv + bv).reshape(Bb, T, H, hd).transpose(0, 2, 1, 3)
            att = jnp.einsum('bhqd,bhkd->bhqk', q, k) * hd ** (-0.5)
            causal = jnp.tril(jnp.ones((T, T), bool))
            att = jnp.where(causal, att, -jnp.inf)
            att = jax.nn.softmax(att, axis=-1)
            y = jnp.einsum('bhqk,bhkd->bhqd', att, v).transpose(0, 2, 1, 3).reshape(Bb, T, C)
            return y @ wo + bo

        def _ffn(h, w1, b1, w2, b2):
            return jax.nn.gelu(h @ w1 + b1, approximate=False) @ w2 + b2

        def _combine_weights(logits):
            vals, idx = jax.lax.top_k(logits, K)
            w = jax.nn.softmax(vals, axis=-1)
            onehot = (idx[..., None] == jnp.arange(E)).astype(w.dtype)
            return jnp.sum(w[..., None] * onehot, axis=-2)

        def _token_moe(h, gw, gb, w1, b1, w2, b2):
            cw = _combine_weights(h @ gw + gb)
            out = jnp.zeros_like(h)
            for e in range(E):
                out = out + _ffn(h, w1[e], b1[e], w2[e], b2[e]) * cw[..., e:e + 1]
            return out

        def _seq_moe(h, gw, gb, w1, b1, w2, b2):
            cw = _combine_weights(h.mean(axis=1) @ gw + gb)
            out = jnp.zeros_like(h)
            for e in range(E):
                out = out + _ffn(h, w1[e], b1[e], w2[e], b2[e]) * cw[:, e, None, None]
            return out
        for l in range(L):
            x = x + _attn(_ln(x, ln1_w[l], ln1_b[l]), wq[l], wk[l], wv[l], wo[l], bq[l], bk[l], bv[l], bo[l])
            h = _ln(x, ln2_w[l], ln2_b[l])
            moe = _token_moe if l % 2 == 0 else _seq_moe
            x = x + moe(h, gate_w[l], gate_b[l], e_w1[l], e_b1[l], e_w2[l], e_b2[l])
        return x

    def _L3_xattn_ref(query, key, value, w_q, w_k, w_v, w_o):
        import jax, jax.numpy as jnp
        import numpy as np
        HIDDEN = 256
        HEADS = 16
        HEAD_DIM = 64
        B, Q, _ = query.shape
        Kl = key.shape[1]
        scale = HEAD_DIM ** (-0.5)
        q = (query @ w_q).reshape(B, Q, HEADS, HEAD_DIM).transpose(0, 2, 1, 3)
        k = (key @ w_k).reshape(B, Kl, HEADS, HEAD_DIM).transpose(0, 2, 1, 3)
        v = (value @ w_v).reshape(B, Kl, HEADS, HEAD_DIM).transpose(0, 2, 1, 3)
        scores = jnp.einsum('bhqd,bhkd->bhqk', q, k) * scale
        attn = jax.nn.softmax(scores, axis=-1)
        out = jnp.einsum('bhqk,bhkd->bhqd', attn, v)
        out = out.transpose(0, 2, 1, 3).reshape(B, Q, HEADS * HEAD_DIM)
        return out @ w_o

    def _L3_ffn_ref(x, w_gate, w_up, w_down):
        import jax, jax.numpy as jnp
        import numpy as np
        EPS = 1e-05

        def act_quant(x):
            scale = 127.0 / jnp.clip(jnp.max(jnp.abs(x), axis=-1, keepdims=True), EPS, None)
            q = jnp.clip(jnp.round(x * scale), -128.0, 127.0) / scale
            return x + jax.lax.stop_gradient(q - x)

        def weight_quant(w):
            scale = 1.0 / jnp.clip(jnp.mean(jnp.abs(w)), EPS, None)
            q = jnp.clip(jnp.round(w * scale), -1.0, 1.0) / scale
            return w + jax.lax.stop_gradient(q - w)

        def bitlinear(x, w):
            return act_quant(x) @ weight_quant(w).T
        g = bitlinear(x, w_gate)
        u = bitlinear(x, w_up)
        h = jnp.square(jax.nn.relu(g)) * u
        return bitlinear(h, w_down)
    x = x + jnp.tanh(g_xattn[0]) * _L0_xattn_ref(_layernorm(x, axis=-1), ctx_1024, L0_xattn_qkv_w, L0_xattn_qkv_b, L0_xattn_sa_out_w, L0_xattn_sa_out_b, L0_xattn_in_proj_w, L0_xattn_in_proj_b, L0_xattn_mha_out_w, L0_xattn_mha_out_b, L0_xattn_lin1_w, L0_xattn_lin1_b, L0_xattn_lin2_w, L0_xattn_lin2_b, L0_xattn_ln1_g, L0_xattn_ln1_b, L0_xattn_ln2_g, L0_xattn_ln2_b, L0_xattn_ln3_g, L0_xattn_ln3_b)
    x = x + jnp.tanh(g_ffn[0]) * _L0_ffn_ref(_layernorm(x, axis=-1), L0_ffn_W_r, L0_ffn_W_k, L0_ffn_W_v, L0_ffn_mu_r, L0_ffn_mu_k)
    x = x + jnp.tanh(g_xattn[1]) * _L1_xattn_ref(_layernorm(x, axis=-1), ctx_1024, ctx_1024, mask_1xSxS2_ik0, L1_xattn_Wq, L1_xattn_bq, L1_xattn_Wk, L1_xattn_bk, L1_xattn_Wv, L1_xattn_bv, L1_xattn_Wo, L1_xattn_bo)
    x = x + jnp.tanh(g_ffn[1]) * _L1_ffn_ref(_layernorm(x, axis=-1), L1_ffn_gate_w, L1_ffn_Wg, L1_ffn_Wu, L1_ffn_Wd, L1_ffn_Ws_g, L1_ffn_Ws_u, L1_ffn_Ws_d)
    x = x + jnp.tanh(g_xattn[2]) * _L2_xattn_ref(_layernorm(x, axis=-1), ctx_1024, ctx_1024, mask_BxSxS2_ik1, L2_xattn_Wq, L2_xattn_bq, L2_xattn_Wk, L2_xattn_bk, L2_xattn_Wv, L2_xattn_bv, L2_xattn_Wo, L2_xattn_bo)
    x = x + jnp.tanh(g_ffn[2]) * _L2_ffn_ref(_layernorm(x, axis=-1), L2_ffn_ln1_w, L2_ffn_ln1_b, L2_ffn_ln2_w, L2_ffn_ln2_b, L2_ffn_wq, L2_ffn_wk, L2_ffn_wv, L2_ffn_wo, L2_ffn_bq, L2_ffn_bk, L2_ffn_bv, L2_ffn_bo, L2_ffn_gate_w, L2_ffn_gate_b, L2_ffn_e_w1, L2_ffn_e_b1, L2_ffn_e_w2, L2_ffn_e_b2)
    x = x + jnp.tanh(g_xattn[3]) * _L3_xattn_ref(_layernorm(x, axis=-1), ctx_1024, ctx_1024, L3_xattn_w_q, L3_xattn_w_k, L3_xattn_w_v, L3_xattn_w_o)
    x = x + jnp.tanh(g_ffn[3]) * _L3_ffn_ref(_layernorm(x, axis=-1), L3_ffn_w_gate, L3_ffn_w_up, L3_ffn_w_down)
    return x

_drawn_inputs = setup_inputs


def setup_inputs(seed=0):
    import zlib

    import numpy as np

    out = dict(_drawn_inputs(seed))
    spreads = {'L0_xattn_qkv_b': (0.0, 0.625),
     'L0_xattn_sa_out_b': (0.0, 0.1),
     'L0_xattn_in_proj_b': (0.0, 0.526),
     'L0_xattn_mha_out_b': (0.0, 0.1),
     'L0_xattn_lin1_b': (0.0, 0.457),
     'L0_xattn_lin2_b': (0.0, 0.1),
     'L0_xattn_ln1_g': (1.0, 0.2),
     'L0_xattn_ln1_b': (0.0, 0.1),
     'L0_xattn_ln2_g': (1.0, 0.2),
     'L0_xattn_ln2_b': (0.0, 0.1),
     'L0_xattn_ln3_g': (1.0, 0.2),
     'L0_xattn_ln3_b': (0.0, 0.1),
     'L1_xattn_bq': (0.0, 0.554),
     'L1_xattn_bk': (0.0, 2.0),
     'L1_xattn_bv': (0.0, 0.1),
     'L1_xattn_bo': (0.0, 0.1),
     'L2_xattn_bq': (0.0, 2.0),
     'L2_xattn_bk': (0.0, 2.0),
     'L2_xattn_bv': (0.0, 0.359),
     'L2_xattn_bo': (0.0, 0.355),
     'L2_ffn_ln1_w': (1.0, 0.6),
     'L2_ffn_ln1_b': (0.0, 0.8),
     'L2_ffn_ln2_w': (1.0, 0.6),
     'L2_ffn_ln2_b': (0.0, 1.15),
     'L2_ffn_bq': (0.0, 2.0),
     'L2_ffn_bk': (0.0, 2.0),
     'L2_ffn_bv': (0.0, 0.288),
     'L2_ffn_bo': (0.0, 0.1),
     'L2_ffn_gate_b': (0.0, 0.1),
     'L2_ffn_e_b1': (0.0, 0.396),
     'L2_ffn_e_b2': (0.0, 0.297)}
    factors = {'g_ffn': 8.0,
     'L0_ffn_W_r': 6.559,
     'L0_ffn_mu_r': 8.0,
     'L0_ffn_mu_k': 3.222,
     'L1_ffn_gate_w': 8.0,
     'L1_ffn_Wg': 8.0,
     'L1_ffn_Wu': 8.0,
     'L1_ffn_Wd': 8.0,
     'L1_ffn_Ws_g': 4.953,
     'L1_ffn_Ws_u': 4.736,
     'L1_ffn_Ws_d': 4.624,
     'L2_ffn_wq': 8.0,
     'L2_ffn_wk': 8.0,
     'L3_ffn_w_gate': 8.0,
     'L3_ffn_w_up': 6.348,
     'L3_ffn_w_down': 6.228}
    for name, (base, spread) in spreads.items():
        noise = np.random.default_rng([zlib.crc32(name.encode()), seed]).standard_normal(out[name].shape)
        drawn = base * np.exp(spread * noise) if base else spread * noise
        out[name] = jnp.asarray(drawn.astype(out[name].dtype))
    for name, factor in factors.items():
        out[name] = (out[name] * factor).astype(out[name].dtype)
    return out
```

```python
from contextlib import ExitStack

import numpy as np

import concourse.bass as bass
from concourse import mybir

F32 = mybir.dt.float32
BF16 = mybir.dt.bfloat16
I32 = mybir.dt.int32
U32 = mybir.dt.uint32
ALU = mybir.AluOpType
ACT = mybir.ActivationFunctionType
AX_X = mybir.AxisListType.X

B, T, C = 8, 112, 256
S2 = 375
P = 128
KC = C // P
LANES = 4
ITERS = B // LANES
TOP2 = 2
SEQ_ITEMS = LANES * TOP2
SEQ_SLOTS = 4
KEY_TILES, KEY_W = 3, S2 // 3
E1, FE = 16, 512
CAP = T * 2 // E1
HALF_E = E1 // 2
E2, FF = 8, 1024
HALF_T = 4 * T
EPS = 1e-5
BIG = 1.0e30
ROUND = 1.5 * 2.0 ** 23

ROWS = ["sa_b", "ln1_g", "ln1_b", "l0_bv", "l0_bo", "ln2_g", "ln2_b", "lin2_b", "ln3_g", "ln3_b",
        "l1_bv", "l1_bo", "l2_bv", "l2_bo"]
ROWS2 = ["ln1_w", "ln1_b", "bv", "bo", "ln2_w", "ln2_b"]
COLS = {"l0_sv": 2, "l0_bq": 2, "l0_bk": 2, "lin1_b": 8, "mu_r": 2, "mu_k": 2, "l1_bq": 1, "l1_bk": 1,
        "l2_bq": 2, "l2_bk": 2, "f0_bq": 2, "f0_bk": 2, "f1_bq": 2, "f1_bk": 2,
        "head_rows": 14}


class Signal:

    def __init__(self, sem, base, times, lanes):
        self.sem, self.base, self.times, self.lanes = sem, base, times, lanes

    def at(self, it, r=0, j=0):
        return self.sem, it * (self.times * self.lanes) + (self.base + r * self.lanes + j + 1)


def phase_signals(known, make, turns, one, lanes, times):
    signals = {}
    for name, n in times.items():
        if not n:
            continue
        width = 1 if name in one else lanes
        if name not in known:
            known[name] = [make(name), 0]
        sem, base = known[name]
        signals[name] = Signal(sem, base, n, width)
        known[name][1] = base + turns * n * width
    return signals


class Attention:

    def __init__(self, tiles, heads, d, keys, key_tiles, wq, wk, wv, bq=None, bk=None, bv=None,
                 mask=None, guard=False):
        self.tiles, self.heads, self.d, self.keys, self.key_tiles = tiles, heads, d, keys, key_tiles
        self.key_w = keys // key_tiles
        self.batch = min(4, heads)
        self.masks = None if heads == 1 else {8: 0, 4: 8, 2: 12}[heads]
        self.group = 4 if key_tiles == 1 else 1
        self.groups = heads // self.group
        self.wq, self.wk, self.wv, self.bq, self.bk, self.bv = wq, wk, wv, bq, bk, bv
        self.mask, self.guard, self.scale = mask, guard, float(d) ** -0.5


def flamingo(nc, A, out):
    ctx = ExitStack()
    with ctx:
        def sb(name, shape, dt=F32):
            return ctx.enter_context(nc.sbuf_tensor(name, shape, dt))

        def make(name):
            return ctx.enter_context(nc.semaphore(name))

        known = {}

        def phase(turns, one=(), lanes=LANES, **times):
            return phase_signals(known, make, turns, one, lanes, times)

        bank = [ctx.enter_context(nc.psum_tensor(f"bank{i}", [P, 512], F32)) for i in range(8)]
        bank_s, bank_t = bank[0:4], bank[4:8]
        bank_bf = [b[:, :].bitcast(BF16) for b in bank]

        X = sb("x_state", [T, B, C])
        ident = sb("identity", [P, P])
        ident_bf = sb("identity_bf", [P, P], BF16)
        iota = sb("token_number", [P, 1])
        causal = sb("causal_mask", [T, T])
        gates = sb("tanh_gates", [P, 8])
        cols = sb("columns", [P, sum(COLS.values()) ])
        rows = sb("rows", [P, len(ROWS), C])
        minus_half = sb("minus_half", [P, LANES])
        stats = sb("bn_sums", [T, LANES, 6])
        mv = sb("mean_var", [T, LANES, 2])
        veps = sb("var_eps", [T, LANES])
        rstd = sb("rstd", [T, LANES])
        rowmin = sb("rowmin", [T, LANES, 4])
        rowsum = sb("rowsum", [T, LANES, 4])
        rinv = sb("rinv", [T, LANES, 4])
        omu = sb("one_minus_mu", [P, 4])
        one_col = sb("one_column", [P, 1])
        iota8 = sb("expert_number", [T, E2])
        gate_b = sb("moe_gate_bias", [T, 2, E2])
        b1c = sb("moe_b1", [P, 2, E2 * 8])
        cw = sb("moe_weight", [T, B, E2])
        gsm = sb("gate_small", [T, 8, LANES, E2])
        gix = sb("gate_index", [T, LANES, E2], U32)
        ids = sb("seq_experts", [T, B, TOP2], I32)
        b1q = sb("seq_moe_b1", [P, SEQ_SLOTS, E2])
        hmean = sb("h_mean", [P, 2, LANES, KC])
        tiny = sb("tiny", [T, 20, LANES])
        wabs = sb("weight_abs", [P, 3, 3])
        region0 = sb("region0", [P, 9728])
        region1 = sb("region1", [P, 8720])
        stream = sb("stream", [P, 8192])
        LB = 4864
        arena = sb("arena", [P, LANES * LB])

        at = {"n": 0}

        def cut(region, words, dt=F32):
            n = at["n"]
            at["n"] = n + words
            ap = region[:, n:n + words]
            return ap if dt == F32 else ap.bitcast(dt)

        def three(ap, k):
            return ap.rearrange("p (k n) -> p k n", k=k)

        w_sv, w_so = three(cut(region0, 512), 2), three(cut(region0, 512), 2)
        w_q0, w_k0, w_v0, w_o0 = (three(cut(region0, 512), 2) for _ in range(4))
        w_l1, w_l2 = three(cut(region0, 2048), 2), three(cut(region0, 2048), 8)
        w_r, w_k, w_v = (three(cut(region0, 512), 2) for _ in range(3))
        w_q1, w_k1, w_v1 = (three(cut(region0, 256), 2) for _ in range(3))
        w_o1 = three(cut(region0, 256), 1)
        assert at["n"] <= 9728
        at["n"] = 0
        w_q3, w_k3, w_v3 = (three(cut(region0, 2048), 2) for _ in range(3))
        w_o3 = three(cut(region0, 2048), 8)
        at["n"] = 0
        w_sg, w_su = three(cut(region1, 1024), 2), three(cut(region1, 1024), 2)
        w_sd = three(cut(region1, 1024), 4)
        w_gate1 = three(cut(region1, 32), 2)
        w_q2, w_k2, w_v2, w_o2 = (three(cut(region1, 512), 2) for _ in range(4))

        def f_weights():
            return [three(cut(region1, 512), 2) for _ in range(4)] + [three(cut(region1, 16), 2)]

        w_f = [f_weights()]
        assert at["n"] <= 8720
        at["n"] = 0
        w_f.append(f_weights())
        raw3 = [cut(region1, 2048) for _ in range(3)]
        assert at["n"] <= 8720
        at["n"] = 0
        tern = [cut(stream, 1024, BF16) for _ in range(3)]
        w_tg, w_tu, w_td = three(tern[0], 2), three(tern[1], 2), three(tern[2], 8)
        abs_out = cut(stream, 2048)
        xn, xa, y, xT, cT, qT, kT, V, E, PT, O, wide, ga, accs, qm = ([] for _ in range(15))
        off = {}
        for j in range(LANES):
            at["n"] = j * LB
            xa.append(cut(arena, 256)[0:T, :])
            qm.append(three(arena[:, at["n"]:at["n"] + 4 * T], 4))
            xn.append(cut(arena, 256)[0:T, :])
            y.append(cut(arena, 256)[0:T, :])
            xT.append(three(cut(arena, 2 * T), 2))
            qT.append(three(cut(arena, 2 * T), 2))
            kT.append(cut(arena, S2))
            V.append(three(cut(arena, 3 * P), 3))
            off["e"] = at["n"] - j * LB
            E.append(cut(arena, 4 * T))
            PT.append(cut(arena, 4 * T))
            ga.append(arena[0:T, j * LB + off["e"]:j * LB + off["e"] + 512])
            O.append(cut(arena, P)[0:T, :])
            at["n"] += at["n"] % 2
            off["c"] = at["n"] - j * LB
            cT.append(three(cut(arena, 2 * S2), 2))
            off["w"] = at["n"] - j * LB
            wide.append(cut(arena, 1024))
            accs.append(three(arena[0:T, j * LB + off["w"] + 256:j * LB + off["w"] + 256 + 2 * C], 2))
            assert at["n"] <= (j + 1) * LB, at["n"] - j * LB
        assert 2 * 2 * 4 * T <= off["e"] * 1
        maskb = [w[0:T, 512:512 + S2] for w in wide]
        OT = [three(w[:, 0:8 * T], 8) for w in wide]
        qx = [a[:, 0:128].bitcast(BF16) for a in xa]
        xqT = [three(a[:, 0, :].bitcast(BF16), 2) for a in xT]
        hq = [a[0:T, :, :].rearrange("p k s -> p (k s)")[:, 0:512].bitcast(BF16) for a in cT]
        hqT = [three(arena[:, j * LB + off["e"]:j * LB + off["e"] + 4 * T].bitcast(BF16), 8) for j in range(LANES)]
        by_lane = arena[:, :].rearrange("p (j l) -> p j l", j=LANES)
        h2T = [[by_lane[:, :, off["c"] + (i * KC + k) * T:off["c"] + (i * KC + k + 1) * T] for k in range(KC)]
               for i in range(ITERS)]
        h2w = [three(arena[:, j * LB + off["c"]:j * LB + off["c"] + 2 * KC * T], 2) for j in range(LANES)]

        def hid(half, m):
            n = m // 2 * LB + (half * 2 + m % 2) * HALF_T
            return arena[:, n:n + HALF_T]

        def col(name, i=0, n=1):
            at_ = 0
            for k, v in COLS.items():
                if k == name:
                    return cols[:, at_ + i:at_ + i + n]
                at_ += v

        def row(name, n=T):
            return rows[0:n, ROWS.index(name), :]

        def row2(l, name, n=T):
            return rows[0:n, l * len(ROWS2) + ROWS2.index(name), :]

        def norm_counts(n, affine):
            return dict(stats_done=n, var_ready=n, veps_ready=n, rstd_ready=n, normed=n,
                        **({"scaled": affine} if affine else {}))

        def attn_counts(a, n=1):
            g = a.tiles * a.groups * n
            return dict(projected=a.tiles * n, qv_ready=a.tiles * n, k_ready=a.tiles * n, scores=g,
                        q_masked=g * a.group // a.batch if a.heads > 1 else 0, rowmin_ready=g, probs=g, probs_turned=g, probs_T=g, rinv_ready=g * (2 if a.guard else 1), heads_out=g,
                        heads_ready=g, o_turned=a.tiles * n, o_T=a.tiles * n)

        a0 = Attention(2, 4, 32, S2, KEY_TILES, w_q0, w_k0, w_v0, "l0_bq", "l0_bk", row("l0_bv", KEY_W))
        a1 = Attention(1, 1, 128, S2, KEY_TILES, w_q1, w_k1, w_v1, "l1_bq", "l1_bk", row("l1_bv", KEY_W),
                       mask=lambda j: maskb[0], guard=True)
        a2 = Attention(2, 8, 16, S2, KEY_TILES, w_q2, w_k2, w_v2, "l2_bq", "l2_bk", row("l2_bv", KEY_W),
                       mask=lambda j: maskb[j])
        af = [Attention(2, 8, 16, T, 1, w_f[l][0], w_f[l][1], w_f[l][2], f"f{l}_bq", f"f{l}_bk",
                        row2(l, "bv"), mask=lambda j: causal[:, :]) for l in range(2)]
        a3 = Attention(8, 2, 64, S2, KEY_TILES, w_q3, w_k3, w_v3)

        one = ("rstd_ready", "veps_ready")
        p_l0x = phase(ITERS, one, **norm_counts(4, 3), turned=3, xT_ready=3, self_v=1, self_vT=1,
                      proj_out=3, part=3, summed=3, x_added=1, hid=1, hid_a=1, hid_b=1, **attn_counts(a0))
        p_l0f = phase(ITERS, one, **norm_counts(1, 0), turned=1, xT_ready=1, shifted=1, mixed_r=1, mixed=1,
                      rk=1, k_relu=1, k_sq=1, sig=1, proj_out=1, gated=1, x_added=1)
        p_l1x = phase(ITERS, one, **norm_counts(1, 0), turned=1, xT_ready=1, proj_out=1, part=1, x_added=1,
                      **attn_counts(a1))
        p_rt = phase(ITERS, one, **norm_counts(1, 0), turned=1, xT_ready=1, xT_spread=1, logits=1, lmax=1,
                     lexp=1, linv=1, scored=1)
        two = dict(lanes=2)
        p_ex = phase(E1 // 2, gu_out=1, e_gelu=1, e_hid=1, e_out=1, e_kept=1, **two)
        p_sh = phase(B // 2, gu_out=1, e_gelu=1, e_hid=1, e_out=1, sh_added=1, **two)
        p_l2x = phase(ITERS, one, **norm_counts(1, 0), turned=1, xT_ready=1, proj_out=1, part=1, x_added=1,
                      mask_ready=1, **attn_counts(a2))
        p_f, p_m = [], []
        gate_steps = ("g_top", "g_topf", "g_diff", "g_exp", "g_sum", "g_w1", "g_w2", "g_cw")
        for l in range(2):
            p_f.append(phase(ITERS, one + gate_steps + ("ids_ready",), **norm_counts(3 - l, 2), turned=2, xT_ready=2, h_spread=1,
                             proj_out=1, part=1, summed=1, hmean_sum=l, hmean_ready=l, ids_ready=l, g_out=1, g_val=1,
                             g_maxed=1, g_half=1, cw_turned=1, cwT_ready=1, cw_spread=1, b2_out=1, acc_ready=1,
                             **{n: 1 for n in gate_steps}, **attn_counts(af[l])))
        p_m.append(phase(E2 // 2, lanes=1, h_out=32, h_gelu=32, y_out=16, y_added=16))
        p_m.append(phase(ITERS, lanes=1, h_out=2 * SEQ_ITEMS, h_gelu=2 * SEQ_ITEMS, y_out=SEQ_ITEMS,
                         y_added=SEQ_ITEMS))
        p_l3x = phase(ITERS, one, **norm_counts(1, 0), turned=1, xT_ready=1, proj_out=1, x_added=1,
                      **attn_counts(a3))
        p_l3f = phase(ITERS, one + ("tiny_done",), **norm_counts(1, 0), amax_ready=1, tiny_done=12, rounded=1,
                      q_ready=1, turned=1, xq_ready=1, g_u_out=2, g_relu=2, g_sq=2, h_part=2, amax2_ready=1,
                      rounded2=1, q2_ready=1, q2_turned=1, q2T_ready=1, proj_out=1, out_scaled=1, x_added=1)
        (s_const, s_wl0, s_wl1, s_wl3, s_rows2, s_wf1, s_raw3, s_x, s_mask1, s_gates, s_omu, s_half, s_one,
         s_mask1b, s_shift0, s_topT, s_scoreT, s_topstep, s_idx, s_sel, s_gather, s_taken, s_selT, s_selTk,
         s_stored, s_rows_in, s_abs, s_wsum, s_wmean, s_tern, s_gadd, s_out) = (make(n) for n in (
             "constants_loaded", "weights_l0_loaded", "weights_l1_l2_loaded", "weights_l3_loaded",
             "rows2_loaded", "weights_f1_loaded", "raw_l3_loaded", "x_loaded", "mask1_loaded",
             "tanh_gates_ready", "one_minus_mu_ready", "minus_half_set", "one_set", "mask1_bias_ready",
             "shift_columns_zeroed", "score_turned", "scoreT_ready", "top_step_done", "indices_spread",
             "selection_ready", "gathered", "taken_ready", "selection_turned", "selT_ready",
             "expert_rows_stored", "expert_rows_loaded", "weights_abs_summed", "weights_sum_out",
             "weights_mean_step", "ternary_step", "x_gated_added", "out_stored"))
        s_ctx = [make(f"context_loaded{j}") for j in range(LANES)]
        s_maskl = [make(f"mask_loaded{j}") for j in range(LANES)]
        s_ew = [make(f"expert_weights_loaded{s}") for s in range(2)]
        s_mw = [make(f"moe_weights_loaded{s}") for s in range(2)]
        s_qw = [make(f"seq_moe_weights_loaded{s}") for s in range(SEQ_SLOTS)]

        def wait_first(eng, sem, value):
            eng.wait_ge(sem, value)
            eng.nop(nofuse=True)

        def norm_stats(v, p, it, r, src, ready=None):
            for j in range(LANES):
                if ready is not None:
                    wait_first(v, *ready(j))
                v.bn_stats(stats[:, j, :], src(j)).then_inc(p["stats_done"].sem, 1)
            for j in range(LANES):
                wait_first(v, *p["stats_done"].at(it, r, j))
                v.bn_aggr(mv[:, j, :], stats[:, j, :]).then_inc(p["var_ready"].sem, 1)

        def norm_rstd(g, p, it, r):
            wait_first(g, *p["var_ready"].at(it, r, LANES - 1))
            g.tensor_scalar(veps[:, :], mv[:, :, 1], EPS, None, ALU.add).then_inc(p["veps_ready"].sem, 1)
            g.wait_ge(*p["veps_ready"].at(it, r))
            g.tensor_tensor(rstd[:, :], veps[:, :], minus_half[0:T, :], ALU.pow).then_inc(p["rstd_ready"].sem, 1)

        def norm_apply(v, p, it, r, src, dst):
            v.wait_ge(*p["rstd_ready"].at(it, r))
            for j in range(LANES):
                v.tensor_scalar(dst(j), src(j), mv[:, j, 0:1], rstd[:, j:j + 1], ALU.subtract,
                                ALU.mult).then_inc(p["normed"].sem, 1)

        def norm_apply_affine(v, p, it, r, ra, src, dst, g, b):
            for j in range(LANES):
                v.wait_ge(*p["var_ready"].at(it, r, j))
                v.scalar_tensor_tensor(dst(j), src(j), mv[:, j, 0:1], g, ALU.subtract,
                                       ALU.mult).then_inc(p["scaled"].sem, 1)
            v.wait_ge(*p["rstd_ready"].at(it, r))
            for j in range(LANES):
                v.wait_ge(*p["scaled"].at(it, ra, j))
                v.scalar_tensor_tensor(dst(j), dst(j), rstd[:, j:j + 1], b, ALU.mult,
                                       ALU.add).then_inc(p["normed"].sem, 1)

        def turn(pe, p, it, r, rn, src):
            for j in range(LANES):
                pe.wait_ge(*p["normed"].at(it, rn, j))
                for c in range(KC):
                    last = pe.transpose(bank_t[j][:, c * T:(c + 1) * T], src[j][:, c * P:(c + 1) * P],
                                        ident[0:T, 0:T])
                last.then_inc(p["turned"].sem, 1)

        def keep_turned(act, p, it, r):
            for j in range(LANES):
                act.wait_ge(*p["turned"].at(it, r, j))
                act.copy(xT[j], three(bank_t[j][:, 0:2 * T], 2)).then_inc(p["xT_ready"].sem, 1)

        def matmuls(pe, dst, pairs):
            n = len(pairs)
            for i, (l, r) in enumerate(pairs):
                last = pe.matmul(dst, l, r, start=(i == 0), stop=(i == n - 1))
            return last

        def attend_tensor(pe, a, p, it, rx, source, keys_of, keys_ready):
            for m in range(a.tiles):
                f = slice(m * P, (m + 1) * P)
                for j in range(LANES):
                    if m == 0:
                        pe.wait_ge(*p["xT_ready"].at(it, rx, j))
                        if keys_ready is not None:
                            pe.wait_ge(*keys_ready(it, j))
                    else:
                        pe.wait_ge(*p["o_T"].at(it, m - 1, j))
                    q, k = xT[j], keys_of(j)
                    wq = a.wq
                    matmuls(pe, bank_t[j][:, 0:T], [(wq[:, c, f], q[:, c, :]) for c in range(KC)])
                    matmuls(pe, bank_s[j][:, 0:a.keys], [(a.wk[:, c, f], k[:, c, :]) for c in range(KC)])
                    for t in range(a.key_tiles):
                        ks = slice(t * a.key_w, (t + 1) * a.key_w)
                        last = matmuls(pe, bank_t[j][0:a.key_w, T + t * P:T + (t + 1) * P],
                                       [(k[:, c, ks], a.wv[:, c, f]) for c in range(KC)])
                    last.then_inc(p["projected"].sem, 1)
                for g in range(a.groups):
                    r = m * a.groups + g
                    heads = [g * a.group + i for i in range(a.group)]
                    for j in range(LANES):
                        if g == 0:
                            pe.wait_ge(*p["qv_ready"].at(it, m, j))
                            pe.wait_ge(*p["k_ready"].at(it, m, j))
                        else:
                            pe.wait_ge(*p["heads_ready"].at(it, r - 1, j))
                        if a.heads > 1 and heads[0] % a.batch == 0:
                            pe.wait_ge(*p["q_masked"].at(it, r * a.group // a.batch, j))
                        for i, h in enumerate(heads):
                            last = pe.matmul(bank_s[j][0:T, i * a.keys:(i + 1) * a.keys],
                                             qT[j][:, 0, :] if a.heads == 1 else qm[j][:, h % a.batch, :],
                                             kT[j][:, 0:a.keys], start=True, stop=True)
                        last.then_inc(p["scores"].sem, 1)
                    for j in range(LANES):
                        pe.wait_ge(*p["probs"].at(it, r, j))
                        for i in range(a.group * a.key_tiles):
                            last = pe.transpose(bank_t[j][0:a.key_w, i * T:(i + 1) * T],
                                                E[j][0:T, i * a.key_w:(i + 1) * a.key_w], ident[0:T, 0:T])
                        last.then_inc(p["probs_turned"].sem, 1)
                    for j in range(LANES):
                        pe.wait_ge(*p["probs_T"].at(it, r, j))
                        for i, h in enumerate(heads):
                            last = matmuls(pe, bank_s[j][0:T, i * a.d:(i + 1) * a.d],
                                           [(PT[j][0:a.key_w, (i * a.key_tiles + t) * T:(i * a.key_tiles + t + 1) * T],
                                             V[j][0:a.key_w, t, h * a.d:(h + 1) * a.d])
                                            for t in range(a.key_tiles)])
                        last.then_inc(p["heads_out"].sem, 1)
                for j in range(LANES):
                    pe.wait_ge(*p["heads_ready"].at(it, (m + 1) * a.groups - 1, j))
                    pe.transpose(bank_t[j][:, 0:T], O[j], ident[0:T, 0:T]).then_inc(p["o_turned"].sem, 1)

        def attend_vector(v, a, p, it):
            for m in range(a.tiles):
                for j in range(LANES):
                    v.wait_ge(*p["projected"].at(it, m, j))
                    ps = bank_t[j][:, 0:T]
                    if a.bq is None:
                        v.tensor_scalar(qT[j][:, 0, :], ps, -a.scale, None, ALU.mult)
                    else:
                        v.tensor_scalar(qT[j][:, 0, :], ps, col(a.bq, m), -a.scale, ALU.add, ALU.mult)
                    vs = three(bank_t[j][0:a.key_w, T:T + a.key_tiles * P], a.key_tiles)
                    vd = V[j][0:a.key_w, 0:a.key_tiles, :]
                    if a.bv is None:
                        last = v.tensor_copy(vd, vs)
                    else:
                        bv = a.bv[0:a.key_w, m * P:(m + 1) * P].unsqueeze(1).broadcast_to([a.key_w, a.key_tiles, P])
                        last = v.tensor_tensor(vd, vs, bv, ALU.add)
                    last.then_inc(p["qv_ready"].sem, 1)
                for g in range(a.groups):
                    r = m * a.groups + g
                    for j in range(LANES):
                        wait_first(v, *p["scores"].at(it, r, j))
                        if a.mask is None:
                            last = v.tensor_reduce(rowmin[:, j, 0:1], bank_s[j][0:T, 0:a.keys], AX_X, ALU.min)
                        else:
                            for i in range(a.group):
                                ks = slice(i * a.keys, (i + 1) * a.keys)
                                last = nc.vector.tensor_tensor_reduce(
                                    out=E[j][0:T, ks], in0=bank_s[j][0:T, ks], in1=a.mask(j), scale=1.0,
                                    scalar=3.0e38, op0=ALU.add, op1=ALU.min, accum_out=rowmin[:, j, i:i + 1])
                        last.then_inc(p["rowmin_ready"].sem, 1)
                    for j in range(LANES):
                        v.wait_ge(*p["probs"].at(it, r, j))
                        v.reciprocal(rinv[:, j, 0:a.group], rowsum[:, j, 0:a.group]).then_inc(p["rinv_ready"].sem, 1)
                    if a.guard:
                        for j in range(LANES):
                            v.wait_ge(*p["rinv_ready"].at(it, 2 * r, j))
                            v.scalar_tensor_tensor(rinv[:, j, 0:1], rowmin[:, j, 0:1], 0.5 * BIG, rinv[:, j, 0:1],
                                                   ALU.is_lt, ALU.mult).then_inc(p["rinv_ready"].sem, 1)
                    for j in range(LANES):
                        v.wait_ge(*p["heads_out"].at(it, r, j))
                        v.wait_ge(*(p["rinv_ready"].at(it, 2 * r + 1, j) if a.guard else p["rinv_ready"].at(it, r, j)))
                        dst = O[j][:, g * a.group * a.d:(g + 1) * a.group * a.d]
                        ps = bank_s[j][0:T, 0:a.group * a.d]
                        if a.group == 1:
                            last = v.tensor_scalar(dst, ps, rinv[:, j, 0:1], None, ALU.mult)
                        else:
                            last = v.tensor_tensor(three(dst, a.group), three(ps, a.group),
                                                   rinv[:, j, 0:a.group].unsqueeze(2).broadcast_to([T, a.group, a.d]),
                                                   ALU.mult)
                        last.then_inc(p["heads_ready"].sem, 1)

        def attend_scalar(act, a, p, it):
            for m in range(a.tiles):
                for j in range(LANES):
                    act.wait_ge(*p["projected"].at(it, m, j))
                    if a.bk is None:
                        last = act.copy(kT[j][:, 0:a.keys], bank_s[j][:, 0:a.keys])
                    else:
                        last = act.activation(kT[j][:, 0:a.keys], bank_s[j][:, 0:a.keys], ACT.Identity,
                                              bias=col(a.bk, m))
                    last.then_inc(p["k_ready"].sem, 1)
                for g in range(a.groups):
                    r = m * a.groups + g
                    for j in range(LANES):
                        act.wait_ge(*p["rowmin_ready"].at(it, r, j))
                        for i in range(a.group):
                            ks = slice(i * a.keys, (i + 1) * a.keys)
                            src = bank_s[j] if a.mask is None else E[j]
                            last = act.activation(E[j][0:T, ks], src[0:T, ks], ACT.Exp,
                                                  bias=rowmin[:, j, i:i + 1], scale=-1.0,
                                                  accum_out=rowsum[:, j, i:i + 1])
                        last.then_inc(p["probs"].sem, 1)
                    for j in range(LANES):
                        n = a.group * a.key_tiles * T
                        act.wait_ge(*p["probs_turned"].at(it, r, j))
                        act.copy(PT[j][0:a.key_w, 0:n], bank_t[j][0:a.key_w, 0:n]).then_inc(p["probs_T"].sem, 1)
                for j in range(LANES):
                    act.wait_ge(*p["o_turned"].at(it, m, j))
                    act.copy(OT[j][:, m, :], bank_t[j][:, 0:T]).then_inc(p["o_T"].sem, 1)

        def attend_gpsimd(g, a, p, it):
            per = a.heads // a.batch
            for m in range(a.tiles):
                for n in range(per):
                    for j in range(LANES):
                        g.wait_ge(*p["qv_ready"].at(it, m, j))
                        if n:
                            g.wait_ge(*p["scores"].at(it, m * a.groups + n * a.batch // a.group - 1, j))
                        rows_of = col("head_rows", a.masks + n * a.batch, a.batch)
                        g.tensor_tensor(qm[j][:, 0:a.batch, :],
                                        qT[j][:, 0:1, :].broadcast_to([P, a.batch, T]),
                                        rows_of.unsqueeze(2).broadcast_to([P, a.batch, T]), ALU.mult)\
                            .then_inc(p["q_masked"].sem, 1)

        def project_out(pe, p, it, r, w, ready):
            for j in range(LANES):
                pe.wait_ge(*ready(j))
                matmuls(pe, bank_s[j][0:T, 0:C], [(OT[j][:, c, :], w[:, c, :]) for c in range(w.shape[1])]) \
                    .then_inc(p["proj_out"].sem, 1)

        def x_at(it, j):
            return X[:, it * LANES + j, :]

        def add_gated(v, p, it, src, gate, ready):
            for j in range(LANES):
                v.wait_ge(*ready(j))
                v.scalar_tensor_tensor(x_at(it, j), src(j), gates[0:T, gate:gate + 1], x_at(it, j), ALU.mult,
                                       ALU.add).then_inc(p["x_added"].sem, 1)

        def add_row(v, p, it, r, b):
            for j in range(LANES):
                v.wait_ge(*p["proj_out"].at(it, r, j))
                v.tensor_tensor(y[j], bank_s[j][0:T, 0:C], b, ALU.add).then_inc(p["part"].sem, 1)

        at["n"] = 0
        xn_all = cut(arena, B * C)[0:T, :].rearrange("t (b c) -> t b c", b=B)
        sel = cut(arena, CAP * P)[0:T, :].rearrange("t (c g) -> t c g", c=CAP)
        selw = cut(arena, CAP * P)[0:T, :].rearrange("t (g c) -> t g c", c=CAP)
        expert_rows = arena[0:T, 0:2 * B * C].rearrange("s (b h f) -> s b h f", b=B, h=2)
        xnT_all = cut(arena, KC * B * T).rearrange("p (k b t) -> p k b t", k=KC, b=B)
        taken = cut(arena, KC * E1 * B * CAP).rearrange("p (k e n) -> p k e n", k=KC, e=E1)
        selT = cut(arena, B * 2 * T)[0:T, :].rearrange("s (b h t) -> s b h t", b=B, h=2)
        eo = cut(arena, E1 * C)[0:T, :].rearrange("s (e c) -> s e c", e=E1)
        hbuf = [cut(arena, 4 * T) for _ in range(2)]
        score = cut(arena, B * E1)[0:T, :].rearrange("t (b e) -> t b e", b=B)
        scoreT, scoreT2 = cut(arena, T), cut(arena, T)
        top16, topi16, topf = cut(arena, 16), cut(arena, 16, U32), cut(arena, CAP)
        rsc = cut(arena, 4 * LANES)[0:T, :].rearrange("t (n j) -> t n j", n=4)
        assert at["n"] <= LANES * LB, at["n"]
        at["n"] = 6144
        rxT = [three(cut(stream, KC * T), KC) for _ in range(LANES)]
        scratch = nc.dram_tensor("expert_out", (E1, B, CAP, C), F32, kind="Internal").ap()

        def expert_slot(s):
            n = s * 3072
            return (three(stream[:, n:n + 1024], 2), three(stream[:, n + 1024:n + 2048], 2),
                    three(stream[:, n + 2048:n + 3072], 4))

        def moe_slot(s):
            n = s * 4096
            return three(stream[:, n:n + 2048], 2), three(stream[:, n + 2048:n + 4096], 8)

        def seq_slot(s):
            if s < 2:
                return moe_slot(s)
            n = (s - 2) * 2 * LB
            return three(arena[:, n:n + 2048], 2), three(arena[:, n + LB:n + LB + 2048], 8)

        def seq_hid(s):
            return arena[:, s * LB + 2048:s * LB + 2048 + 8 * T]

        ctx_turn = {"l0": 0, "l1": 1, "l2": 2, "l3": 3}

        def ctx_ready(which):
            return lambda it, j: (s_ctx[j], it * 16 + (ctx_turn[which] * ITERS * 16 + 16))

        end = {k: (v.sem, v.base + n) for k, (v, n) in {
            "l0x": (p_l0x["x_added"], B), "l0f": (p_l0f["x_added"], B), "l1x": (p_l1x["x_added"], B),
            "sh": (p_sh["sh_added"], B), "l2x": (p_l2x["x_added"], B), "l3x": (p_l3x["x_added"], B),
            "l3f": (p_l3f["x_added"], B), "f0": (p_f[0]["acc_ready"], B), "f1": (p_f[1]["acc_ready"], B),
            "m0": (p_m[0]["y_added"], 64), "m1": (p_m[1]["y_added"], ITERS * SEQ_ITEMS)}.items()}

        block = ctx.enter_context(nc.Block())

        @block.sync
        def _(sp):
            def load(dst, src, s):
                sp.dma_start(dst, src).then_inc(s, 16)

            def weight(dst, name, s):
                load(dst, A[name].rearrange("(k p) n -> p k n", p=P), s)

            def context(which, it, j, before=None):
                if before is not None:
                    sp.wait_ge(*before)
                load(cT[j], A["ctxT"][:, it * LANES + j, :].rearrange("(k p) s -> p k s", p=P), s_ctx[j])

            load(X[:, :, :], A["x"].rearrange("b t c -> t b c"), s_x)
            load(ident[:, :], A["identity"], s_const)
            load(cols[:, :], A["columns"], s_const)
            load(rows[:, :, :], A["rows"].partition_broadcast(P), s_const)
            load(gates[:, :], A["gates"].partition_broadcast(P), s_const)
            load(causal[:, :], A["causal"], s_const)
            load(iota[:, :], A["iota"], s_const)
            load(iota8[:, :], A["iota8"].partition_broadcast(T), s_const)
            load(gate_b[:, :, :], A["moe_gate_b"].partition_broadcast(T), s_const)
            load(b1c[:, :, :], A["moe_b1"], s_const)
            for dst, name in ((w_sv, "l0_wsv"), (w_so, "l0_wso"), (w_q0, "l0_wq"), (w_k0, "l0_wk"),
                              (w_v0, "l0_wv")):
                weight(dst, name, s_wl0)
            for j in range(LANES):
                context("l0", 0, j)
            for dst, name in ((w_o0, "l0_wo"), (w_l1, "l0_w1"), (w_l2, "l0_w2"), (w_r, "l0_wr"),
                              (w_k, "l0_wkk"), (w_v, "l0_wvv"), (w_q1, "l1_wq"), (w_k1, "l1_wk"),
                              (w_v1, "l1_wv"), (w_o1, "l1_wo")):
                weight(dst, name, s_wl0)
            for dst, name in ((w_sg, "ws_g"), (w_su, "ws_u"), (w_sd, "ws_d"), (w_gate1, "l1_gate"),
                              (w_q2, "l2_wq"), (w_k2, "l2_wk"), (w_v2, "l2_wv"), (w_o2, "l2_wo"),
                              (w_f[0][0], "f0_wq"), (w_f[0][1], "f0_wk"), (w_f[0][2], "f0_wv"),
                              (w_f[0][3], "f0_wo"), (w_f[0][4], "f0_gate")):
                weight(dst, name, s_wl1)

            def expert(e, s):
                wg, wu, wd = expert_slot(s)
                load(wg, A["e_wg"][e].rearrange("(k p) n -> p k n", p=P), s_ew[s])
                load(wu, A["e_wu"][e].rearrange("(k p) n -> p k n", p=P), s_ew[s])
                load(wd, A["e_wd"][e].rearrange("(k p) n -> p k n", p=P), s_ew[s])

            for s in range(2):
                expert(s, s)
            for j in range(LANES):
                context("l0", 1, j, p_l0x["projected"].at(0, a0.tiles - 1, j))
            sp.wait_ge(*end["l0x"])
            load(maskb[0].bitcast(I32), A["mask1"][0], s_mask1)
            sp.wait_ge(*end["l0f"])
            for j in range(LANES):
                context("l1", 0, j)
            for j in range(LANES):
                context("l1", 1, j, p_l1x["projected"].at(0, a1.tiles - 1, j))
            sp.wait_ge(*end["l1x"])
            load(rows[:, 0:2 * len(ROWS2), :], A["rows2"].partition_broadcast(P), s_rows2)
            for dst, name in ((w_q3, "l3_wq"), (w_k3, "l3_wk"), (w_v3, "l3_wv"), (w_o3, "l3_wo")):
                weight(dst, name, s_wl3)
            with sp.Fori(1, E1 // 2) as i:
                for s in range(2):
                    sp.wait_ge(*p_ex["e_out"].at(i - 1, 0, s))
                    expert(i * 2 + s, s)
            sp.wait_ge(s_stored, 16 * E1)
            sp.wait_ge(s_selTk, B)
            for e in range(E1):
                h, i = e // HALF_E, e % HALF_E
                load(expert_rows[i * CAP:(i + 1) * CAP, :, h, :], scratch[e].rearrange("b c f -> c b f"), s_rows_in)

            def moe(l, e, s):
                w1, w2 = moe_slot(s)
                load(w1, A["moe_w1"][l, e].rearrange("(k p) n -> p k n", p=P), s_mw[s])
                load(w2, A["moe_w2"][l, e].rearrange("(k p) n -> p k n", p=P), s_mw[s])

            sp.wait_ge(*p_ex["e_out"].at(E1 // 2 - 1, 0, 1))
            for s in range(2):
                moe(0, s, s)
            sp.wait_ge(*end["sh"])
            for dst, name in ((w_f[1][0], "f1_wq"), (w_f[1][1], "f1_wk"), (w_f[1][2], "f1_wv"),
                              (w_f[1][3], "f1_wo"), (w_f[1][4], "f1_gate")):
                weight(dst, name, s_wf1)
            for it in range(ITERS):
                for j in range(LANES):
                    context("l2", it, j, p_l2x["projected"].at(0, a2.tiles - 1, j) if it else None)
                    if it:
                        sp.wait_ge(*p_l2x["rowmin_ready"].at(0, a2.tiles * a2.groups - 1, j))
                    load(maskb[j].bitcast(I32), A["mask2"][it * LANES + j], s_maskl[j])
            sp.wait_ge(*end["l2x"])
            load(rows[0:E2, 12:14, :], A["moe_b2"], s_rows2)
            sp.wait_ge(*end["f0"])
            for i in range(3):
                load(raw3[i], A[("raw_g", "raw_u", "raw_d")[i]], s_raw3)
            with sp.Fori(1, E2 // 2) as i:
                for s in range(2):
                    sp.wait_ge(*p_m[0]["y_out"].at(i - 1, 8 * s + 7))
                    moe(0, i * 2 + s, s)
            sp.wait_ge(*p_m[0]["y_out"].at(E2 // 2 - 1, 15))

            def seq_expert(it, r):
                s = r % SEQ_SLOTS
                e = sp.value_load(ids[0:1, bass.ds(it * LANES + r // TOP2, 1), r % TOP2], min_val=0, max_val=E2 - 1)
                w1, w2 = seq_slot(s)
                load(w1, A["moe_w1"][1, bass.ds(e, 1)].rearrange("o (k p) n -> p (o k) n", p=P), s_qw[s])
                load(w2, A["moe_w2"][1, bass.ds(e, 1)].rearrange("o (k p) n -> p (o k) n", p=P), s_qw[s])
                load(b1q[:, s, :], A["moe_b1"][:, 1, bass.ds(e * E2, E2)], s_qw[s])

            for it in range(ITERS):
                sp.wait_ge(*p_f[1]["ids_ready"].at(it))
                for r in range(SEQ_ITEMS):
                    n = it * SEQ_ITEMS + r
                    if n == 2:
                        sp.wait_ge(*end["f1"])
                    if n >= SEQ_SLOTS:
                        sp.wait_ge(*p_m[1]["y_out"].at(0, n - SEQ_SLOTS))
                    seq_expert(it, r)
            sp.wait_ge(*end["m1"])
            for it in range(ITERS):
                for j in range(LANES):
                    context("l3", it, j, p_l3x["projected"].at(0, a3.tiles - 1, j) if it else None)
            for it in range(ITERS):
                for j in range(LANES):
                    sp.wait_ge(*p_l3f["x_added"].at(it, 0, j))
                    b = it * LANES + j
                    load(out[b], X[:, b, :], s_out)
            sp.wait_ge(s_out, 16 * B)

        @block.gpsimd
        def _(g):
            g.memset(minus_half[:, :], -0.5).then_inc(s_half, 1)
            g.memset(one_col[:, :], 1.0).then_inc(s_one, 1)
            g.wait_ge(s_half, 1)

            def chain(p, before, a=None, after=0):
                with g.Fori(0, ITERS) as it:
                    for r in range(before):
                        norm_rstd(g, p, it, r)
                    if a is not None:
                        attend_gpsimd(g, a, p, it)
                    for r in range(before, before + after):
                        norm_rstd(g, p, it, r)

            chain(p_l0x, 2, a0, 2)
            chain(p_l0f, 1)
            chain(p_l1x, 1)
            chain(p_rt, 1)
            chain(p_l2x, 1, a2)
            chain(p_f[0], 2, af[0], 1)
            chain(p_f[1], 1, af[1], 1)
            g.wait_ge(s_wmean, 2)
            for i in range(3):
                g.tensor_scalar(raw3[i], raw3[i], wabs[:, 2, i:i + 1], ROUND, ALU.mult, ALU.add).then_inc(s_tern, 1)
            for i in range(3):
                g.wait_ge(s_tern, i + 1)
                g.tensor_scalar(raw3[i], raw3[i], -ROUND, 1.0, ALU.add, ALU.min).then_inc(s_tern, 1)
            for i in range(3):
                g.wait_ge(s_tern, 3 + i + 1)
                g.tensor_scalar(tern[i], raw3[i], -1.0, None, ALU.max).then_inc(s_tern, 1)
            chain(p_l3x, 1, a3)
            chain(p_l3f, 1)

        @block.scalar
        def _(act):
            act.wait_ge(s_const, 16 * 9)
            act.activation(gates[:, :], gates[:, :], ACT.Tanh).then_inc(s_gates, 1)

            with act.Fori(0, ITERS) as it:
                p = p_l0x
                keep_turned(act, p, it, 0)
                for j in range(LANES):
                    act.wait_ge(*p["self_v"].at(it, 0, j))
                    for m in range(KC):
                        last = act.activation(qT[j][:, m, :], bank_s[j][:, m * T:(m + 1) * T], ACT.Identity,
                                              bias=col("l0_sv", m))
                    last.then_inc(p["self_vT"].sem, 1)
                keep_turned(act, p, it, 1)
                attend_scalar(act, a0, p, it)
                keep_turned(act, p, it, 2)
                for j in range(LANES):
                    act.wait_ge(*p["hid"].at(it, 0, j))
                    for m in range(0, 4):
                        last = act.activation(OT[j][:, m, :], bank_s[j][:, m * T:(m + 1) * T], ACT.Relu,
                                              bias=col("lin1_b", m))
                    last.then_inc(p["hid_a"].sem, 1)
            with act.Fori(0, ITERS) as it:
                p = p_l0f
                for j in range(LANES):
                    act.wait_ge(*p["turned"].at(it, 0, j))
                    act.copy(cT[j][:, :, 1:T + 1], three(bank_t[j][:, 0:2 * T], 2)).then_inc(p["xT_ready"].sem, 1)
                for j in range(LANES):
                    act.wait_ge(*p["rk"].at(it, 0, j))
                    act.activation(V[j][:, 0:2, 0:T], three(bank_t[j][:, 0:2 * T], 2), ACT.Relu)\
                        .then_inc(p["k_relu"].sem, 1)
                    act.activation(y[j], bank_s[j][0:T, 0:C], ACT.Sigmoid).then_inc(p["sig"].sem, 1)
            with act.Fori(0, ITERS) as it:
                keep_turned(act, p_l1x, it, 0)
                attend_scalar(act, a1, p_l1x, it)
            p = p_rt
            for it in range(ITERS):
                for j in range(LANES):
                    act.wait_ge(*p["turned"].at(it, 0, j))
                    act.copy(rxT[j], three(bank_t[j][:, 0:2 * T], 2)).then_inc(p["xT_ready"].sem, 1)
                for j in range(LANES):
                    b = it * LANES + j
                    act.copy(xnT_all[:, :, b, :], three(bank_t[j][:, 0:2 * T], 2)).then_inc(p["xT_spread"].sem, 1)
                for j in range(LANES):
                    act.wait_ge(*p["lmax"].at(it, 0, j))
                    act.activation(score[:, it * LANES + j, :], bank_s[j][0:T, 0:E1], ACT.Exp,
                                   bias=rsc[:, 0, j:j + 1], accum_out=rsc[:, 1, j:j + 1]).then_inc(p["lexp"].sem, 1)
            act.wait_ge(s_topT, 1)
            act.copy(scoreT, bank[0][:, 0:T]).then_inc(s_scoreT, 1)
            for b in range(B):
                act.wait_ge(s_gather, b + 1)
                for k in range(KC):
                    last = act.copy(taken[:, k, :, b * CAP:(b + 1) * CAP],
                                    bank[b][:, k * CAP * E1:(k + 1) * CAP * E1].rearrange("p (c e) -> p e c", c=CAP))
                last.then_inc(s_taken, 1)
            with act.Fori(0, E1 // 2) as i:
                for s in range(2):
                    act.wait_ge(*p_ex["gu_out"].at(i, 0, s))
                    act.activation(hbuf[s], bank[3 * s][:, 0:4 * T], ACT.Gelu).then_inc(p_ex["e_gelu"].sem, 1)
                for s in range(2):
                    act.wait_ge(*p_ex["e_out"].at(i, 0, s))
                    act.copy(eo[:, i * 2 + s, :], bank[3 * s + 2][0:T, 0:C]).then_inc(p_ex["e_kept"].sem, 1)
                    act.wait_ge(*p_ex["e_kept"].at(i, 0, s))
                    act.dma_start(scratch[i * 2 + s].rearrange("b c f -> (b c) f"), eo[:, i * 2 + s, :])\
                        .then_inc(s_stored, 16)
            for b in range(B):
                act.wait_ge(*p_sh["gu_out"].at(b // 2, 0, b % 2))
                act.activation(hbuf[b % 2], bank[3 * (b % 2)][:, 0:4 * T], ACT.Gelu).then_inc(p_sh["e_gelu"].sem, 1)
            with act.Fori(0, ITERS) as it:
                keep_turned(act, p_l2x, it, 0)
                attend_scalar(act, a2, p_l2x, it)
            for l in range(2):
                p = p_f[l]
                with act.Fori(0, ITERS) as it:
                    keep_turned(act, p, it, 0)
                    attend_scalar(act, af[l], p, it)
                    keep_turned(act, p, it, 1)
                    for j in range(LANES):
                        act.copy(h2w[j][:, it, :], bank_t[j][:, 0:2 * T]).then_inc(p["h_spread"].sem, 1)
                    act.wait_ge(*p["g_diff"].at(it))
                    act.activation(tiny[:, 1, :], tiny[:, 0, :], ACT.Exp).then_inc(p["g_exp"].sem, 1)
                    for j in range(LANES):
                        act.wait_ge(*p["cw_turned"].at(it, 0, j))
                        act.copy(E[j][0:E2, 0:T], bank_t[j][0:E2, 0:T]).then_inc(p["cwT_ready"].sem, 1)
                if l == 1:
                    with act.Fori(0, ITERS) as it:
                        for r in range(SEQ_ITEMS):
                            if r >= 2:
                                act.wait_ge(*p_m[1]["y_out"].at(it, r - 2))
                            for m in range(8):
                                if m % 4 == 0:
                                    act.wait_ge(*p_m[1]["h_out"].at(it, 2 * r + m // 4))
                                last = act.activation(seq_hid(r % 2)[:, m * T:(m + 1) * T],
                                                      bank[r % 2 * 2 + m // 4][:, m % 4 * T:(m % 4 + 1) * T],
                                                      ACT.Gelu, bias=b1q[:, r % SEQ_SLOTS, m:m + 1])
                                if m % 4 == 3:
                                    last.then_inc(p_m[1]["h_gelu"].sem, 1)
                    continue
                with act.Fori(0, E2 // 2) as i:
                    for q in range(4):
                        for m in range(8):
                            r = q * 8 + m
                            if m == 0 and q >= 2:
                                wait_first(act, *p_m[l]["y_out"].at(i, 4 * (q - 2) + 3))
                            wait_first(act, *p_m[l]["h_out"].at(i, r))
                            act.activation(hid(q % 2, m), bank[m % 4][:, 0:HALF_T], ACT.Gelu,
                                           bias=b1c[:, l, bass.ds(i * 16 + (8 * (q // 2) + m), 1)])\
                                .then_inc(p_m[l]["h_gelu"].sem, 1)
            act.wait_ge(s_raw3, 48)
            act.wait_ge(*end["m1"])
            for i in range(3):
                act.activation(abs_out, raw3[i], ACT.Abs, accum_out=wabs[:, 0, i:i + 1]).then_inc(s_abs, 1)
                act.wait_ge(s_abs, i + 1)
            with act.Fori(0, ITERS) as it:
                keep_turned(act, p_l3x, it, 0)
                attend_scalar(act, a3, p_l3x, it)
            with act.Fori(0, ITERS) as it:
                p = p_l3f
                for h in range(2):
                    for j in range(LANES):
                        act.wait_ge(*p["g_u_out"].at(it, h, j))
                        if h == 1:
                            act.wait_ge(*p["h_part"].at(it, 0, j))
                        act.activation(ga[j], bank_s[j][0:T, :], ACT.Relu).then_inc(p["g_relu"].sem, 1)
                    for j in range(LANES):
                        act.wait_ge(*p["g_relu"].at(it, h, j))
                        act.activation(ga[j], ga[j], ACT.Square).then_inc(p["g_sq"].sem, 1)

        @block.tensor
        def _(pe):
            pe.wait_ge(s_const, 16 * 9)
            pe.wait_ge(s_wl0, 16 * 15)
            with pe.Fori(0, ITERS) as it:
                p = p_l0x
                turn(pe, p, it, 0, 0, xn)
                for j in range(LANES):
                    pe.wait_ge(*p["xT_ready"].at(it, 0, j))
                    for m in range(KC):
                        last = matmuls(pe, bank_s[j][:, m * T:(m + 1) * T],
                                       [(w_sv[:, c, m * P:(m + 1) * P], xT[j][:, c, :]) for c in range(KC)])
                    last.then_inc(p["self_v"].sem, 1)
                for j in range(LANES):
                    pe.wait_ge(*p["self_vT"].at(it, 0, j))
                    matmuls(pe, bank_s[j][0:T, 0:C], [(qT[j][:, c, :], w_so[:, c, :]) for c in range(KC)])\
                        .then_inc(p["proj_out"].sem, 1)
                turn(pe, p, it, 1, 1, xa)
                attend_tensor(pe, a0, p, it, 1, None, lambda j: cT[j], ctx_ready("l0"))
                project_out(pe, p, it, 1, w_o0, lambda j: p["o_T"].at(it, a0.tiles - 1, j))
                turn(pe, p, it, 2, 2, xn)
                for j in range(LANES):
                    pe.wait_ge(*p["xT_ready"].at(it, 2, j))
                    for m in range(8):
                        dst = (bank_s if m < 4 else bank_t)[j]
                        last = matmuls(pe, dst[:, m % 4 * T:(m % 4 + 1) * T],
                                       [(w_l1[:, c, m * P:(m + 1) * P], xT[j][:, c, :]) for c in range(KC)])
                    last.then_inc(p["hid"].sem, 1)
                pe.wait_ge(*p["hid_b"].at(it, 0, LANES - 1))
                project_out(pe, p, it, 2, w_l2, lambda j: p["hid_a"].at(it, 0, j))
            with pe.Fori(0, ITERS) as it:
                p = p_l0f
                turn(pe, p, it, 0, 0, xn)
                for j in range(LANES):
                    pe.wait_ge(*p["mixed"].at(it, 0, j))
                    mr, mk = qT[j], three(PT[j][:, 0:2 * T], 2)
                    matmuls(pe, bank_s[j][0:T, 0:C], [(mr[:, c, :], w_r[:, c, :]) for c in range(KC)])
                    for m in range(KC):
                        last = matmuls(pe, bank_t[j][:, m * T:(m + 1) * T],
                                       [(w_k[:, c, m * P:(m + 1) * P], mk[:, c, :]) for c in range(KC)])
                    last.then_inc(p["rk"].sem, 1)
                pe.wait_ge(*p["sig"].at(it, 0, LANES - 1))
                project_out(pe, p, it, 0, w_v, lambda j: p["k_sq"].at(it, 0, j))
            with pe.Fori(0, ITERS) as it:
                p = p_l1x
                turn(pe, p, it, 0, 0, xn)
                attend_tensor(pe, a1, p, it, 0, None, lambda j: cT[j], ctx_ready("l1"))
                project_out(pe, p, it, 0, w_o1, lambda j: p["o_T"].at(it, a1.tiles - 1, j))
            pe.wait_ge(s_wl1, 16 * 13)
            p = p_rt
            for it in range(ITERS):
                for j in range(LANES):
                    pe.wait_ge(*p["normed"].at(it, 0, j))
                    for c in range(KC):
                        last = pe.transpose(bank_t[j][:, c * T:(c + 1) * T],
                                            xn_all[:, it * LANES + j, c * P:(c + 1) * P], ident[0:T, 0:T])
                    last.then_inc(p["turned"].sem, 1)
                for j in range(LANES):
                    pe.wait_ge(*p["xT_ready"].at(it, 0, j))
                    matmuls(pe, bank_s[j][0:T, 0:E1], [(rxT[j][:, c, :], w_gate1[:, c, :]) for c in range(KC)])\
                        .then_inc(p["logits"].sem, 1)
                pe.wait_ge(*p["xT_spread"].at(it, 0, LANES - 1))
                pe.wait_ge(*p["lexp"].at(it, 0, LANES - 1))
            pe.wait_ge(*p["scored"].at(ITERS - 1, 0, LANES - 1))
            pe.transpose(bank[0][:, 0:T], score.rearrange("t b e -> t (b e)"), ident[0:T, 0:T]).then_inc(s_topT, 1)
            pe.wait_ge(s_topstep, 7)
            for c in range(CAP):
                last = pe.matmul(bank[4 + c // 4][0:T, c % 4 * P:(c % 4 + 1) * P],
                                 topf[:, c:c + 1].broadcast_to([P, T]), ident[:, :], start=True, stop=True)
            last.then_inc(s_idx, 1)
            for b in range(B):
                if b == 0:
                    pe.wait_ge(s_sel, 4)
                for k in range(KC):
                    last = pe.matmul(bank[b][:, k * CAP * E1:(k + 1) * CAP * E1], xn_all[:, b, k * P:(k + 1) * P],
                                     sel[:, :, b * E1:(b + 1) * E1], start=True, stop=True)
                last.then_inc(s_gather, 1)
            pe.wait_ge(s_sel, 5)
            for b in range(B):
                pe.wait_ge(s_taken, b + 1)
                for h in range(2):
                    g0 = b * E1 + h * HALF_E
                    last = pe.transpose(bank[b][0:T, h * T:(h + 1) * T],
                                        selw[:, g0:g0 + HALF_E, :].rearrange("t e c -> t (e c)"), ident[0:T, 0:T])
                last.then_inc(s_selT, 1)

            def gate_up(s, wg, wu, rhs, sig):
                for dst, w in ((bank[3 * s], wg), (bank[3 * s + 1], wu)):
                    for m in range(4):
                        last = matmuls(pe, dst[:, m * T:(m + 1) * T],
                                       [(w[:, c, m * P:(m + 1) * P], rhs(c)) for c in range(KC)])
                last.then_inc(sig.sem, 1)

            pe.wait_ge(s_selTk, B)
            with pe.Fori(0, E1 // 2) as i:
                for s in range(2):
                    pe.wait_ge(s_ew[s], i * 48 + 48)
                    wg, wu, wd = expert_slot(s)
                    gate_up(s, wg, wu, lambda c: taken[:, c, i * 2 + s, :], p_ex["gu_out"])
                for s in range(2):
                    wg, wu, wd = expert_slot(s)
                    pe.wait_ge(*p_ex["e_hid"].at(i, 0, s))
                    matmuls(pe, bank[3 * s + 2][0:T, 0:C],
                            [(hbuf[s][:, m * T:(m + 1) * T], wd[:, m, :]) for m in range(4)])\
                        .then_inc(p_ex["e_out"].sem, 1)
                pe.wait_ge(*p_ex["e_kept"].at(i, 0, 1))
            for i in range(B // 2):
                for s in range(2):
                    b = 2 * i + s
                    gate_up(s, w_sg, w_su, lambda c: xnT_all[:, c, b, :], p_sh["gu_out"])
                for s in range(2):
                    b = 2 * i + s
                    if b == 0:
                        pe.wait_ge(s_rows_in, 16 * E1)
                    pe.wait_ge(*p_sh["e_hid"].at(i, 0, s))
                    matmuls(pe, bank[3 * s + 2][0:T, 0:C],
                            [(hbuf[s][:, m * T:(m + 1) * T], w_sd[:, m, :]) for m in range(4)]
                            + [(selT[:, b, h, :], expert_rows[:, b, h, :]) for h in range(2)])\
                        .then_inc(p_sh["e_out"].sem, 1)
                pe.wait_ge(*p_sh["sh_added"].at(i, 0, 1))
            with pe.Fori(0, ITERS) as it:
                p = p_l2x
                turn(pe, p, it, 0, 0, xn)
                attend_tensor(pe, a2, p, it, 0, None, lambda j: cT[j], ctx_ready("l2"))
                project_out(pe, p, it, 0, w_o2, lambda j: p["o_T"].at(it, a2.tiles - 1, j))
            for l in range(2):
                p = p_f[l]
                if l == 1:
                    pe.wait_ge(s_wf1, 80)
                with pe.Fori(0, ITERS) as it:
                    turn(pe, p, it, 0, 1 - l, xn)
                    attend_tensor(pe, af[l], p, it, 0, None, lambda j: xT[j], None)
                    project_out(pe, p, it, 0, w_f[l][3], lambda j: p["o_T"].at(it, af[l].tiles - 1, j))
                    turn(pe, p, it, 1, 2 - l, xn)
                    for j in range(LANES):
                        pe.wait_ge(*(p["xT_ready"].at(it, 1, j) if l == 0 else p["hmean_ready"].at(it, 0, j)))
                        lhs = [xT[j][:, c, :] if l == 0 else hmean[:, 1, j, c:c + 1].broadcast_to([P, T])
                               for c in range(KC)]
                        matmuls(pe, bank_s[j][0:T, 0:E2], [(lhs[c], w_f[l][4][:, c, :]) for c in range(KC)])\
                            .then_inc(p["g_out"].sem, 1)
                    for j in range(LANES):
                        pe.wait_ge(*p["g_cw"].at(it))
                        pe.wait_ge(*p["h_spread"].at(it, 0, j))
                        pe.transpose(bank_t[j][0:E2, 0:T], gsm[:, 4, j, :], ident[0:T, 0:T]).then_inc(p["cw_turned"].sem, 1)
                    for j in range(LANES):
                        if j == 0:
                            pe.wait_ge(s_rows2, 32)
                        pe.wait_ge(*p["cwT_ready"].at(it, 0, j))
                        matmuls(pe, bank_s[j][0:T, 0:C], [(E[j][0:E2, 0:T], rows[0:E2, 12 + l, :])])\
                            .then_inc(p["b2_out"].sem, 1)
                pe.wait_ge(*end[f"f{l}"])

                if l == 1:
                    p = p_m[1]

                    def pair_hidden(it, r):
                        w1, _ = seq_slot(r % SEQ_SLOTS)
                        pe.wait_ge(s_qw[r % SEQ_SLOTS], it * (48 * SEQ_ITEMS // SEQ_SLOTS)
                                   + 48 * (r // SEQ_SLOTS + 1))
                        for half in range(2):
                            if r >= 2:
                                pe.wait_ge(*p["h_gelu"].at(it, 2 * (r - 2) + half))
                            for m in range(4 * half, 4 * half + 4):
                                last = matmuls(pe, bank[r % 2 * 2 + half][:, m % 4 * T:(m % 4 + 1) * T],
                                               [(w1[:, c, m * P:(m + 1) * P],
                                                 h2w[r // TOP2][:, bass.ds(it, 1), c * T:(c + 1) * T])
                                                for c in range(KC)])
                            last.then_inc(p["h_out"].sem, 1)

                    def pair_outputs(it, r):
                        _, w2 = seq_slot(r % SEQ_SLOTS)
                        if r >= 2:
                            pe.wait_ge(*p["y_added"].at(it, r - 2))
                        pe.wait_ge(*p["h_gelu"].at(it, 2 * r + 1))
                        matmuls(pe, bank[4 + r % 2][0:T, 0:C],
                                [(seq_hid(r % 2)[:, m * T:(m + 1) * T], w2[:, m, :]) for m in range(8)])\
                            .then_inc(p["y_out"].sem, 1)

                    with pe.Fori(0, ITERS) as it:
                        pair_hidden(it, 0)
                        for r in range(SEQ_ITEMS):
                            if r + 1 < SEQ_ITEMS:
                                pair_hidden(it, r + 1)
                            pair_outputs(it, r)
                        pe.wait_ge(*p["y_added"].at(it, SEQ_ITEMS - 1))
                    continue

                def hidden(i, q):
                    w1, _ = moe_slot(q // 2)
                    for m in range(8):
                        r = q * 8 + m
                        if r >= 4:
                            pe.wait_ge(*p_m[l]["h_gelu"].at(i, r - 4))
                        matmuls(pe, bank[m % 4][:, 0:HALF_T],
                                [(w1[:, c, m * P:(m + 1) * P], h2T[q % 2][c]) for c in range(KC)])\
                            .then_inc(p_m[l]["h_out"].sem, 1)

                def outputs(i, q):
                    _, w2 = moe_slot(q // 2)
                    pe.wait_ge(*p_m[l]["h_gelu"].at(i, q * 8 + 7))
                    for j in range(LANES):
                        r = q * 4 + j
                        if q >= 1:
                            pe.wait_ge(*p_m[l]["y_added"].at(i, r - 4))
                        matmuls(pe, bank[4 + j][0:T, 0:C],
                                [(hid(q % 2, m)[:, j * T:(j + 1) * T], w2[:, m, :]) for m in range(8)])\
                            .then_inc(p_m[l]["y_out"].sem, 1)

                with pe.Fori(0, E2 // 2) as i:
                    pe.wait_ge(s_mw[0], i * 32 + (l * (E2 // 2) * 32 + 32))
                    hidden(i, 0)
                    hidden(i, 1)
                    outputs(i, 0)
                    pe.wait_ge(s_mw[1], i * 32 + (l * (E2 // 2) * 32 + 32))
                    hidden(i, 2)
                    outputs(i, 1)
                    hidden(i, 3)
                    outputs(i, 2)
                    outputs(i, 3)
                    pe.wait_ge(*p_m[l]["y_added"].at(i, 15))
            pe.wait_ge(s_abs, 3)
            pe.wait_ge(s_one, 1)
            pe.matmul(bank[0][:, 0:3], one_col[:, 0:1].broadcast_to([P, P]), wabs[:, 0, :], start=True, stop=True)\
                .then_inc(s_wsum, 1)
            pe.wait_ge(s_wl3, 64)
            pe.wait_ge(s_wmean, 1)
            with pe.Fori(0, ITERS) as it:
                p = p_l3x
                turn(pe, p, it, 0, 0, xn)
                attend_tensor(pe, a3, p, it, 0, None, lambda j: cT[j], ctx_ready("l3"))
                project_out(pe, p, it, 0, w_o3, lambda j: p["o_T"].at(it, a3.tiles - 1, j))
            pe.wait_ge(s_tern, 9)
            with pe.Fori(0, ITERS) as it:
                p = p_l3f
                for j in range(LANES):
                    pe.wait_ge(*p["q_ready"].at(it, 0, j))
                    for c in range(KC):
                        last = pe.transpose(bank_bf[4 + j][:, c * T:(c + 1) * T],
                                            qx[j][:, c * P:(c + 1) * P], ident_bf[0:T, 0:T])
                    last.then_inc(p["turned"].sem, 1)
                for h in range(2):
                    for j in range(LANES):
                        if h == 0:
                            pe.wait_ge(*p["xq_ready"].at(it, 0, j))
                        else:
                            pe.wait_ge(*p["h_part"].at(it, 0, j))
                        for dst, w in ((bank_s[j], w_tg), (bank_t[j], w_tu)):
                            last = matmuls(pe, dst[0:T, :], [(xqT[j][:, c, :], w[:, c, h * 512:(h + 1) * 512])
                                                             for c in range(KC)])
                        last.then_inc(p["g_u_out"].sem, 1)
                for j in range(LANES):
                    pe.wait_ge(*p["q2_ready"].at(it, 0, j))
                    for c in range(8):
                        last = pe.transpose(bank_bf[j][:, c * T:(c + 1) * T], hq[j][:, c * P:(c + 1) * P],
                                            ident_bf[0:T, 0:T])
                    last.then_inc(p["q2_turned"].sem, 1)
                for j in range(LANES):
                    pe.wait_ge(*p["q2T_ready"].at(it, 0, j))
                    matmuls(pe, bank_t[j][0:T, 0:C], [(hqT[j][:, c, :], w_td[:, c, :]) for c in range(8)])\
                        .then_inc(p["proj_out"].sem, 1)

        @block.vector
        def _(v):
            v.wait_ge(s_const, 16 * 9)
            v.tensor_copy(ident_bf[:, :], ident[:, :]).then_inc(s_omu, 1)
            v.tensor_scalar(omu[:, :], col("mu_r", 0, 4), -1.0, 1.0, ALU.mult, ALU.add).then_inc(s_omu, 1)
            v.wait_ge(s_x, 16)
            v.wait_ge(s_gates, 1)
            with v.Fori(0, ITERS) as it:
                p = p_l0x
                norm_stats(v, p, it, 0, lambda j: x_at(it, j))
                norm_apply(v, p, it, 0, lambda j: x_at(it, j), lambda j: xn[j])
                add_row(v, p, it, 0, row("sa_b"))
                for j in range(LANES):
                    v.wait_ge(*p["part"].at(it, 0, j))
                    v.tensor_tensor(y[j], y[j], xn[j], ALU.add).then_inc(p["summed"].sem, 1)
                norm_stats(v, p, it, 1, lambda j: y[j], lambda j: p["summed"].at(it, 0, j))
                norm_apply_affine(v, p, it, 1, 0, lambda j: y[j], lambda j: xa[j], row("ln1_g"), row("ln1_b"))
                attend_vector(v, a0, p, it)
                add_row(v, p, it, 1, row("l0_bo"))
                for j in range(LANES):
                    v.wait_ge(*p["part"].at(it, 1, j))
                    v.tensor_tensor(y[j], y[j], xa[j], ALU.add).then_inc(p["summed"].sem, 1)
                norm_stats(v, p, it, 2, lambda j: y[j], lambda j: p["summed"].at(it, 1, j))
                norm_apply_affine(v, p, it, 2, 1, lambda j: y[j], lambda j: xn[j], row("ln2_g"), row("ln2_b"))
                for j in range(LANES):
                    v.wait_ge(*p["hid"].at(it, 0, j))
                    for m in range(4, 8):
                        last = v.tensor_scalar(OT[j][:, m, :], bank_t[j][:, (m - 4) * T:(m - 3) * T],
                                               col("lin1_b", m), 0.0, ALU.add, ALU.max)
                    last.then_inc(p["hid_b"].sem, 1)
                add_row(v, p, it, 2, row("lin2_b"))
                for j in range(LANES):
                    v.wait_ge(*p["part"].at(it, 2, j))
                    v.tensor_tensor(y[j], y[j], xn[j], ALU.add).then_inc(p["summed"].sem, 1)
                norm_stats(v, p, it, 3, lambda j: y[j], lambda j: p["summed"].at(it, 2, j))
                norm_apply_affine(v, p, it, 3, 2, lambda j: y[j], lambda j: xa[j], row("ln3_g"), row("ln3_b"))
                add_gated(v, p, it, lambda j: xa[j], 0, lambda j: p["normed"].at(it, 3, j))
            v.wait_ge(*end["l0x"])
            for j in range(LANES):
                v.memset(cT[j][:, :, 0:1], 0.0).then_inc(s_shift0, 1)
            v.wait_ge(s_shift0, LANES)
            v.wait_ge(s_omu, 2)
            with v.Fori(0, ITERS) as it:
                p = p_l0f
                norm_stats(v, p, it, 0, lambda j: x_at(it, j))
                norm_apply(v, p, it, 0, lambda j: x_at(it, j), lambda j: xn[j])
                for j in range(LANES):
                    v.wait_ge(*p["xT_ready"].at(it, 0, j))
                    for i in range(4):
                        last = v.tensor_scalar(E[j][:, i * T:(i + 1) * T], cT[j][:, i % 2, 0:T], omu[:, i:i + 1],
                                               None, ALU.mult)
                    last.then_inc(p["mixed_r"].sem, 1)
                for j in range(LANES):
                    v.wait_ge(*p["mixed_r"].at(it, 0, j))
                    for i in range(4):
                        dst = qT[j][:, i, :] if i < 2 else PT[j][:, (i - 2) * T:(i - 1) * T]
                        last = v.scalar_tensor_tensor(dst, cT[j][:, i % 2, 1:T + 1], col("mu_r", i),
                                                      E[j][:, i * T:(i + 1) * T], ALU.mult, ALU.add)
                    last.then_inc(p["mixed"].sem, 1)
                for j in range(LANES):
                    v.wait_ge(*p["k_relu"].at(it, 0, j))
                    v.tensor_tensor(OT[j][:, 0:2, :], V[j][:, 0:2, 0:T], V[j][:, 0:2, 0:T], ALU.mult)\
                        .then_inc(p["k_sq"].sem, 1)
                for j in range(LANES):
                    v.wait_ge(*p["proj_out"].at(it, 0, j))
                    v.wait_ge(*p["sig"].at(it, 0, j))
                    v.tensor_tensor(xa[j], y[j], bank_s[j][0:T, 0:C], ALU.mult).then_inc(p["gated"].sem, 1)
                add_gated(v, p, it, lambda j: xa[j], 4, lambda j: p["gated"].at(it, 0, j))
            v.wait_ge(*end["l0f"])
            v.wait_ge(s_mask1, 16)
            v.tensor_scalar(maskb[0], maskb[0].bitcast(I32), 0.0, BIG, ALU.is_equal, ALU.mult).then_inc(s_mask1b, 1)
            v.wait_ge(s_mask1b, 1)
            with v.Fori(0, ITERS) as it:
                p = p_l1x
                norm_stats(v, p, it, 0, lambda j: x_at(it, j))
                norm_apply(v, p, it, 0, lambda j: x_at(it, j), lambda j: xn[j])
                attend_vector(v, a1, p, it)
                add_row(v, p, it, 0, row("l1_bo"))
                add_gated(v, p, it, lambda j: y[j], 1, lambda j: p["part"].at(it, 0, j))
            p = p_rt
            v.wait_ge(*end["l1x"])
            for it in range(ITERS):
                norm_stats(v, p, it, 0, lambda j: x_at(it, j))
                norm_apply(v, p, it, 0, lambda j: x_at(it, j), lambda j: xn_all[:, it * LANES + j, :])
                for j in range(LANES):
                    v.wait_ge(*p["logits"].at(it, 0, j))
                    v.tensor_reduce(rsc[:, 0, j:j + 1], bank_s[j][0:T, 0:E1], AX_X, ALU.max, negate=True)\
                        .then_inc(p["lmax"].sem, 1)
                for j in range(LANES):
                    v.wait_ge(*p["lexp"].at(it, 0, j))
                    v.reciprocal(rsc[:, 2, j:j + 1], rsc[:, 1, j:j + 1]).then_inc(p["linv"].sem, 1)
                for j in range(LANES):
                    v.wait_ge(*p["linv"].at(it, 0, j))
                    v.tensor_scalar(score[:, it * LANES + j, :], score[:, it * LANES + j, :], rsc[:, 2, j:j + 1],
                                    None, ALU.mult).then_inc(p["scored"].sem, 1)
            v.wait_ge(s_scoreT, 1)
            v.max(top16[:, 0:8], scoreT).then_inc(s_topstep, 1)
            v.wait_ge(s_topstep, 1)
            v.match_replace(scoreT2, top16[:, 0:8], scoreT, -1.0).then_inc(s_topstep, 1)
            v.max_index(topi16[:, 0:8], top16[:, 0:8], scoreT).then_inc(s_topstep, 1)
            v.wait_ge(s_topstep, 2)
            v.max(top16[:, 8:16], scoreT2).then_inc(s_topstep, 1)
            v.wait_ge(s_topstep, 4)
            v.max_index(topi16[:, 8:16], top16[:, 8:16], scoreT2).then_inc(s_topstep, 1)
            v.tensor_copy(topf[:, 0:8], topi16[:, 0:8]).then_inc(s_topstep, 1)
            v.wait_ge(s_topstep, 6)
            v.tensor_copy(topf[:, 8:CAP], topi16[:, 8:CAP]).then_inc(s_topstep, 1)
            v.wait_ge(s_idx, 1)
            for k in range(4):
                n = min(4, CAP - 4 * k)
                v.tensor_scalar(sel[:, 4 * k:4 * k + n, :], three(bank[4 + k][0:T, 0:n * P], n), iota[0:T, 0:1],
                                None, ALU.is_equal).then_inc(s_sel, 1)
            v.wait_ge(s_sel, 4)
            v.tensor_tensor(selw.rearrange("t g c -> t c g"), sel, score.rearrange("t b e -> t (b e)").unsqueeze(1).broadcast_to([T, CAP, P]),
                            ALU.mult).then_inc(s_sel, 1)
            for b in range(B):
                v.wait_ge(s_selT, b + 1)
                v.tensor_copy(selT[:, b, :, :], three(bank[b][0:T, 0:2 * T], 2)).then_inc(s_selTk, 1)
            with v.Fori(0, E1 // 2) as i:
                for s in range(2):
                    v.wait_ge(*p_ex["e_gelu"].at(i, 0, s))
                    v.tensor_tensor(hbuf[s], hbuf[s], bank[3 * s + 1][:, 0:4 * T], ALU.mult).then_inc(p_ex["e_hid"].sem, 1)
            for i in range(B // 2):
                for s in range(2):
                    v.wait_ge(*p_sh["e_gelu"].at(i, 0, s))
                    v.tensor_tensor(hbuf[s], hbuf[s], bank[3 * s + 1][:, 0:4 * T], ALU.mult).then_inc(p_sh["e_hid"].sem, 1)
                for s in range(2):
                    b = 2 * i + s
                    v.wait_ge(*p_sh["e_out"].at(i, 0, s))
                    v.scalar_tensor_tensor(X[:, b, :], bank[3 * s + 2][0:T, 0:C], gates[0:T, 5:6], X[:, b, :],
                                           ALU.mult, ALU.add).then_inc(p_sh["sh_added"].sem, 1)
            v.wait_ge(*end["sh"])
            with v.Fori(0, ITERS) as it:
                p = p_l2x
                norm_stats(v, p, it, 0, lambda j: x_at(it, j))
                norm_apply(v, p, it, 0, lambda j: x_at(it, j), lambda j: xn[j])
                for j in range(LANES):
                    v.wait_ge(s_maskl[j], it * 16 + 16)
                    v.tensor_scalar(maskb[j], maskb[j].bitcast(I32), 0.0, BIG, ALU.is_equal, ALU.mult)\
                        .then_inc(p["mask_ready"].sem, 1)
                v.wait_ge(*p["mask_ready"].at(it, 0, LANES - 1))
                attend_vector(v, a2, p, it)
                add_row(v, p, it, 0, row("l2_bo"))
                add_gated(v, p, it, lambda j: y[j], 2, lambda j: p["part"].at(it, 0, j))
            v.wait_ge(*end["l2x"])
            for l in range(2):
                p = p_f[l]
                if l == 1:
                    v.wait_ge(*end["m0"])
                v.wait_ge(s_rows2, 16 if l == 0 else 32)
                with v.Fori(0, ITERS) as it:
                    acc = lambda j: accs[j][:, it, :]
                    n = 0
                    if l == 0:
                        norm_stats(v, p, it, 0, lambda j: x_at(it, j))
                        norm_apply(v, p, it, 0, lambda j: x_at(it, j), acc)
                        n = 1
                    norm_stats(v, p, it, n, acc, (lambda j: p["normed"].at(it, 0, j)) if l == 0 else None)
                    norm_apply_affine(v, p, it, n, 0, acc, lambda j: xn[j], row2(l, "ln1_w"), row2(l, "ln1_b"))
                    attend_vector(v, af[l], p, it)
                    add_row(v, p, it, 0, row2(l, "bo"))
                    for j in range(LANES):
                        v.wait_ge(*p["part"].at(it, 0, j))
                        v.tensor_tensor(acc(j), acc(j), y[j], ALU.add).then_inc(p["summed"].sem, 1)
                    norm_stats(v, p, it, n + 1, acc, lambda j: p["summed"].at(it, 0, j))
                    norm_apply_affine(v, p, it, n + 1, 1, acc, lambda j: xn[j], row2(l, "ln2_w"), row2(l, "ln2_b"))
                    if l == 1:
                        for j in range(LANES):
                            v.wait_ge(*p["xT_ready"].at(it, 1, j))
                            v.tensor_reduce(hmean[:, 0, j, :], xT[j], AX_X, ALU.add).then_inc(p["hmean_sum"].sem, 1)
                        for j in range(LANES):
                            v.wait_ge(*p["hmean_sum"].at(it, 0, j))
                            v.tensor_scalar(hmean[:, 1, j, :], hmean[:, 0, j, :], 1.0 / T, None, ALU.mult)\
                                .then_inc(p["hmean_ready"].sem, 1)
                    for j in range(LANES):
                        v.wait_ge(*p["g_out"].at(it, 0, j))
                        v.tensor_tensor(gsm[:, 0, j, :], bank_s[j][0:T, 0:E2], gate_b[:, l, :], ALU.add)\
                            .then_inc(p["g_val"].sem, 1)
                    for j in range(LANES):
                        wait_first(v, *p["g_val"].at(it, 0, j))
                        v.max(gsm[:, 1, j, :], gsm[:, 0, j, :]).then_inc(p["g_maxed"].sem, 1)
                    for j in range(LANES):
                        wait_first(v, *p["g_maxed"].at(it, 0, j))
                        last = v.max_index(gix[:, j, :], gsm[:, 1, j, :], gsm[:, 0, j, :])
                    last.then_inc(p["g_top"].sem, 1)
                    v.tensor_tensor(tiny[:, 0, :], gsm[:, 1, :, 1], gsm[:, 1, :, 0], ALU.subtract)\
                        .then_inc(p["g_diff"].sem, 1)
                    v.wait_ge(*p["g_top"].at(it))
                    v.tensor_copy(gsm[:, 5, :, :], gix[:, :, :]).then_inc(p["g_topf"].sem, 1)
                    v.wait_ge(*p["g_exp"].at(it))
                    v.tensor_scalar(tiny[:, 2, :], tiny[:, 1, :], 1.0, None, ALU.add).then_inc(p["g_sum"].sem, 1)
                    v.wait_ge(*p["g_sum"].at(it))
                    v.reciprocal(tiny[:, 3, :], tiny[:, 2, :]).then_inc(p["g_w1"].sem, 1)
                    v.wait_ge(*p["g_w1"].at(it))
                    v.tensor_tensor(tiny[:, 4, :], tiny[:, 3, :], tiny[:, 1, :], ALU.mult).then_inc(p["g_w2"].sem, 1)
                    v.wait_ge(*p["g_w2"].at(it))
                    v.wait_ge(*p["g_topf"].at(it))
                    for j in range(LANES):
                        for k in range(2):
                            last = v.tensor_scalar(gsm[:, 2 + k, j, :], iota8[:, :], gsm[:, 5, j, k:k + 1],
                                                   tiny[:, 3 + k, j:j + 1], ALU.is_equal, ALU.mult)
                        last.then_inc(p["g_half"].sem, 1)
                    v.wait_ge(*p["g_half"].at(it, 0, LANES - 1))
                    v.tensor_tensor(gsm[:, 4, :, :], gsm[:, 2, :, :], gsm[:, 3, :, :], ALU.add).then_inc(p["g_cw"].sem, 1)
                    v.wait_ge(*p["g_cw"].at(it))
                    if l == 0:
                        v.tensor_copy(cw[:, bass.ds(it * LANES, LANES), :], gsm[:, 4, :, :])\
                            .then_inc(p["cw_spread"].sem, LANES)
                    else:
                        v.tensor_copy(cw[:, bass.ds(it * LANES, LANES), 0:TOP2],
                                      tiny[:, 3:3 + TOP2, :].rearrange("t k j -> t j k"))\
                            .then_inc(p["cw_spread"].sem, LANES)
                        v.tensor_copy(ids[:, bass.ds(it * LANES, LANES), :], gix[:, :, 0:TOP2])\
                            .then_inc(p["ids_ready"].sem, 1)
                    for j in range(LANES):
                        v.wait_ge(*p["b2_out"].at(it, 0, j))
                        v.tensor_tensor(acc(j), acc(j), bank_s[j][0:T, 0:C], ALU.add).then_inc(p["acc_ready"].sem, 1)
                v.wait_ge(*p["cw_spread"].at(ITERS - 1, 0, LANES - 1))
                v.wait_ge(*end[f"f{l}"])
                if l == 1:
                    with v.Fori(0, ITERS) as it:
                        for r in range(SEQ_ITEMS):
                            j, k = r // TOP2, r % TOP2
                            v.wait_ge(*p_m[1]["y_out"].at(it, r))
                            if k:
                                v.wait_ge(*p_m[1]["y_added"].at(it, r - 1))
                            dst = accs[j][:, it, :]
                            v.scalar_tensor_tensor(dst, bank[4 + r % 2][0:T, 0:C],
                                                   cw[:, bass.ds(it * LANES + j, 1), k], dst, ALU.mult, ALU.add)\
                                .then_inc(p_m[1]["y_added"].sem, 1)
                    v.wait_ge(*end["m1"])
                    continue
                with v.Fori(0, E2 // 2) as i:
                    for q in range(4):
                        for j in range(LANES):
                            r, b = q * 4 + j, q % 2 * LANES + j
                            v.wait_ge(*p_m[l]["y_out"].at(i, r))
                            if q >= 1:
                                v.wait_ge(*p_m[l]["y_added"].at(i, r - 4))
                            dst = accs[j][:, q % 2, :]
                            v.scalar_tensor_tensor(dst, bank[4 + j][0:T, 0:C],
                                                   cw[:, b, bass.ds(i * 2 + q // 2, 1)], dst, ALU.mult, ALU.add)\
                                .then_inc(p_m[l]["y_added"].sem, 1)
                    v.wait_ge(*p_m[l]["y_added"].at(i, 15))
            for b in range(B):
                dst = X[:, b, :]
                v.scalar_tensor_tensor(dst, accs[b % LANES][:, b // LANES, :], gates[0:T, 6:7], dst,
                                       ALU.mult, ALU.add).then_inc(s_gadd, 1)
            v.wait_ge(s_wsum, 1)
            v.tensor_scalar(wabs[:, 1, :], bank[0][:, 0:3], 1.0 / (C * FF), EPS, ALU.mult, ALU.max).then_inc(s_wmean, 1)
            v.wait_ge(s_wmean, 1)
            v.reciprocal(wabs[:, 2, :], wabs[:, 1, :]).then_inc(s_wmean, 1)
            v.wait_ge(s_gadd, B)
            with v.Fori(0, ITERS) as it:
                p = p_l3x
                norm_stats(v, p, it, 0, lambda j: x_at(it, j))
                norm_apply(v, p, it, 0, lambda j: x_at(it, j), lambda j: xn[j])
                attend_vector(v, a3, p, it)
                add_gated(v, p, it, lambda j: bank_s[j][0:T, 0:C], 3, lambda j: p["proj_out"].at(it, 0, j))
            v.wait_ge(*end["l3x"])
            with v.Fori(0, ITERS) as it:
                p = p_l3f
                norm_stats(v, p, it, 0, lambda j: x_at(it, j))
                norm_apply(v, p, it, 0, lambda j: x_at(it, j), lambda j: xn[j])
                for j in range(LANES):
                    v.wait_ge(*p["normed"].at(it, 0, j))
                    v.tensor_reduce(tiny[:, 0, j:j + 1], xn[j], AX_X, ALU.max, apply_absolute_value=True)\
                        .then_inc(p["amax_ready"].sem, 1)
                v.wait_ge(*p["amax_ready"].at(it, 0, LANES - 1))
                v.tensor_scalar(tiny[:, 1, :], tiny[:, 0, :], EPS, None, ALU.max).then_inc(p["tiny_done"].sem, 1)
                v.wait_ge(*p["tiny_done"].at(it, 0))
                v.reciprocal(tiny[:, 2, :], tiny[:, 1, :]).then_inc(p["tiny_done"].sem, 1)
                v.tensor_scalar(tiny[:, 4, :], tiny[:, 1, :], 1.0 / 127.0, wabs[0:T, 1, 0:1], ALU.mult, ALU.mult)\
                    .then_inc(p["tiny_done"].sem, 1)
                v.tensor_scalar(tiny[:, 5, :], tiny[:, 1, :], 1.0 / 127.0, wabs[0:T, 1, 1:2], ALU.mult, ALU.mult)\
                    .then_inc(p["tiny_done"].sem, 1)
                v.wait_ge(*p["tiny_done"].at(it, 1))
                v.tensor_scalar(tiny[:, 3, :], tiny[:, 2, :], 127.0, None, ALU.mult).then_inc(p["tiny_done"].sem, 1)
                v.wait_ge(*p["tiny_done"].at(it, 3))
                v.tensor_tensor(tiny[:, 6, :], tiny[:, 4, :], tiny[:, 4, :], ALU.mult).then_inc(p["tiny_done"].sem, 1)
                v.wait_ge(*p["tiny_done"].at(it, 5))
                v.tensor_tensor(tiny[:, 7, :], tiny[:, 6, :], tiny[:, 5, :], ALU.mult).then_inc(p["tiny_done"].sem, 1)
                for j in range(LANES):
                    v.tensor_scalar(y[j], xn[j], tiny[:, 3, j:j + 1], ROUND, ALU.mult, ALU.add).then_inc(p["rounded"].sem, 1)
                for j in range(LANES):
                    v.wait_ge(*p["rounded"].at(it, 0, j))
                    v.tensor_scalar(qx[j], y[j], ROUND, 127.0, ALU.subtract, ALU.min).then_inc(p["q_ready"].sem, 1)
                for j in range(LANES):
                    v.wait_ge(*p["turned"].at(it, 0, j))
                    v.tensor_scalar(xqT[j], three(bank_bf[4 + j][:, 0:2 * T], 2), -128.0, None, ALU.max)\
                        .then_inc(p["xq_ready"].sem, 1)
                for h in range(2):
                    for j in range(LANES):
                        v.wait_ge(*p["g_sq"].at(it, h, j))
                        v.tensor_tensor(wide[j][0:T, h * 512:(h + 1) * 512], ga[j], bank_t[j][0:T, :], ALU.mult)\
                            .then_inc(p["h_part"].sem, 1)
                for j in range(LANES):
                    v.wait_ge(*p["h_part"].at(it, 1, j))
                    v.tensor_reduce(tiny[:, 8, j:j + 1], wide[j][0:T, :], AX_X, ALU.max, apply_absolute_value=True)\
                        .then_inc(p["amax2_ready"].sem, 1)
                v.wait_ge(*p["amax2_ready"].at(it, 0, LANES - 1))
                v.tensor_tensor(tiny[:, 9, :], tiny[:, 8, :], tiny[:, 7, :], ALU.mult).then_inc(p["tiny_done"].sem, 1)
                v.wait_ge(*p["tiny_done"].at(it, 7))
                v.tensor_scalar(tiny[:, 10, :], tiny[:, 9, :], EPS, None, ALU.max).then_inc(p["tiny_done"].sem, 1)
                v.wait_ge(*p["tiny_done"].at(it, 8))
                v.reciprocal(tiny[:, 11, :], tiny[:, 10, :]).then_inc(p["tiny_done"].sem, 1)
                v.tensor_scalar(tiny[:, 13, :], tiny[:, 10, :], 1.0 / 127.0, wabs[0:T, 1, 2:3], ALU.mult, ALU.mult)\
                    .then_inc(p["tiny_done"].sem, 1)
                v.wait_ge(*p["tiny_done"].at(it, 9))
                v.scalar_tensor_tensor(tiny[:, 12, :], tiny[:, 11, :], 127.0, tiny[:, 7, :], ALU.mult, ALU.mult)\
                    .then_inc(p["tiny_done"].sem, 1)
                v.wait_ge(*p["tiny_done"].at(it, 11))
                for j in range(LANES):
                    v.tensor_scalar(wide[j][0:T, :], wide[j][0:T, :], tiny[:, 12, j:j + 1], ROUND, ALU.mult, ALU.add)\
                        .then_inc(p["rounded2"].sem, 1)
                for j in range(LANES):
                    v.wait_ge(*p["rounded2"].at(it, 0, j))
                    v.tensor_scalar(hq[j], wide[j][0:T, :], ROUND, 127.0, ALU.subtract, ALU.min)\
                        .then_inc(p["q2_ready"].sem, 1)
                for j in range(LANES):
                    v.wait_ge(*p["q2_turned"].at(it, 0, j))
                    v.tensor_scalar(hqT[j], three(bank_bf[j][:, 0:8 * T], 8), -128.0, None, ALU.max)\
                        .then_inc(p["q2T_ready"].sem, 1)
                for j in range(LANES):
                    v.wait_ge(*p["proj_out"].at(it, 0, j))
                    v.tensor_scalar(y[j], bank_t[j][0:T, 0:C], tiny[:, 13, j:j + 1], gates[0:T, 7:8], ALU.mult,
                                    ALU.mult).then_inc(p["out_scaled"].sem, 1)
                for j in range(LANES):
                    v.wait_ge(*p["out_scaled"].at(it, 0, j))
                    v.tensor_tensor(x_at(it, j), x_at(it, j), y[j], ALU.add).then_inc(p["x_added"].sem, 1)


def _lay_out(i):
    f = lambda n: np.asarray(i[n])
    tr = lambda a: np.ascontiguousarray(np.swapaxes(a, -1, -2))
    columns = lambda v: v.reshape(-1, P).T

    a = {"x": f("x"), "ctxT": np.ascontiguousarray(f("ctx_1024").transpose(2, 0, 1)),
         "mask1": f("mask_1xSxS2_ik0"), "mask2": f("mask_BxSxS2_ik1")}
    a["identity"] = np.eye(P, dtype=np.float32)
    a["iota"] = np.arange(P, dtype=np.float32).reshape(P, 1)
    a["iota8"] = np.arange(E2, dtype=np.float32)
    n = np.arange(T)
    a["causal"] = np.where(n[None, :] > n[:, None], np.float32(BIG), np.float32(0))
    a["gates"] = np.concatenate([f("g_xattn"), f("g_ffn")])
    w, b = tr(f("L0_xattn_in_proj_w")), f("L0_xattn_in_proj_b")
    a["l0_wsv"] = np.ascontiguousarray(tr(f("L0_xattn_qkv_w"))[:, 2 * C:])
    a["l0_wso"] = tr(f("L0_xattn_sa_out_w"))
    for k, n in enumerate(("l0_wq", "l0_wk", "l0_wv")):
        a[n] = np.ascontiguousarray(w[:, k * C:(k + 1) * C])
    a["l0_wo"], a["l0_w1"], a["l0_w2"] = (tr(f("L0_xattn_" + n)) for n in ("mha_out_w", "lin1_w", "lin2_w"))
    a["l0_wr"], a["l0_wkk"], a["l0_wvv"] = (tr(f("L0_ffn_" + n)) for n in ("W_r", "W_k", "W_v"))
    a["l1_wq"], a["l1_wk"], a["l1_wv"], a["l1_wo"] = (f("L1_xattn_" + n) for n in ("Wq", "Wk", "Wv", "Wo"))
    a["l1_gate"] = tr(f("L1_ffn_gate_w"))
    a["e_wg"], a["e_wu"], a["e_wd"] = (tr(f("L1_ffn_" + n)) for n in ("Wg", "Wu", "Wd"))
    a["ws_g"], a["ws_u"], a["ws_d"] = (tr(f("L1_ffn_" + n)) for n in ("Ws_g", "Ws_u", "Ws_d"))
    a["l2_wq"] = tr(f("L2_xattn_Wq"))
    a["l2_wk"], a["l2_wv"], a["l2_wo"] = (tr(f("L2_xattn_" + n)) for n in ("Wk", "Wv", "Wo"))
    for l in range(2):
        for n in ("wq", "wk", "wv", "wo"):
            a[f"f{l}_{n}"] = f("L2_ffn_" + n)[l]
        a[f"f{l}_gate"] = f("L2_ffn_gate_w")[l]
    a["moe_gate_b"] = f("L2_ffn_gate_b")
    a["moe_w1"], a["moe_w2"] = f("L2_ffn_e_w1"), f("L2_ffn_e_w2")
    a["moe_b1"] = np.ascontiguousarray(f("L2_ffn_e_b1").reshape(2, E2 * 8, P).transpose(2, 0, 1))
    a["moe_b2"] = np.ascontiguousarray(f("L2_ffn_e_b2").transpose(1, 0, 2))
    a["l3_wq"], a["l3_wk"], a["l3_wv"], a["l3_wo"] = (f("L3_xattn_" + n) for n in ("w_q", "w_k", "w_v", "w_o"))
    for n, m in (("raw_g", "w_gate"), ("raw_u", "w_up"), ("raw_d", "w_down")):
        t = tr(f("L3_ffn_" + m))
        a[n] = np.ascontiguousarray(t.reshape(-1, P, t.shape[1]).transpose(1, 0, 2).reshape(P, -1))
    vec = {"l0_sv": f("L0_xattn_qkv_b")[2 * C:], "l0_bq": b[0:C], "l0_bk": b[C:2 * C],
           "lin1_b": f("L0_xattn_lin1_b"), "mu_r": f("L0_ffn_mu_r"), "mu_k": f("L0_ffn_mu_k"),
           "l1_bq": f("L1_xattn_bq"), "l1_bk": f("L1_xattn_bk"), "l2_bq": f("L2_xattn_bq"),
           "l2_bk": f("L2_xattn_bk")}
    for l in range(2):
        vec[f"f{l}_bq"] = f("L2_ffn_bq")[l]
        vec[f"f{l}_bk"] = f("L2_ffn_bk")[l]
    vec["head_rows"] = np.concatenate([(np.arange(P) // d == h).astype(np.float32)
                                       for d in (16, 32, 64) for h in range(P // d)])
    a["columns"] = np.ascontiguousarray(np.concatenate([columns(vec[n]) for n in COLS], 1))
    r = {"sa_b": f("L0_xattn_sa_out_b"), "ln1_g": f("L0_xattn_ln1_g"), "ln1_b": f("L0_xattn_ln1_b"),
         "l0_bv": b[2 * C:], "l0_bo": f("L0_xattn_mha_out_b"), "ln2_g": f("L0_xattn_ln2_g"),
         "ln2_b": f("L0_xattn_ln2_b"), "lin2_b": f("L0_xattn_lin2_b"), "ln3_g": f("L0_xattn_ln3_g"),
         "ln3_b": f("L0_xattn_ln3_b"), "l1_bv": np.pad(f("L1_xattn_bv"), (0, C - P)), "l1_bo": f("L1_xattn_bo"),
         "l2_bv": f("L2_xattn_bv"), "l2_bo": f("L2_xattn_bo")}
    a["rows"] = np.stack([r[n] for n in ROWS])
    a["rows2"] = np.stack([f("L2_ffn_" + n)[l] for l in range(2) for n in ROWS2])
    return a


def kernel(**inputs):
    import concourse.bacc as bacc
    from concourse.bass_utils import run_bass_kernel_spmd

    nc = bacc.Bacc("TRN2", target_bir_lowering=False, num_devices=1)
    arrays, aps = {}, {}
    for name, a in _lay_out(inputs).items():
        a = np.ascontiguousarray(a)
        arrays["in_" + name] = a
        aps[name] = nc.dram_tensor("in_" + name, a.shape, mybir.dt.from_np(a.dtype), kind="ExternalInput").ap()
    out = nc.dram_tensor("out_x", (B, T, C), F32, kind="ExternalOutput").ap()
    flamingo(nc, aps, out)
    return run_bass_kernel_spmd(nc, [arrays], core_ids=[0]).results[0]["out_x"]
```

```python
from contextlib import ExitStack

import numpy as np

import concourse.bass as bass
from concourse import mybir

F32 = mybir.dt.float32
BF16 = mybir.dt.bfloat16
I32 = mybir.dt.int32
U32 = mybir.dt.uint32
ALU = mybir.AluOpType
ACT = mybir.ActivationFunctionType
AX_X = mybir.AxisListType.X

B, T, C = 8, 112, 256
S2 = 375
P = 128
KC = C // P
LANES = 4
ITERS = B // LANES
TOP2 = 2
PAIRS = B * TOP2
SEQ_ITEMS = LANES * TOP2
SEQ_SLOTS = 4
KEY_TILES, KEY_W = 3, S2 // 3
E1, FE = 16, 512
CAP = T * 2 // E1
HALF_E = E1 // 2
E2, FF = 8, 1024
MAX_OF = -(-B * T // P)
TOK_SLOTS = 4
MAX_CHUNKS = (B * T * TOP2 + E2 * (P - 1)) // P
MIN_TURNS = -(-B * T * TOP2 // (P * TOK_SLOTS))
MAX_TURNS = -(-MAX_CHUNKS // TOK_SLOTS)
EPS = 1e-5
BIG = 1.0e30
ROUND = 1.5 * 2.0 ** 23

ROWS = ["sa_b", "ln1_g", "ln1_b", "l0_bv", "l0_bo", "ln2_g", "ln2_b", "lin2_b", "ln3_g", "ln3_b",
        "l1_bv", "l1_bo", "l2_bv", "l2_bo"]
ROWS2 = ["ln1_w", "ln1_b", "bv", "bo", "ln2_w", "ln2_b"]
COLS = {"l0_sv": 2, "l0_bq": 2, "l0_bk": 2, "lin1_b": 8, "mu_r": 2, "mu_k": 2, "l1_bq": 1, "l1_bk": 1,
        "l2_bq": 2, "l2_bk": 2, "f0_bq": 2, "f0_bk": 2, "f1_bq": 2, "f1_bk": 2,
        "head_rows": 14}


class Signal:

    def __init__(self, sem, base, times, lanes):
        self.sem, self.base, self.times, self.lanes = sem, base, times, lanes

    def at(self, it, r=0, j=0):
        return self.sem, it * (self.times * self.lanes) + (self.base + r * self.lanes + j + 1)


def phase_signals(known, make, turns, one, lanes, times):
    signals = {}
    for name, n in times.items():
        if not n:
            continue
        width = 1 if name in one else lanes
        if name not in known:
            known[name] = [make(name), 0]
        sem, base = known[name]
        signals[name] = Signal(sem, base, n, width)
        known[name][1] = base + turns * n * width
    return signals


class Attention:

    def __init__(self, tiles, heads, d, keys, key_tiles, wq, wk, wv, bq=None, bk=None, bv=None,
                 mask=None, guard=False):
        self.tiles, self.heads, self.d, self.keys, self.key_tiles = tiles, heads, d, keys, key_tiles
        self.key_w = keys // key_tiles
        self.batch = min(4, heads)
        self.masks = None if heads == 1 else {8: 0, 4: 8, 2: 12}[heads]
        self.group = 4 if key_tiles == 1 else 1
        self.groups = heads // self.group
        self.wq, self.wk, self.wv, self.bq, self.bk, self.bv = wq, wk, wv, bq, bk, bv
        self.mask, self.guard, self.scale = mask, guard, float(d) ** -0.5


def flamingo(nc, A, out):
    ctx = ExitStack()
    with ctx:
        def sb(name, shape, dt=F32):
            return ctx.enter_context(nc.sbuf_tensor(name, shape, dt))

        def make(name):
            return ctx.enter_context(nc.semaphore(name))

        known = {}

        def phase(turns, one=(), lanes=LANES, **times):
            return phase_signals(known, make, turns, one, lanes, times)

        bank = [ctx.enter_context(nc.psum_tensor(f"bank{i}", [P, 512], F32)) for i in range(8)]
        bank_s, bank_t = bank[0:4], bank[4:8]
        bank_bf = [b[:, :].bitcast(BF16) for b in bank]

        X = sb("x_state", [T, B, C])
        ident = sb("identity", [P, P])
        ident_bf = sb("identity_bf", [P, P], BF16)
        iota = sb("token_number", [P, 1])
        causal = sb("causal_mask", [T, T])
        gates = sb("tanh_gates", [P, 8])
        cols = sb("columns", [P, sum(COLS.values()) ])
        rows = sb("rows", [P, len(ROWS), C])
        minus_half = sb("minus_half", [P, LANES])
        stats = sb("bn_sums", [T, LANES, 6])
        mv = sb("mean_var", [T, LANES, 2])
        veps = sb("var_eps", [T, LANES])
        rstd = sb("rstd", [T, LANES])
        rowmin = sb("rowmin", [T, LANES, 4])
        rowsum = sb("rowsum", [T, LANES, 4])
        rinv = sb("rinv", [T, LANES, 4])
        omu = sb("one_minus_mu", [P, 4])
        one_col = sb("one_column", [P, 1])
        iota8 = sb("expert_number", [T, E2])
        gate_b = sb("moe_gate_bias", [T, 2, E2])
        cw = sb("moe_weight", [T, B, TOP2])
        gsm = sb("gate_small", [T, 8, LANES, E2])
        gix = sb("gate_index", [T, LANES, E2], U32)
        ids = sb("seq_experts", [T, B, TOP2], I32)
        b1q = sb("moe_b1", [P, SEQ_SLOTS, FF // P])
        tok_slot = sb("token_slots", [T, PAIRS], U32)
        tok_ids = sb("chunk_experts", [1, MAX_TURNS * TOK_SLOTS + 1], I32)
        hmean = sb("h_mean", [P, 2, LANES, KC])
        tiny = sb("tiny", [T, 20, LANES])
        wabs = sb("weight_abs", [P, 3, 3])
        region0 = sb("region0", [P, 9728])
        region1 = sb("region1", [P, 8720])
        stream = sb("stream", [P, 8192])
        LB = 4864
        arena = sb("arena", [P, LANES * LB])

        at = {"n": 0}

        def cut(region, words, dt=F32):
            n = at["n"]
            at["n"] = n + words
            ap = region[:, n:n + words]
            return ap if dt == F32 else ap.bitcast(dt)

        def three(ap, k):
            return ap.rearrange("p (k n) -> p k n", k=k)

        w_sv, w_so = three(cut(region0, 512), 2), three(cut(region0, 512), 2)
        w_q0, w_k0, w_v0, w_o0 = (three(cut(region0, 512), 2) for _ in range(4))
        w_l1, w_l2 = three(cut(region0, 2048), 2), three(cut(region0, 2048), 8)
        w_r, w_k, w_v = (three(cut(region0, 512), 2) for _ in range(3))
        w_q1, w_k1, w_v1 = (three(cut(region0, 256), 2) for _ in range(3))
        w_o1 = three(cut(region0, 256), 1)
        assert at["n"] <= 9728
        at["n"] = 0
        w_q3, w_k3, w_v3 = (three(cut(region0, 2048), 2) for _ in range(3))
        w_o3 = three(cut(region0, 2048), 8)
        at["n"] = 0
        w_sg, w_su = three(cut(region1, 1024), 2), three(cut(region1, 1024), 2)
        w_sd = three(cut(region1, 1024), 4)
        w_gate1 = three(cut(region1, 32), 2)
        w_q2, w_k2, w_v2, w_o2 = (three(cut(region1, 512), 2) for _ in range(4))

        def f_weights():
            return [three(cut(region1, 512), 2) for _ in range(4)] + [three(cut(region1, 16), 2)]

        w_f = [f_weights()]
        assert at["n"] <= 8720
        at["n"] = 0
        w_f.append(f_weights())
        raw3 = [cut(region1, 2048) for _ in range(3)]
        assert at["n"] <= 8720
        tern = [region1[:, 0:1024].bitcast(BF16), region1[:, 1024:2048].bitcast(BF16), raw3[0][:, 0:1024].bitcast(BF16)]
        w_tg, w_tu, w_td = three(tern[0], 2), three(tern[1], 2), three(tern[2], 8)
        xn, xa, y, xT, cT, qT, kT, V, E, PT, O, wide, ga, accs, qm = ([] for _ in range(15))
        off = {}
        for j in range(LANES):
            at["n"] = j * LB
            xa.append(cut(arena, 256)[0:T, :])
            qm.append(three(arena[:, at["n"]:at["n"] + 4 * T], 4))
            xn.append(cut(arena, 256)[0:T, :])
            y.append(cut(arena, 256)[0:T, :])
            xT.append(three(cut(arena, 2 * T), 2))
            qT.append(three(cut(arena, 2 * T), 2))
            kT.append(cut(arena, S2))
            V.append(three(cut(arena, 3 * P), 3))
            off["e"] = at["n"] - j * LB
            E.append(cut(arena, 4 * T))
            PT.append(cut(arena, 4 * T))
            ga.append(arena[0:T, j * LB + off["e"]:j * LB + off["e"] + 512])
            O.append(cut(arena, P)[0:T, :])
            at["n"] += at["n"] % 2
            off["c"] = at["n"] - j * LB
            cT.append(three(cut(arena, 2 * S2), 2))
            off["w"] = at["n"] - j * LB
            wide.append(cut(arena, 1024))
            accs.append(three(arena[0:T, j * LB + off["w"] + 256:j * LB + off["w"] + 256 + 2 * C], 2))
            assert at["n"] <= (j + 1) * LB, at["n"] - j * LB
        assert 2 * 2 * 4 * T <= off["e"] * 1
        maskb = [w[0:T, 512:512 + S2] for w in wide]
        OT = [three(w[:, 0:8 * T], 8) for w in wide]
        qx = [a[:, 0:128].bitcast(BF16) for a in xa]
        xqT = [three(a[:, 0, :].bitcast(BF16), 2) for a in xT]
        hq = [a[0:T, :, :].rearrange("p k s -> p (k s)")[:, 0:512].bitcast(BF16) for a in cT]
        hqT = [three(arena[:, j * LB + off["e"]:j * LB + off["e"] + 4 * T].bitcast(BF16), 8) for j in range(LANES)]
        h2w = [three(arena[:, j * LB + off["c"]:j * LB + off["c"] + 2 * KC * T], 2) for j in range(LANES)]

        n = off["c"] + 72
        hrow = [three(arena[0:T, j * LB + n:j * LB + n + 2 * C], 2) for j in range(LANES)]
        n += 2 * C
        picks = arena[0:T, n:n + P].rearrange("t (g e) -> t g e", e=E2)
        picks_of = arena[0:T, n:n + P].rearrange("t (b k e) -> t b k e", k=TOP2, e=E2)
        before = arena[0:T, LB + n:LB + n + T]
        steps = arena[0:1, LB + n + T:LB + n + T + 30]
        groups_before = arena[:, 2 * LB + n:2 * LB + n + P]
        n += 3 * LB
        chunks_before = arena[0:E2, n:n + P]
        chunks_upto, whole = arena[0:E2, n + P:n + P + E2], arena[0:E2, n + P + E2:n + P + E2 + MAX_OF]
        of_expert = arena[:, n + P + 15:n + P + 15 + E2]
        assert n + P + 15 + E2 <= 3 * LB + off["w"]
        count = arena[:, 2048:2048 + T]
        place = arena[0:T, LB + 2048:LB + 2048 + P].rearrange("t (g e) -> t g e", e=E2)
        placef = arena[0:T, 2 * LB + 2048:2 * LB + 2048 + PAIRS]
        fill, used = arena[0:E2, 3 * LB + 2048:3 * LB + 2048 + MAX_OF], arena[0:E2, 3 * LB + 2060:3 * LB + 2061]
        held = arena[0:1, 3 * LB + 2100:3 * LB + 2100 + 240].rearrange("o (c e) -> o c e", e=E2)
        idf = arena[0:1, 3 * LB + 2400:3 * LB + 2430]
        tok_hid = [arena[:, s * LB + 2048:s * LB + 2048 + 8 * P] for s in range(2)]
        tok_x = [arena[:, (2 + s) * LB + 2048:(2 + s) * LB + 2048 + C] for s in range(2)]
        tok_xT = [three(arena[:, (2 + s) * LB + 2048 + C:(2 + s) * LB + 2048 + 2 * C], 2) for s in range(2)]
        tok_y = [arena[:, (2 + s % 2) * LB + 2048 + (2 + s // 2) * C:(2 + s % 2) * LB + 2048 + (3 + s // 2) * C]
                 for s in range(TOK_SLOTS)]
        tok_got = [arena[0:T, j * LB:j * LB + 4 * C].rearrange("t (i k c) -> t i k c", i=2, k=2)
                   for j in range(LANES)]

        def col(name, i=0, n=1):
            at_ = 0
            for k, v in COLS.items():
                if k == name:
                    return cols[:, at_ + i:at_ + i + n]
                at_ += v

        def row(name, n=T):
            return rows[0:n, ROWS.index(name), :]

        def row2(l, name, n=T):
            return rows[0:n, l * len(ROWS2) + ROWS2.index(name), :]

        def norm_counts(n, affine):
            return dict(stats_done=n, var_ready=n, veps_ready=n, rstd_ready=n, normed=n,
                        **({"scaled": affine} if affine else {}))

        def attn_counts(a, n=1):
            g = a.tiles * a.groups * n
            return dict(projected=a.tiles * n, qv_ready=a.tiles * n, k_ready=a.tiles * n, scores=g,
                        q_masked=g * a.group // a.batch if a.heads > 1 else 0, rowmin_ready=g, probs=g, probs_turned=g, probs_T=g, rinv_ready=g * (2 if a.guard else 1), heads_out=g,
                        heads_ready=g, o_turned=a.tiles * n, o_T=a.tiles * n)

        a0 = Attention(2, 4, 32, S2, KEY_TILES, w_q0, w_k0, w_v0, "l0_bq", "l0_bk", row("l0_bv", KEY_W))
        a1 = Attention(1, 1, 128, S2, KEY_TILES, w_q1, w_k1, w_v1, "l1_bq", "l1_bk", row("l1_bv", KEY_W),
                       mask=lambda j: maskb[0], guard=True)
        a2 = Attention(2, 8, 16, S2, KEY_TILES, w_q2, w_k2, w_v2, "l2_bq", "l2_bk", row("l2_bv", KEY_W),
                       mask=lambda j: maskb[j])
        af = [Attention(2, 8, 16, T, 1, w_f[l][0], w_f[l][1], w_f[l][2], f"f{l}_bq", f"f{l}_bk",
                        row2(l, "bv"), mask=lambda j: causal[:, :]) for l in range(2)]
        a3 = Attention(8, 2, 64, S2, KEY_TILES, w_q3, w_k3, w_v3)

        one = ("rstd_ready", "veps_ready")
        p_l0x = phase(ITERS, one, **norm_counts(4, 3), turned=3, xT_ready=3, self_v=1, self_vT=1,
                      proj_out=3, part=3, summed=3, x_added=1, hid=1, hid_a=1, hid_b=1, **attn_counts(a0))
        p_l0f = phase(ITERS, one, **norm_counts(1, 0), turned=1, xT_ready=1, shifted=1, mixed_r=1, mixed=1,
                      rk=1, k_relu=1, k_sq=1, sig=1, proj_out=1, gated=1, x_added=1)
        p_l1x = phase(ITERS, one, **norm_counts(1, 0), turned=1, xT_ready=1, proj_out=1, part=1, x_added=1,
                      **attn_counts(a1))
        p_rt = phase(ITERS, one, **norm_counts(1, 0), turned=1, xT_ready=1, xT_spread=1, logits=1, lmax=1,
                     lexp=1, linv=1, scored=1)
        two = dict(lanes=2)
        p_ex = phase(E1 // 2, gu_out=1, e_gelu=1, e_hid=1, e_out=1, e_kept=1, **two)
        p_sh = phase(B // 2, gu_out=1, e_gelu=1, e_hid=1, e_out=1, added=1, **two)
        p_l2x = phase(ITERS, one, **norm_counts(1, 0), turned=1, xT_ready=1, proj_out=1, part=1, x_added=1,
                      mask_ready=1, **attn_counts(a2))
        p_f, p_m = [], []
        gate_steps = ("g_top", "g_topf", "g_diff", "g_exp", "g_sum", "g_w1", "g_w2", "g_cw")
        for l in range(2):
            p_f.append(phase(ITERS, one + gate_steps + ("ids_ready",), **norm_counts(3 - l, 2), turned=2, xT_ready=2, h_spread=l, h_kept=1 - l,
                             proj_out=1, part=1, summed=1, hmean_sum=l, hmean_ready=l, ids_ready=l, g_out=1, g_val=1,
                             g_maxed=1, g_half=1, cw_turned=1, cwT_ready=1, cw_spread=1, b2_out=1, acc_ready=1,
                             **{n: 1 for n in gate_steps}, **attn_counts(af[l])))
        p_m.append(phase(MAX_TURNS, lanes=1, tok_turned=TOK_SLOTS, tok_xT=TOK_SLOTS, tok_h_out=2 * TOK_SLOTS,
                         tok_gelu=2 * TOK_SLOTS, tok_y_out=TOK_SLOTS, tok_y_kept=TOK_SLOTS))
        p_m.append(phase(ITERS, lanes=1, gu_out=2 * SEQ_ITEMS, e_gelu=2 * SEQ_ITEMS,
                         e_out=SEQ_ITEMS, added=SEQ_ITEMS))
        p_l3x = phase(ITERS, one, **norm_counts(1, 0), turned=1, xT_ready=1, proj_out=1, x_added=1,
                      **attn_counts(a3))
        p_l3f = phase(ITERS, one + ("tiny_done",), **norm_counts(1, 0), amax_ready=2, tiny_done=12, rounded=2,
                      q_ready=2, turned=1, xq_ready=1, g_u_out=2, g_relu=2, g_sq=2, h_part=2, 
                      q2_turned=1, q2T_ready=1, proj_out=1, out_scaled=1, x_added=1)
        (s_const, s_wl0, s_wl1, s_wl3, s_rows2, s_wf1, s_raw3, s_x, s_mask1, s_gates, s_omu, s_half, s_one,
         s_mask1b, s_shift0, s_topT, s_scoreT, s_topstep, s_idx, s_sel, s_gather, s_taken, s_selT, s_selTk,
         s_stored, s_rows_in, s_abs, s_wsum, s_wmean, s_tern, s_gadd, s_out) = (make(n) for n in (
             "constants_loaded", "weights_l0_loaded", "weights_l1_l2_loaded", "weights_l3_loaded",
             "rows2_loaded", "weights_f1_loaded", "raw_l3_loaded", "x_loaded", "mask1_loaded",
             "tanh_gates_ready", "one_minus_mu_ready", "minus_half_set", "one_set", "mask1_bias_ready",
             "shift_columns_zeroed", "score_turned", "scoreT_ready", "top_step_done", "indices_spread",
             "selection_ready", "gathered", "taken_ready", "selection_turned", "selT_ready",
             "expert_rows_stored", "expert_rows_loaded", "weights_abs_summed", "weights_sum_out",
             "weights_mean_step", "ternary_step", "x_gated_added", "out_stored"))
        s_ctx = [make(f"context_loaded{j}") for j in range(LANES)]
        s_maskl = [make(f"mask_loaded{j}") for j in range(LANES)]
        s_ew = [make(f"expert_weights_loaded{s}") for s in range(2)]
        s_tw = [make(f"token_moe_weights_loaded{s}") for s in range(TOK_SLOTS)]
        s_xr = [make(f"token_rows_loaded{s}") for s in range(2)]
        s_yst = [make(f"token_outputs_stored{s}") for s in range(2)]
        s_route, s_rmm, s_tokadd, s_scat, s_zero, s_rconst, s_tid, s_picks, s_rid, s_yg = (make(n) for n in (
            "routing_step", "routing_products", "token_outputs_added", "token_rows_scattered",
            "token_rows_zeroed", "routing_constants_loaded", "token_experts_ready", "pairs_picked", "chunk_experts_counted", "token_outputs_gathered"))
        s_qw = [make(f"seq_moe_weights_loaded{s}") for s in range(SEQ_SLOTS)]

        def wait_first(eng, sem, value):
            eng.wait_ge(sem, value)
            eng.nop(nofuse=True)

        def norm_stats(v, p, it, r, src, ready=None):
            for j in range(LANES):
                if ready is not None:
                    wait_first(v, *ready(j))
                v.bn_stats(stats[:, j, :], src(j)).then_inc(p["stats_done"].sem, 1)
            for j in range(LANES):
                wait_first(v, *p["stats_done"].at(it, r, j))
                v.bn_aggr(mv[:, j, :], stats[:, j, :]).then_inc(p["var_ready"].sem, 1)

        def norm_rstd(g, p, it, r):
            wait_first(g, *p["var_ready"].at(it, r, LANES - 1))
            g.tensor_scalar(veps[:, :], mv[:, :, 1], EPS, None, ALU.add).then_inc(p["veps_ready"].sem, 1)
            g.wait_ge(*p["veps_ready"].at(it, r))
            g.tensor_tensor(rstd[:, :], veps[:, :], minus_half[0:T, :], ALU.pow).then_inc(p["rstd_ready"].sem, 1)

        def norm_apply(v, p, it, r, src, dst):
            v.wait_ge(*p["rstd_ready"].at(it, r))
            for j in range(LANES):
                v.tensor_scalar(dst(j), src(j), mv[:, j, 0:1], rstd[:, j:j + 1], ALU.subtract,
                                ALU.mult).then_inc(p["normed"].sem, 1)

        def norm_apply_affine(v, p, it, r, ra, src, dst, g, b):
            for j in range(LANES):
                v.wait_ge(*p["var_ready"].at(it, r, j))
                v.scalar_tensor_tensor(dst(j), src(j), mv[:, j, 0:1], g, ALU.subtract,
                                       ALU.mult).then_inc(p["scaled"].sem, 1)
            v.wait_ge(*p["rstd_ready"].at(it, r))
            for j in range(LANES):
                v.wait_ge(*p["scaled"].at(it, ra, j))
                v.scalar_tensor_tensor(dst(j), dst(j), rstd[:, j:j + 1], b, ALU.mult,
                                       ALU.add).then_inc(p["normed"].sem, 1)

        def turn(pe, p, it, r, rn, src):
            for j in range(LANES):
                pe.wait_ge(*p["normed"].at(it, rn, j))
                for c in range(KC):
                    last = pe.transpose(bank_t[j][:, c * T:(c + 1) * T], src[j][:, c * P:(c + 1) * P],
                                        ident[0:T, 0:T])
                last.then_inc(p["turned"].sem, 1)

        def keep_turned(act, p, it, r):
            for j in range(LANES):
                act.wait_ge(*p["turned"].at(it, r, j))
                act.copy(xT[j], three(bank_t[j][:, 0:2 * T], 2)).then_inc(p["xT_ready"].sem, 1)

        def matmuls(pe, dst, pairs):
            n = len(pairs)
            for i, (l, r) in enumerate(pairs):
                last = pe.matmul(dst, l, r, start=(i == 0), stop=(i == n - 1))
            return last

        def attend_tensor(pe, a, p, it, rx, source, keys_of, keys_ready):
            for m in range(a.tiles):
                f = slice(m * P, (m + 1) * P)
                for j in range(LANES):
                    if m == 0:
                        pe.wait_ge(*p["xT_ready"].at(it, rx, j))
                        if keys_ready is not None:
                            pe.wait_ge(*keys_ready(it, j))
                    else:
                        pe.wait_ge(*p["o_T"].at(it, m - 1, j))
                    q, k = xT[j], keys_of(j)
                    wq = a.wq
                    matmuls(pe, bank_t[j][:, 0:T], [(wq[:, c, f], q[:, c, :]) for c in range(KC)])
                    matmuls(pe, bank_s[j][:, 0:a.keys], [(a.wk[:, c, f], k[:, c, :]) for c in range(KC)])
                    for t in range(a.key_tiles):
                        ks = slice(t * a.key_w, (t + 1) * a.key_w)
                        last = matmuls(pe, bank_t[j][0:a.key_w, T + t * P:T + (t + 1) * P],
                                       [(k[:, c, ks], a.wv[:, c, f]) for c in range(KC)])
                    last.then_inc(p["projected"].sem, 1)
                for g in range(a.groups):
                    r = m * a.groups + g
                    heads = [g * a.group + i for i in range(a.group)]
                    for j in range(LANES):
                        if g == 0:
                            pe.wait_ge(*p["qv_ready"].at(it, m, j))
                            pe.wait_ge(*p["k_ready"].at(it, m, j))
                        else:
                            pe.wait_ge(*p["heads_ready"].at(it, r - 1, j))
                        if a.heads > 1 and heads[0] % a.batch == 0:
                            pe.wait_ge(*p["q_masked"].at(it, r * a.group // a.batch, j))
                        for i, h in enumerate(heads):
                            last = pe.matmul(bank_s[j][0:T, i * a.keys:(i + 1) * a.keys],
                                             qT[j][:, 0, :] if a.heads == 1 else qm[j][:, h % a.batch, :],
                                             kT[j][:, 0:a.keys], start=True, stop=True)
                        last.then_inc(p["scores"].sem, 1)
                    for j in range(LANES):
                        pe.wait_ge(*p["probs"].at(it, r, j))
                        for i in range(a.group * a.key_tiles):
                            last = pe.transpose(bank_t[j][0:a.key_w, i * T:(i + 1) * T],
                                                E[j][0:T, i * a.key_w:(i + 1) * a.key_w], ident[0:T, 0:T])
                        last.then_inc(p["probs_turned"].sem, 1)
                    for j in range(LANES):
                        pe.wait_ge(*p["probs_T"].at(it, r, j))
                        for i, h in enumerate(heads):
                            last = matmuls(pe, bank_s[j][0:T, i * a.d:(i + 1) * a.d],
                                           [(PT[j][0:a.key_w, (i * a.key_tiles + t) * T:(i * a.key_tiles + t + 1) * T],
                                             V[j][0:a.key_w, t, h * a.d:(h + 1) * a.d])
                                            for t in range(a.key_tiles)])
                        last.then_inc(p["heads_out"].sem, 1)
                for j in range(LANES):
                    pe.wait_ge(*p["heads_ready"].at(it, (m + 1) * a.groups - 1, j))
                    pe.transpose(bank_t[j][:, 0:T], O[j], ident[0:T, 0:T]).then_inc(p["o_turned"].sem, 1)

        def attend_vector(v, a, p, it):
            for m in range(a.tiles):
                for j in range(LANES):
                    v.wait_ge(*p["projected"].at(it, m, j))
                    ps = bank_t[j][:, 0:T]
                    if a.bq is None:
                        v.tensor_scalar(qT[j][:, 0, :], ps, -a.scale, None, ALU.mult)
                    else:
                        v.tensor_scalar(qT[j][:, 0, :], ps, col(a.bq, m), -a.scale, ALU.add, ALU.mult)
                    vs = three(bank_t[j][0:a.key_w, T:T + a.key_tiles * P], a.key_tiles)
                    vd = V[j][0:a.key_w, 0:a.key_tiles, :]
                    if a.bv is None:
                        last = v.tensor_copy(vd, vs)
                    else:
                        bv = a.bv[0:a.key_w, m * P:(m + 1) * P].unsqueeze(1).broadcast_to([a.key_w, a.key_tiles, P])
                        last = v.tensor_tensor(vd, vs, bv, ALU.add)
                    last.then_inc(p["qv_ready"].sem, 1)
                for g in range(a.groups):
                    r = m * a.groups + g
                    for j in range(LANES):
                        wait_first(v, *p["scores"].at(it, r, j))
                        if a.mask is None:
                            last = v.tensor_reduce(rowmin[:, j, 0:1], bank_s[j][0:T, 0:a.keys], AX_X, ALU.min)
                        else:
                            for i in range(a.group):
                                ks = slice(i * a.keys, (i + 1) * a.keys)
                                last = nc.vector.tensor_tensor_reduce(
                                    out=E[j][0:T, ks], in0=bank_s[j][0:T, ks], in1=a.mask(j), scale=1.0,
                                    scalar=3.0e38, op0=ALU.add, op1=ALU.min, accum_out=rowmin[:, j, i:i + 1])
                        last.then_inc(p["rowmin_ready"].sem, 1)
                    for j in range(LANES):
                        v.wait_ge(*p["probs"].at(it, r, j))
                        v.reciprocal(rinv[:, j, 0:a.group], rowsum[:, j, 0:a.group]).then_inc(p["rinv_ready"].sem, 1)
                    if a.guard:
                        for j in range(LANES):
                            v.wait_ge(*p["rinv_ready"].at(it, 2 * r, j))
                            v.scalar_tensor_tensor(rinv[:, j, 0:1], rowmin[:, j, 0:1], 0.5 * BIG, rinv[:, j, 0:1],
                                                   ALU.is_lt, ALU.mult).then_inc(p["rinv_ready"].sem, 1)
                    for j in range(LANES):
                        v.wait_ge(*p["heads_out"].at(it, r, j))
                        v.wait_ge(*(p["rinv_ready"].at(it, 2 * r + 1, j) if a.guard else p["rinv_ready"].at(it, r, j)))
                        dst = O[j][:, g * a.group * a.d:(g + 1) * a.group * a.d]
                        ps = bank_s[j][0:T, 0:a.group * a.d]
                        if a.group == 1:
                            last = v.tensor_scalar(dst, ps, rinv[:, j, 0:1], None, ALU.mult)
                        else:
                            last = v.tensor_tensor(three(dst, a.group), three(ps, a.group),
                                                   rinv[:, j, 0:a.group].unsqueeze(2).broadcast_to([T, a.group, a.d]),
                                                   ALU.mult)
                        last.then_inc(p["heads_ready"].sem, 1)

        def attend_scalar(act, a, p, it):
            for m in range(a.tiles):
                for j in range(LANES):
                    act.wait_ge(*p["projected"].at(it, m, j))
                    if a.bk is None:
                        last = act.copy(kT[j][:, 0:a.keys], bank_s[j][:, 0:a.keys])
                    else:
                        last = act.activation(kT[j][:, 0:a.keys], bank_s[j][:, 0:a.keys], ACT.Identity,
                                              bias=col(a.bk, m))
                    last.then_inc(p["k_ready"].sem, 1)
                for g in range(a.groups):
                    r = m * a.groups + g
                    for j in range(LANES):
                        act.wait_ge(*p["rowmin_ready"].at(it, r, j))
                        for i in range(a.group):
                            ks = slice(i * a.keys, (i + 1) * a.keys)
                            src = bank_s[j] if a.mask is None else E[j]
                            last = act.activation(E[j][0:T, ks], src[0:T, ks], ACT.Exp,
                                                  bias=rowmin[:, j, i:i + 1], scale=-1.0,
                                                  accum_out=rowsum[:, j, i:i + 1])
                        last.then_inc(p["probs"].sem, 1)
                    for j in range(LANES):
                        n = a.group * a.key_tiles * T
                        act.wait_ge(*p["probs_turned"].at(it, r, j))
                        act.copy(PT[j][0:a.key_w, 0:n], bank_t[j][0:a.key_w, 0:n]).then_inc(p["probs_T"].sem, 1)
                for j in range(LANES):
                    act.wait_ge(*p["o_turned"].at(it, m, j))
                    act.copy(OT[j][:, m, :], bank_t[j][:, 0:T]).then_inc(p["o_T"].sem, 1)

        def attend_gpsimd(g, a, p, it):
            per = a.heads // a.batch
            for m in range(a.tiles):
                for n in range(per):
                    for j in range(LANES):
                        g.wait_ge(*p["qv_ready"].at(it, m, j))
                        if n:
                            g.wait_ge(*p["scores"].at(it, m * a.groups + n * a.batch // a.group - 1, j))
                        rows_of = col("head_rows", a.masks + n * a.batch, a.batch)
                        g.tensor_tensor(qm[j][:, 0:a.batch, :],
                                        qT[j][:, 0:1, :].broadcast_to([P, a.batch, T]),
                                        rows_of.unsqueeze(2).broadcast_to([P, a.batch, T]), ALU.mult)\
                            .then_inc(p["q_masked"].sem, 1)

        def project_out(pe, p, it, r, w, ready):
            for j in range(LANES):
                pe.wait_ge(*ready(j))
                matmuls(pe, bank_s[j][0:T, 0:C], [(OT[j][:, c, :], w[:, c, :]) for c in range(w.shape[1])]) \
                    .then_inc(p["proj_out"].sem, 1)

        def x_at(it, j):
            return X[:, it * LANES + j, :]

        def add_gated(v, p, it, src, gate, ready):
            for j in range(LANES):
                v.wait_ge(*ready(j))
                v.scalar_tensor_tensor(x_at(it, j), src(j), gates[0:T, gate:gate + 1], x_at(it, j), ALU.mult,
                                       ALU.add).then_inc(p["x_added"].sem, 1)

        def add_row(v, p, it, r, b):
            for j in range(LANES):
                v.wait_ge(*p["proj_out"].at(it, r, j))
                v.tensor_tensor(y[j], bank_s[j][0:T, 0:C], b, ALU.add).then_inc(p["part"].sem, 1)

        at["n"] = 0
        xn_all = cut(arena, B * C)[0:T, :].rearrange("t (b c) -> t b c", b=B)
        sel = cut(arena, CAP * P)[0:T, :].rearrange("t (c g) -> t c g", c=CAP)
        selw = cut(arena, CAP * P)[0:T, :].rearrange("t (g c) -> t g c", c=CAP)
        expert_rows = arena[0:T, 0:2 * B * C].rearrange("s (b h f) -> s b h f", b=B, h=2)
        xnT_all = cut(arena, KC * B * T).rearrange("p (k b t) -> p k b t", k=KC, b=B)
        taken = cut(arena, KC * E1 * B * CAP).rearrange("p (k e n) -> p k e n", k=KC, e=E1)
        selT = cut(arena, B * 2 * T)[0:T, :].rearrange("s (b h t) -> s b h t", b=B, h=2)
        eo = cut(arena, E1 * C)[0:T, :].rearrange("s (e c) -> s e c", e=E1)
        hbuf = [cut(arena, 4 * T) for _ in range(2)]
        score = cut(arena, B * E1)[0:T, :].rearrange("t (b e) -> t b e", b=B)
        scoreT, scoreT2 = cut(arena, T), cut(arena, T)
        top16, topi16, topf = cut(arena, 16), cut(arena, 16, U32), cut(arena, CAP)
        rsc = cut(arena, 4 * LANES)[0:T, :].rearrange("t (n j) -> t n j", n=4)
        assert at["n"] <= LANES * LB, at["n"]
        at["n"] = 6144
        rxT = [three(cut(stream, KC * T), KC) for _ in range(LANES)]
        scratch = nc.dram_tensor("expert_out", (E1, B, CAP, C), F32, kind="Internal").ap()

        tok_rows = nc.dram_tensor("token_rows", ((MAX_TURNS * TOK_SLOTS + 2) * P, C), F32, kind="Internal").ap()
        tok_outs = nc.dram_tensor("token_outputs", (MAX_TURNS * TOK_SLOTS * P, C), F32, kind="Internal").ap()

        def expert_slot(s):
            n = s * 3072
            return (three(stream[:, n:n + 1024], 2), three(stream[:, n + 1024:n + 2048], 2),
                    three(stream[:, n + 2048:n + 3072], 4))

        def moe_slot(s):
            if s < 2:
                return (three(stream[:, s * 4096:s * 4096 + 2048], 2),
                        three(stream[:, s * 4096 + 2048:s * 4096 + 4096], 8))
            n = (s - 2) * 2 * LB
            return three(arena[:, n:n + 2048], 2), three(arena[:, n + LB:n + LB + 2048], 8)

        def seq_hid(s):
            return arena[:, s * LB + 2048:s * LB + 2048 + 8 * T]

        ctx_turn = {"l0": 0, "l1": 1, "l2": 2, "l3": 3}

        def ctx_ready(which):
            return lambda it, j: (s_ctx[j], it * 16 + (ctx_turn[which] * ITERS * 16 + 16))

        end = {k: (v.sem, v.base + n) for k, (v, n) in {
            "l0x": (p_l0x["x_added"], B), "l0f": (p_l0f["x_added"], B), "l1x": (p_l1x["x_added"], B),
            "sh": (p_sh["added"], B), "l2x": (p_l2x["x_added"], B), "l3x": (p_l3x["x_added"], B),
            "l3f": (p_l3f["x_added"], B), "f0": (p_f[0]["acc_ready"], B), "f1": (p_f[1]["acc_ready"], B),
            "m1": (p_m[1]["added"], ITERS * SEQ_ITEMS)}.items()}
        end["m0"] = (s_tokadd, PAIRS)

        block = ctx.enter_context(nc.Block())

        @block.sync
        def _(sp):
            def load(dst, src, s):
                sp.dma_start(dst, src).then_inc(s, 16)

            def weight(dst, name, s):
                load(dst, A[name].rearrange("(k p) n -> p k n", p=P), s)

            def context(which, it, j, before=None):
                if before is not None:
                    sp.wait_ge(*before)
                load(cT[j], A["ctxT"][:, it * LANES + j, :].rearrange("(k p) s -> p k s", p=P), s_ctx[j])

            load(X[:, :, :], A["x"].rearrange("b t c -> t b c"), s_x)
            load(ident[:, :], A["identity"], s_const)
            load(cols[:, :], A["columns"], s_const)
            load(rows[:, :, :], A["rows"].partition_broadcast(P), s_const)
            load(gates[:, :], A["gates"].partition_broadcast(P), s_const)
            load(causal[:, :], A["causal"], s_const)
            load(iota[:, :], A["iota"], s_const)
            load(iota8[:, :], A["iota8"].partition_broadcast(T), s_const)
            load(gate_b[:, :, :], A["moe_gate_b"].partition_broadcast(T), s_const)
            for dst, name in ((w_sv, "l0_wsv"), (w_so, "l0_wso"), (w_q0, "l0_wq"), (w_k0, "l0_wk"),
                              (w_v0, "l0_wv")):
                weight(dst, name, s_wl0)
            for j in range(LANES):
                context("l0", 0, j)
            for dst, name in ((w_o0, "l0_wo"), (w_l1, "l0_w1"), (w_l2, "l0_w2"), (w_r, "l0_wr"),
                              (w_k, "l0_wkk"), (w_v, "l0_wvv"), (w_q1, "l1_wq"), (w_k1, "l1_wk"),
                              (w_v1, "l1_wv"), (w_o1, "l1_wo")):
                weight(dst, name, s_wl0)
            for dst, name in ((w_sg, "ws_g"), (w_su, "ws_u"), (w_sd, "ws_d"), (w_gate1, "l1_gate"),
                              (w_q2, "l2_wq"), (w_k2, "l2_wk"), (w_v2, "l2_wv"), (w_o2, "l2_wo"),
                              (w_f[0][0], "f0_wq"), (w_f[0][1], "f0_wk"), (w_f[0][2], "f0_wv"),
                              (w_f[0][3], "f0_wo"), (w_f[0][4], "f0_gate")):
                weight(dst, name, s_wl1)

            load(tok_rows.rearrange("(c p) f -> c p f", p=P),
                 A["zeros"].unsqueeze(0).broadcast_to([MAX_TURNS * TOK_SLOTS + 2, P, C]), s_zero)
            n = MIN_TURNS * TOK_SLOTS
            load(tok_outs[n * P:, :].rearrange("(c p) f -> c p f", p=P),
                 A["zeros"].unsqueeze(0).broadcast_to([MAX_TURNS * TOK_SLOTS - n, P, C]), s_zero)

            def expert(e, s):
                wg, wu, wd = expert_slot(s)
                load(wg, A["e_wg"][e].rearrange("(k p) n -> p k n", p=P), s_ew[s])
                load(wu, A["e_wu"][e].rearrange("(k p) n -> p k n", p=P), s_ew[s])
                load(wd, A["e_wd"][e].rearrange("(k p) n -> p k n", p=P), s_ew[s])

            for s in range(2):
                expert(s, s)
            for j in range(LANES):
                context("l0", 1, j, p_l0x["projected"].at(0, a0.tiles - 1, j))
            sp.wait_ge(*end["l0x"])
            load(maskb[0].bitcast(I32), A["mask1"][0], s_mask1)
            sp.wait_ge(*end["l0f"])
            for j in range(LANES):
                context("l1", 0, j)
            for j in range(LANES):
                context("l1", 1, j, p_l1x["projected"].at(0, a1.tiles - 1, j))
            sp.wait_ge(*end["l1x"])
            load(rows[:, 0:2 * len(ROWS2), :], A["rows2"].partition_broadcast(P), s_rows2)
            for dst, name in ((w_q3, "l3_wq"), (w_k3, "l3_wk"), (w_v3, "l3_wv"), (w_o3, "l3_wo")):
                weight(dst, name, s_wl3)
            with sp.Fori(1, E1 // 2) as i:
                for s in range(2):
                    sp.wait_ge(*p_ex["e_out"].at(i - 1, 0, s))
                    expert(i * 2 + s, s)
            sp.wait_ge(s_stored, 16 * E1)
            sp.wait_ge(s_selTk, B)
            for e in range(E1):
                h, i = e // HALF_E, e % HALF_E
                load(expert_rows[i * CAP:(i + 1) * CAP, :, h, :], scratch[e].rearrange("b c f -> c b f"), s_rows_in)

            def chosen(l, s, sem, e):
                w1, w2 = moe_slot(s)
                load(w1, A["moe_w1"][l, bass.ds(e, 1)].rearrange("o (k p) n -> p (o k) n", p=P), sem)
                load(w2, A["moe_w2"][l, bass.ds(e, 1)].rearrange("o (k p) n -> p (o k) n", p=P), sem)
                load(b1q[:, s, :], A["moe_b1"][:, l, bass.ds(e * E2, E2)], sem)

            sp.wait_ge(*end["sh"])
            for dst, name in ((w_f[1][0], "f1_wq"), (w_f[1][1], "f1_wk"), (w_f[1][2], "f1_wv"),
                              (w_f[1][3], "f1_wo"), (w_f[1][4], "f1_gate")):
                weight(dst, name, s_wf1)
            for it in range(ITERS):
                for j in range(LANES):
                    context("l2", it, j, p_l2x["projected"].at(0, a2.tiles - 1, j) if it else None)
                    if it:
                        sp.wait_ge(*p_l2x["rowmin_ready"].at(0, a2.tiles * a2.groups - 1, j))
                    load(maskb[j].bitcast(I32), A["mask2"][it * LANES + j], s_maskl[j])
            sp.wait_ge(*end["l2x"])
            load(rows[0:E2, 12:14, :], A["moe_b2"], s_rows2)
            for dst, name in ((before, "before"), (steps, "steps"), (groups_before, "groups_before"),
                              (chunks_before, "chunks_before"), (chunks_upto, "chunks_upto"), (whole, "whole"),
                              (of_expert, "of_expert")):
                load(dst, A[name], s_rconst)
            sp.wait_ge(*end["f0"])
            for i in range(3):
                load(raw3[i], A[("raw_g", "raw_u", "raw_d")[i]], s_raw3)
            def chunk_expert(it, r):
                e = sp.value_load(tok_ids[0:1, bass.ds(it * TOK_SLOTS + r, 1)], min_val=0, max_val=E2 - 1)
                chosen(0, r, s_tw[r], e)

            sp.wait_ge(s_tid, 1)
            turns = sp.value_load(tok_ids[0:1, MAX_TURNS * TOK_SLOTS:MAX_TURNS * TOK_SLOTS + 1], min_val=MIN_TURNS,
                                  max_val=MAX_TURNS)
            for r in range(TOK_SLOTS):
                chunk_expert(0, r)
            with sp.Fori(1, turns) as it:
                for r in range(TOK_SLOTS):
                    sp.wait_ge(*p_m[0]["tok_y_out"].at(it - 1, r))
                    chunk_expert(it, r)
            sp.wait_ge(*end["m0"])

            def seq_expert(it, r):
                e = sp.value_load(ids[0:1, bass.ds(it * LANES + r // TOP2, 1), r % TOP2], min_val=0, max_val=E2 - 1)
                chosen(1, r % SEQ_SLOTS, s_qw[r % SEQ_SLOTS], e)

            for it in range(ITERS):
                sp.wait_ge(*p_f[1]["ids_ready"].at(it))
                for r in range(SEQ_ITEMS):
                    n = it * SEQ_ITEMS + r
                    if n == 2:
                        sp.wait_ge(*end["f1"])
                    if n >= SEQ_SLOTS:
                        sp.wait_ge(*p_m[1]["e_out"].at(0, n - SEQ_SLOTS))
                    seq_expert(it, r)
            sp.wait_ge(*end["m1"])
            for it in range(ITERS):
                for j in range(LANES):
                    context("l3", it, j, p_l3x["projected"].at(0, a3.tiles - 1, j) if it else None)
            for it in range(ITERS):
                for j in range(LANES):
                    sp.wait_ge(*p_l3f["x_added"].at(it, 0, j))
                    b = it * LANES + j
                    load(out[b], X[:, b, :], s_out)
            sp.wait_ge(s_out, 16 * B)

        @block.gpsimd
        def _(g):
            g.memset(minus_half[:, :], -0.5).then_inc(s_half, 1)
            g.memset(one_col[:, :], 1.0).then_inc(s_one, 1)
            g.wait_ge(s_half, 1)

            def chain(p, before, a=None, after=0):
                with g.Fori(0, ITERS) as it:
                    for r in range(before):
                        norm_rstd(g, p, it, r)
                    if a is not None:
                        attend_gpsimd(g, a, p, it)
                    for r in range(before, before + after):
                        norm_rstd(g, p, it, r)

            chain(p_l0x, 2, a0, 2)
            chain(p_l0f, 1)
            chain(p_l1x, 1)
            chain(p_rt, 1)
            chain(p_l2x, 1, a2)
            p = p_f[0]
            with g.Fori(0, ITERS) as it:
                for r in range(2):
                    norm_rstd(g, p, it, r)
                attend_gpsimd(g, af[0], p, it)
                norm_rstd(g, p, it, 2)
                for j in range(LANES):
                    g.wait_ge(*p["normed"].at(it, 2, j))
                    g.tensor_copy(hrow[j][:, it, :], xn[j]).then_inc(p["h_kept"].sem, 1)
            g.wait_ge(s_zero, 32)
            g.wait_ge(s_route, 8)
            g.wait_ge(*p["h_kept"].at(ITERS - 1, 0, LANES - 1))
            for b in range(B):
                for k in range(TOP2):
                    n = b * TOP2 + k
                    g.indirect_dma_start(tok_rows, bass.IndirectOffsetOnAxis(ap=tok_slot[:, n:n + 1], axis=0),
                                         hrow[b % LANES][:, b // LANES, :], None).then_inc(s_scat, 16)
            g.wait_ge(s_scat, 16 * PAIRS)
            g.wait_ge(s_tid, 1)
            turns = g.value_load(tok_ids[0:1, MAX_TURNS * TOK_SLOTS:MAX_TURNS * TOK_SLOTS + 1], min_val=MIN_TURNS,
                                 max_val=MAX_TURNS)

            def chunk_rows(it, r):
                g.dma_start(tok_x[r % 2], tok_rows[bass.ds((it * TOK_SLOTS + r) * P, P), :]).then_inc(s_xr[r % 2], 16)

            for r in range(2):
                chunk_rows(0, r)
            with g.Fori(0, turns) as it:
                p = p_m[0]
                for r in range(TOK_SLOTS):
                    wait_first(g, *p["tok_turned"].at(it, r))
                    chunk_rows(it, r + 2)
                    for n in ([r - 1] if r else []) + ([r] if r == TOK_SLOTS - 1 else []):
                        wait_first(g, *p["tok_y_kept"].at(it, n))
                        g.dma_start(tok_outs[bass.ds((it * TOK_SLOTS + n) * P, P), :], tok_y[n])\
                            .then_inc(s_yst[n % 2], 16)
            for s in range(2):
                wait_first(g, s_xr[s], turns * (8 * TOK_SLOTS) + 16)
                wait_first(g, s_yst[s], turns * (8 * TOK_SLOTS))
            for j in range(LANES):
                for i in range(ITERS):
                    for k in range(TOP2):
                        n = (i * LANES + j) * TOP2 + k
                        g.indirect_dma_start(tok_got[j][:, i, k, :], None, tok_outs,
                                             bass.IndirectOffsetOnAxis(ap=tok_slot[:, n:n + 1], axis=0))\
                            .then_inc(s_yg, 16)
            chain(p_f[1], 1, af[1], 1)
            g.wait_ge(s_wmean, 2)
            g.wait_ge(*end["f1"])
            for i in range(3):
                g.tensor_scalar(raw3[i], raw3[i], wabs[:, 2, i:i + 1], ROUND, ALU.mult, ALU.add).then_inc(s_tern, 1)
            for i in range(3):
                g.wait_ge(s_tern, i + 1)
                g.tensor_scalar(raw3[i], raw3[i], -ROUND, 1.0, ALU.add, ALU.min).then_inc(s_tern, 1)
            for i in range(3):
                g.wait_ge(s_tern, 3 + i + 1)
                if i == 2:
                    g.wait_ge(s_tern, 7)
                g.tensor_scalar(tern[i], raw3[i], -1.0, None, ALU.max).then_inc(s_tern, 1)
            chain(p_l3x, 1, a3)
            chain(p_l3f, 1)

        @block.scalar
        def _(act):
            act.wait_ge(s_const, 16 * 8)
            act.activation(gates[:, :], gates[:, :], ACT.Tanh).then_inc(s_gates, 1)

            with act.Fori(0, ITERS) as it:
                p = p_l0x
                keep_turned(act, p, it, 0)
                for j in range(LANES):
                    act.wait_ge(*p["self_v"].at(it, 0, j))
                    for m in range(KC):
                        last = act.activation(qT[j][:, m, :], bank_s[j][:, m * T:(m + 1) * T], ACT.Identity,
                                              bias=col("l0_sv", m))
                    last.then_inc(p["self_vT"].sem, 1)
                keep_turned(act, p, it, 1)
                attend_scalar(act, a0, p, it)
                keep_turned(act, p, it, 2)
                for j in range(LANES):
                    act.wait_ge(*p["hid"].at(it, 0, j))
                    for m in range(0, 4):
                        last = act.activation(OT[j][:, m, :], bank_s[j][:, m * T:(m + 1) * T], ACT.Relu,
                                              bias=col("lin1_b", m))
                    last.then_inc(p["hid_a"].sem, 1)
            with act.Fori(0, ITERS) as it:
                p = p_l0f
                for j in range(LANES):
                    act.wait_ge(*p["turned"].at(it, 0, j))
                    act.copy(cT[j][:, :, 1:T + 1], three(bank_t[j][:, 0:2 * T], 2)).then_inc(p["xT_ready"].sem, 1)
                for j in range(LANES):
                    act.wait_ge(*p["rk"].at(it, 0, j))
                    act.activation(V[j][:, 0:2, 0:T], three(bank_t[j][:, 0:2 * T], 2), ACT.Relu)\
                        .then_inc(p["k_relu"].sem, 1)
                    act.activation(y[j], bank_s[j][0:T, 0:C], ACT.Sigmoid).then_inc(p["sig"].sem, 1)
            with act.Fori(0, ITERS) as it:
                keep_turned(act, p_l1x, it, 0)
                attend_scalar(act, a1, p_l1x, it)
            p = p_rt
            for it in range(ITERS):
                for j in range(LANES):
                    act.wait_ge(*p["turned"].at(it, 0, j))
                    act.copy(rxT[j], three(bank_t[j][:, 0:2 * T], 2)).then_inc(p["xT_ready"].sem, 1)
                for j in range(LANES):
                    b = it * LANES + j
                    act.copy(xnT_all[:, :, b, :], three(bank_t[j][:, 0:2 * T], 2)).then_inc(p["xT_spread"].sem, 1)
                for j in range(LANES):
                    act.wait_ge(*p["lmax"].at(it, 0, j))
                    act.activation(score[:, it * LANES + j, :], bank_s[j][0:T, 0:E1], ACT.Exp,
                                   bias=rsc[:, 0, j:j + 1], accum_out=rsc[:, 1, j:j + 1]).then_inc(p["lexp"].sem, 1)
            act.wait_ge(s_topT, 1)
            act.copy(scoreT, bank[0][:, 0:T]).then_inc(s_scoreT, 1)
            for b in range(B):
                act.wait_ge(s_gather, b + 1)
                for k in range(KC):
                    last = act.copy(taken[:, k, :, b * CAP:(b + 1) * CAP],
                                    bank[b][:, k * CAP * E1:(k + 1) * CAP * E1].rearrange("p (c e) -> p e c", c=CAP))
                last.then_inc(s_taken, 1)
            with act.Fori(0, E1 // 2) as i:
                for s in range(2):
                    act.wait_ge(*p_ex["gu_out"].at(i, 0, s))
                    act.activation(hbuf[s], bank[3 * s][:, 0:4 * T], ACT.Gelu).then_inc(p_ex["e_gelu"].sem, 1)
                for s in range(2):
                    act.wait_ge(*p_ex["e_out"].at(i, 0, s))
                    act.copy(eo[:, i * 2 + s, :], bank[3 * s + 2][0:T, 0:C]).then_inc(p_ex["e_kept"].sem, 1)
                    act.wait_ge(*p_ex["e_kept"].at(i, 0, s))
                    act.dma_start(scratch[i * 2 + s].rearrange("b c f -> (b c) f"), eo[:, i * 2 + s, :])\
                        .then_inc(s_stored, 16)
            for b in range(B):
                act.wait_ge(*p_sh["gu_out"].at(b // 2, 0, b % 2))
                act.activation(hbuf[b % 2], bank[3 * (b % 2)][:, 0:4 * T], ACT.Gelu).then_inc(p_sh["e_gelu"].sem, 1)
            with act.Fori(0, ITERS) as it:
                keep_turned(act, p_l2x, it, 0)
                attend_scalar(act, a2, p_l2x, it)
            for l in range(2):
                p = p_f[l]
                with act.Fori(0, ITERS) as it:
                    keep_turned(act, p, it, 0)
                    attend_scalar(act, af[l], p, it)
                    keep_turned(act, p, it, 1)
                    for j in range(LANES if l else 0):
                        act.copy(h2w[j][:, it, :], bank_t[j][:, 0:2 * T]).then_inc(p["h_spread"].sem, 1)
                    act.wait_ge(*p["g_diff"].at(it))
                    act.activation(tiny[:, 1, :], tiny[:, 0, :], ACT.Exp).then_inc(p["g_exp"].sem, 1)
                    for j in range(LANES):
                        act.wait_ge(*p["cw_turned"].at(it, 0, j))
                        act.copy(E[j][0:E2, 0:T], bank_t[j][0:E2, 0:T]).then_inc(p["cwT_ready"].sem, 1)
                if l == 1:
                    with act.Fori(0, ITERS) as it:
                        for r in range(SEQ_ITEMS):
                            if r >= 2:
                                act.wait_ge(*p_m[1]["e_out"].at(it, r - 2))
                            for m in range(8):
                                if m % 4 == 0:
                                    act.wait_ge(*p_m[1]["gu_out"].at(it, 2 * r + m // 4))
                                last = act.activation(seq_hid(r % 2)[:, m * T:(m + 1) * T],
                                                      bank[r % 2 * 2 + m // 4][:, m % 4 * T:(m % 4 + 1) * T],
                                                      ACT.Gelu, bias=b1q[:, r % SEQ_SLOTS, m:m + 1])
                                if m % 4 == 3:
                                    last.then_inc(p_m[1]["e_gelu"].sem, 1)
                    continue
                act.wait_ge(s_rmm, 1)
                act.copy(count, bank[0][:, 0:T]).then_inc(s_route, 1)
                act.wait_ge(s_tid, 1)
                turns = act.value_load(tok_ids[0:1, MAX_TURNS * TOK_SLOTS:MAX_TURNS * TOK_SLOTS + 1], min_val=MIN_TURNS,
                                       max_val=MAX_TURNS)
                with act.Fori(0, turns) as it:
                    for r in range(TOK_SLOTS):
                        if r >= 2:
                            act.wait_ge(*p_m[0]["tok_y_out"].at(it, r - 2))
                        for m in range(8):
                            if m % 4 == 0:
                                act.wait_ge(*p_m[0]["tok_h_out"].at(it, 2 * r + m // 4))
                            last = act.activation(tok_hid[r % 2][:, m * P:(m + 1) * P],
                                                  bank[r % 2 * 2 + m // 4][:, m % 4 * P:(m % 4 + 1) * P],
                                                  ACT.Gelu, bias=b1q[:, r, m:m + 1])
                            if m % 4 == 3:
                                last.then_inc(p_m[0]["tok_gelu"].sem, 1)
            with act.Fori(0, ITERS) as it:
                keep_turned(act, p_l3x, it, 0)
                attend_scalar(act, a3, p_l3x, it)
            with act.Fori(0, ITERS) as it:
                p = p_l3f
                for h in range(2):
                    for j in range(LANES):
                        act.wait_ge(*p["g_u_out"].at(it, h, j))
                        if h == 1:
                            act.wait_ge(*p["h_part"].at(it, 0, j))
                        act.activation(ga[j], bank_s[j][0:T, :], ACT.Relu).then_inc(p["g_relu"].sem, 1)
                    for j in range(LANES):
                        act.wait_ge(*p["g_relu"].at(it, h, j))
                        act.activation(ga[j], ga[j], ACT.Square).then_inc(p["g_sq"].sem, 1)

        @block.tensor
        def _(pe):
            pe.wait_ge(s_const, 16 * 8)
            pe.wait_ge(s_wl0, 16 * 15)
            with pe.Fori(0, ITERS) as it:
                p = p_l0x
                turn(pe, p, it, 0, 0, xn)
                for j in range(LANES):
                    pe.wait_ge(*p["xT_ready"].at(it, 0, j))
                    for m in range(KC):
                        last = matmuls(pe, bank_s[j][:, m * T:(m + 1) * T],
                                       [(w_sv[:, c, m * P:(m + 1) * P], xT[j][:, c, :]) for c in range(KC)])
                    last.then_inc(p["self_v"].sem, 1)
                for j in range(LANES):
                    pe.wait_ge(*p["self_vT"].at(it, 0, j))
                    matmuls(pe, bank_s[j][0:T, 0:C], [(qT[j][:, c, :], w_so[:, c, :]) for c in range(KC)])\
                        .then_inc(p["proj_out"].sem, 1)
                turn(pe, p, it, 1, 1, xa)
                attend_tensor(pe, a0, p, it, 1, None, lambda j: cT[j], ctx_ready("l0"))
                project_out(pe, p, it, 1, w_o0, lambda j: p["o_T"].at(it, a0.tiles - 1, j))
                turn(pe, p, it, 2, 2, xn)
                for j in range(LANES):
                    pe.wait_ge(*p["xT_ready"].at(it, 2, j))
                    for m in range(8):
                        dst = (bank_s if m < 4 else bank_t)[j]
                        last = matmuls(pe, dst[:, m % 4 * T:(m % 4 + 1) * T],
                                       [(w_l1[:, c, m * P:(m + 1) * P], xT[j][:, c, :]) for c in range(KC)])
                    last.then_inc(p["hid"].sem, 1)
                pe.wait_ge(*p["hid_b"].at(it, 0, LANES - 1))
                project_out(pe, p, it, 2, w_l2, lambda j: p["hid_a"].at(it, 0, j))
            with pe.Fori(0, ITERS) as it:
                p = p_l0f
                turn(pe, p, it, 0, 0, xn)
                for j in range(LANES):
                    pe.wait_ge(*p["mixed"].at(it, 0, j))
                    mr, mk = qT[j], three(PT[j][:, 0:2 * T], 2)
                    matmuls(pe, bank_s[j][0:T, 0:C], [(mr[:, c, :], w_r[:, c, :]) for c in range(KC)])
                    for m in range(KC):
                        last = matmuls(pe, bank_t[j][:, m * T:(m + 1) * T],
                                       [(w_k[:, c, m * P:(m + 1) * P], mk[:, c, :]) for c in range(KC)])
                    last.then_inc(p["rk"].sem, 1)
                pe.wait_ge(*p["sig"].at(it, 0, LANES - 1))
                project_out(pe, p, it, 0, w_v, lambda j: p["k_sq"].at(it, 0, j))
            with pe.Fori(0, ITERS) as it:
                p = p_l1x
                turn(pe, p, it, 0, 0, xn)
                attend_tensor(pe, a1, p, it, 0, None, lambda j: cT[j], ctx_ready("l1"))
                project_out(pe, p, it, 0, w_o1, lambda j: p["o_T"].at(it, a1.tiles - 1, j))
            pe.wait_ge(s_wl1, 16 * 13)
            p = p_rt
            for it in range(ITERS):
                for j in range(LANES):
                    pe.wait_ge(*p["normed"].at(it, 0, j))
                    for c in range(KC):
                        last = pe.transpose(bank_t[j][:, c * T:(c + 1) * T],
                                            xn_all[:, it * LANES + j, c * P:(c + 1) * P], ident[0:T, 0:T])
                    last.then_inc(p["turned"].sem, 1)
                for j in range(LANES):
                    pe.wait_ge(*p["xT_ready"].at(it, 0, j))
                    matmuls(pe, bank_s[j][0:T, 0:E1], [(rxT[j][:, c, :], w_gate1[:, c, :]) for c in range(KC)])\
                        .then_inc(p["logits"].sem, 1)
                pe.wait_ge(*p["xT_spread"].at(it, 0, LANES - 1))
                pe.wait_ge(*p["lexp"].at(it, 0, LANES - 1))
            pe.wait_ge(*p["scored"].at(ITERS - 1, 0, LANES - 1))
            pe.transpose(bank[0][:, 0:T], score.rearrange("t b e -> t (b e)"), ident[0:T, 0:T]).then_inc(s_topT, 1)
            pe.wait_ge(s_topstep, 7)
            for c in range(CAP):
                last = pe.matmul(bank[4 + c // 4][0:T, c % 4 * P:(c % 4 + 1) * P],
                                 topf[:, c:c + 1].broadcast_to([P, T]), ident[:, :], start=True, stop=True)
            last.then_inc(s_idx, 1)
            for b in range(B):
                if b == 0:
                    pe.wait_ge(s_sel, 4)
                for k in range(KC):
                    last = pe.matmul(bank[b][:, k * CAP * E1:(k + 1) * CAP * E1], xn_all[:, b, k * P:(k + 1) * P],
                                     sel[:, :, b * E1:(b + 1) * E1], start=True, stop=True)
                last.then_inc(s_gather, 1)
            pe.wait_ge(s_sel, 5)
            for b in range(B):
                pe.wait_ge(s_taken, b + 1)
                for h in range(2):
                    g0 = b * E1 + h * HALF_E
                    last = pe.transpose(bank[b][0:T, h * T:(h + 1) * T],
                                        selw[:, g0:g0 + HALF_E, :].rearrange("t e c -> t (e c)"), ident[0:T, 0:T])
                last.then_inc(s_selT, 1)

            def gate_up(s, wg, wu, rhs, sig):
                for dst, w in ((bank[3 * s], wg), (bank[3 * s + 1], wu)):
                    for m in range(4):
                        last = matmuls(pe, dst[:, m * T:(m + 1) * T],
                                       [(w[:, c, m * P:(m + 1) * P], rhs(c)) for c in range(KC)])
                last.then_inc(sig.sem, 1)

            pe.wait_ge(s_selTk, B)
            with pe.Fori(0, E1 // 2) as i:
                for s in range(2):
                    pe.wait_ge(s_ew[s], i * 48 + 48)
                    wg, wu, wd = expert_slot(s)
                    gate_up(s, wg, wu, lambda c: taken[:, c, i * 2 + s, :], p_ex["gu_out"])
                for s in range(2):
                    wg, wu, wd = expert_slot(s)
                    pe.wait_ge(*p_ex["e_hid"].at(i, 0, s))
                    matmuls(pe, bank[3 * s + 2][0:T, 0:C],
                            [(hbuf[s][:, m * T:(m + 1) * T], wd[:, m, :]) for m in range(4)])\
                        .then_inc(p_ex["e_out"].sem, 1)
                pe.wait_ge(*p_ex["e_kept"].at(i, 0, 1))
            for i in range(B // 2):
                for s in range(2):
                    b = 2 * i + s
                    gate_up(s, w_sg, w_su, lambda c: xnT_all[:, c, b, :], p_sh["gu_out"])
                for s in range(2):
                    b = 2 * i + s
                    if b == 0:
                        pe.wait_ge(s_rows_in, 16 * E1)
                    pe.wait_ge(*p_sh["e_hid"].at(i, 0, s))
                    matmuls(pe, bank[3 * s + 2][0:T, 0:C],
                            [(hbuf[s][:, m * T:(m + 1) * T], w_sd[:, m, :]) for m in range(4)]
                            + [(selT[:, b, h, :], expert_rows[:, b, h, :]) for h in range(2)])\
                        .then_inc(p_sh["e_out"].sem, 1)
                pe.wait_ge(*p_sh["added"].at(i, 0, 1))
            with pe.Fori(0, ITERS) as it:
                p = p_l2x
                turn(pe, p, it, 0, 0, xn)
                attend_tensor(pe, a2, p, it, 0, None, lambda j: cT[j], ctx_ready("l2"))
                project_out(pe, p, it, 0, w_o2, lambda j: p["o_T"].at(it, a2.tiles - 1, j))
            for l in range(2):
                p = p_f[l]
                if l == 1:
                    pe.wait_ge(s_wf1, 80)
                with pe.Fori(0, ITERS) as it:
                    turn(pe, p, it, 0, 1 - l, xn)
                    attend_tensor(pe, af[l], p, it, 0, None, lambda j: xT[j], None)
                    project_out(pe, p, it, 0, w_f[l][3], lambda j: p["o_T"].at(it, af[l].tiles - 1, j))
                    turn(pe, p, it, 1, 2 - l, xn)
                    for j in range(LANES):
                        pe.wait_ge(*(p["xT_ready"].at(it, 1, j) if l == 0 else p["hmean_ready"].at(it, 0, j)))
                        lhs = [xT[j][:, c, :] if l == 0 else hmean[:, 1, j, c:c + 1].broadcast_to([P, T])
                               for c in range(KC)]
                        matmuls(pe, bank_s[j][0:T, 0:E2], [(lhs[c], w_f[l][4][:, c, :]) for c in range(KC)])\
                            .then_inc(p["g_out"].sem, 1)
                    for j in range(LANES):
                        pe.wait_ge(*p["g_cw"].at(it))
                        if l == 1:
                            pe.wait_ge(*p["h_spread"].at(it, 0, j))
                        pe.transpose(bank_t[j][0:E2, 0:T], gsm[:, 4, j, :], ident[0:T, 0:T]).then_inc(p["cw_turned"].sem, 1)
                    for j in range(LANES):
                        if j == 0:
                            pe.wait_ge(s_rows2, 32)
                        pe.wait_ge(*p["cwT_ready"].at(it, 0, j))
                        matmuls(pe, bank_s[j][0:T, 0:C], [(E[j][0:E2, 0:T], rows[0:E2, 12 + l, :])])\
                            .then_inc(p["b2_out"].sem, 1)
                pe.wait_ge(*end[f"f{l}"])

                if l == 1:
                    p = p_m[1]

                    def pair_hidden(it, r):
                        w1, _ = moe_slot(r % SEQ_SLOTS)
                        pe.wait_ge(s_qw[r % SEQ_SLOTS], it * (48 * SEQ_ITEMS // SEQ_SLOTS)
                                   + 48 * (r // SEQ_SLOTS + 1))
                        for half in range(2):
                            if r >= 2:
                                pe.wait_ge(*p["e_gelu"].at(it, 2 * (r - 2) + half))
                            for m in range(4 * half, 4 * half + 4):
                                last = matmuls(pe, bank[r % 2 * 2 + half][:, m % 4 * T:(m % 4 + 1) * T],
                                               [(w1[:, c, m * P:(m + 1) * P],
                                                 h2w[r // TOP2][:, bass.ds(it, 1), c * T:(c + 1) * T])
                                                for c in range(KC)])
                            last.then_inc(p["gu_out"].sem, 1)

                    def pair_outputs(it, r):
                        _, w2 = moe_slot(r % SEQ_SLOTS)
                        if r >= 2:
                            pe.wait_ge(*p["added"].at(it, r - 2))
                        pe.wait_ge(*p["e_gelu"].at(it, 2 * r + 1))
                        matmuls(pe, bank[4 + r % 2][0:T, 0:C],
                                [(seq_hid(r % 2)[:, m * T:(m + 1) * T], w2[:, m, :]) for m in range(8)])\
                            .then_inc(p["e_out"].sem, 1)

                    with pe.Fori(0, ITERS) as it:
                        pair_hidden(it, 0)
                        for r in range(SEQ_ITEMS):
                            if r + 1 < SEQ_ITEMS:
                                pair_hidden(it, r + 1)
                            pair_outputs(it, r)
                        pe.wait_ge(*p["added"].at(it, SEQ_ITEMS - 1))
                    continue

                p = p_m[0]
                picked = picks.rearrange("t g e -> t (g e)")
                pe.wait_ge(s_picks, ITERS * TOP2)
                pe.matmul(bank[0][:, 0:T], picked, one_col[0:T, 0:1].broadcast_to([T, T]), start=True,
                          stop=True).then_inc(s_rmm, 1)
                pe.wait_ge(s_route, 1)
                pe.wait_ge(s_rconst, 16 * 7)
                pe.matmul(bank[1][0:E2, 0:T], of_expert, count, start=True, stop=True).then_inc(s_rmm, 1)
                pe.wait_ge(s_route, 3)
                pe.matmul(bank[2][0:T, 0:P], before, picked, start=True, stop=False)
                pe.matmul(bank[2][0:T, 0:P], count, groups_before, start=False, stop=False)
                pe.matmul(bank[2][0:T, 0:P], used.broadcast_to([E2, T]), chunks_before, start=False,
                          stop=True).then_inc(s_rmm, 1)
                pe.matmul(bank[3][0:T, 0:E2], used.broadcast_to([E2, T]), chunks_upto, start=True,
                          stop=True).then_inc(s_rmm, 1)

                def turn_rows(it, r):
                    pe.wait_ge(s_xr[r % 2], it * (8 * TOK_SLOTS) + (r // 2 + 1) * 16)
                    for c in range(KC):
                        last = pe.transpose(bank[6 + r % 2][:, c * P:(c + 1) * P], tok_x[r % 2][:, c * P:(c + 1) * P],
                                            ident[:, :])
                    last.then_inc(p["tok_turned"].sem, 1)

                def chunk_hidden(it, r):
                    w1, _ = moe_slot(r)
                    pe.wait_ge(s_tw[r], it * 48 + 48)
                    pe.wait_ge(*p["tok_xT"].at(it, r))
                    for half in range(2):
                        if r >= 2:
                            pe.wait_ge(*p["tok_gelu"].at(it, 2 * (r - 2) + half))
                        for m in range(4 * half, 4 * half + 4):
                            last = matmuls(pe, bank[r % 2 * 2 + half][:, m % 4 * P:(m % 4 + 1) * P],
                                           [(w1[:, c, m * P:(m + 1) * P], tok_xT[r % 2][:, c, :])
                                            for c in range(KC)])
                        last.then_inc(p["tok_h_out"].sem, 1)

                def chunk_outputs(it, r):
                    _, w2 = moe_slot(r)
                    if r >= 2:
                        pe.wait_ge(*p["tok_y_kept"].at(it, r - 2))
                    pe.wait_ge(*p["tok_gelu"].at(it, 2 * r + 1))
                    matmuls(pe, bank[4 + r % 2][:, 0:C],
                            [(tok_hid[r % 2][:, m * P:(m + 1) * P], w2[:, m, :]) for m in range(8)])\
                        .then_inc(p["tok_y_out"].sem, 1)

                pe.wait_ge(s_abs, 3)
                pe.wait_ge(s_one, 1)
                pe.matmul(bank[5][:, 0:3], one_col[:, 0:1].broadcast_to([P, P]), wabs[:, 0, :], start=True,
                          stop=True).then_inc(s_wsum, 1)
                pe.wait_ge(s_wmean, 1)
                pe.wait_ge(s_tid, 1)
                turns = pe.value_load(tok_ids[0:1, MAX_TURNS * TOK_SLOTS:MAX_TURNS * TOK_SLOTS + 1], min_val=MIN_TURNS,
                                      max_val=MAX_TURNS)
                with pe.Fori(0, turns) as it:
                    turn_rows(it, 0)
                    turn_rows(it, 1)
                    chunk_hidden(it, 0)
                    for r in range(TOK_SLOTS):
                        if r + 1 < TOK_SLOTS:
                            chunk_hidden(it, r + 1)
                        if r + 2 < TOK_SLOTS:
                            turn_rows(it, r + 2)
                        chunk_outputs(it, r)
                    pe.wait_ge(*p["tok_y_kept"].at(it, TOK_SLOTS - 1))
            pe.wait_ge(s_wl3, 64)
            with pe.Fori(0, ITERS) as it:
                p = p_l3x
                turn(pe, p, it, 0, 0, xn)
                attend_tensor(pe, a3, p, it, 0, None, lambda j: cT[j], ctx_ready("l3"))
                project_out(pe, p, it, 0, w_o3, lambda j: p["o_T"].at(it, a3.tiles - 1, j))
            pe.wait_ge(s_tern, 9)
            with pe.Fori(0, ITERS) as it:
                p = p_l3f
                for j in range(LANES):
                    pe.wait_ge(*p["q_ready"].at(it, 0, j))
                    for c in range(KC):
                        last = pe.transpose(bank_bf[4 + j][:, c * T:(c + 1) * T],
                                            qx[j][:, c * P:(c + 1) * P], ident_bf[0:T, 0:T])
                    last.then_inc(p["turned"].sem, 1)
                for h in range(2):
                    for j in range(LANES):
                        if h == 0:
                            pe.wait_ge(*p["xq_ready"].at(it, 0, j))
                        else:
                            pe.wait_ge(*p["h_part"].at(it, 0, j))
                        for dst, w in ((bank_s[j], w_tg), (bank_t[j], w_tu)):
                            last = matmuls(pe, dst[0:T, :], [(xqT[j][:, c, :], w[:, c, h * 512:(h + 1) * 512])
                                                             for c in range(KC)])
                        last.then_inc(p["g_u_out"].sem, 1)
                for j in range(LANES):
                    pe.wait_ge(*p["q_ready"].at(it, 1, j))
                    for c in range(8):
                        last = pe.transpose(bank_bf[j][:, c * T:(c + 1) * T], hq[j][:, c * P:(c + 1) * P],
                                            ident_bf[0:T, 0:T])
                    last.then_inc(p["q2_turned"].sem, 1)
                for j in range(LANES):
                    pe.wait_ge(*p["q2T_ready"].at(it, 0, j))
                    matmuls(pe, bank_t[j][0:T, 0:C], [(hqT[j][:, c, :], w_td[:, c, :]) for c in range(8)])\
                        .then_inc(p["proj_out"].sem, 1)

        @block.vector
        def _(v):
            v.wait_ge(s_const, 16 * 8)
            v.tensor_copy(ident_bf[:, :], ident[:, :]).then_inc(s_omu, 1)
            v.tensor_scalar(omu[:, :], col("mu_r", 0, 4), -1.0, 1.0, ALU.mult, ALU.add).then_inc(s_omu, 1)
            v.wait_ge(s_x, 16)
            v.wait_ge(s_gates, 1)
            with v.Fori(0, ITERS) as it:
                p = p_l0x
                norm_stats(v, p, it, 0, lambda j: x_at(it, j))
                norm_apply(v, p, it, 0, lambda j: x_at(it, j), lambda j: xn[j])
                add_row(v, p, it, 0, row("sa_b"))
                for j in range(LANES):
                    v.wait_ge(*p["part"].at(it, 0, j))
                    v.tensor_tensor(y[j], y[j], xn[j], ALU.add).then_inc(p["summed"].sem, 1)
                norm_stats(v, p, it, 1, lambda j: y[j], lambda j: p["summed"].at(it, 0, j))
                norm_apply_affine(v, p, it, 1, 0, lambda j: y[j], lambda j: xa[j], row("ln1_g"), row("ln1_b"))
                attend_vector(v, a0, p, it)
                add_row(v, p, it, 1, row("l0_bo"))
                for j in range(LANES):
                    v.wait_ge(*p["part"].at(it, 1, j))
                    v.tensor_tensor(y[j], y[j], xa[j], ALU.add).then_inc(p["summed"].sem, 1)
                norm_stats(v, p, it, 2, lambda j: y[j], lambda j: p["summed"].at(it, 1, j))
                norm_apply_affine(v, p, it, 2, 1, lambda j: y[j], lambda j: xn[j], row("ln2_g"), row("ln2_b"))
                for j in range(LANES):
                    v.wait_ge(*p["hid"].at(it, 0, j))
                    for m in range(4, 8):
                        last = v.tensor_scalar(OT[j][:, m, :], bank_t[j][:, (m - 4) * T:(m - 3) * T],
                                               col("lin1_b", m), 0.0, ALU.add, ALU.max)
                    last.then_inc(p["hid_b"].sem, 1)
                add_row(v, p, it, 2, row("lin2_b"))
                for j in range(LANES):
                    v.wait_ge(*p["part"].at(it, 2, j))
                    v.tensor_tensor(y[j], y[j], xn[j], ALU.add).then_inc(p["summed"].sem, 1)
                norm_stats(v, p, it, 3, lambda j: y[j], lambda j: p["summed"].at(it, 2, j))
                norm_apply_affine(v, p, it, 3, 2, lambda j: y[j], lambda j: xa[j], row("ln3_g"), row("ln3_b"))
                add_gated(v, p, it, lambda j: xa[j], 0, lambda j: p["normed"].at(it, 3, j))
            v.wait_ge(*end["l0x"])
            for j in range(LANES):
                v.memset(cT[j][:, :, 0:1], 0.0).then_inc(s_shift0, 1)
            v.wait_ge(s_shift0, LANES)
            v.wait_ge(s_omu, 2)
            with v.Fori(0, ITERS) as it:
                p = p_l0f
                norm_stats(v, p, it, 0, lambda j: x_at(it, j))
                norm_apply(v, p, it, 0, lambda j: x_at(it, j), lambda j: xn[j])
                for j in range(LANES):
                    v.wait_ge(*p["xT_ready"].at(it, 0, j))
                    for i in range(4):
                        last = v.tensor_scalar(E[j][:, i * T:(i + 1) * T], cT[j][:, i % 2, 0:T], omu[:, i:i + 1],
                                               None, ALU.mult)
                    last.then_inc(p["mixed_r"].sem, 1)
                for j in range(LANES):
                    v.wait_ge(*p["mixed_r"].at(it, 0, j))
                    for i in range(4):
                        dst = qT[j][:, i, :] if i < 2 else PT[j][:, (i - 2) * T:(i - 1) * T]
                        last = v.scalar_tensor_tensor(dst, cT[j][:, i % 2, 1:T + 1], col("mu_r", i),
                                                      E[j][:, i * T:(i + 1) * T], ALU.mult, ALU.add)
                    last.then_inc(p["mixed"].sem, 1)
                for j in range(LANES):
                    v.wait_ge(*p["k_relu"].at(it, 0, j))
                    v.tensor_tensor(OT[j][:, 0:2, :], V[j][:, 0:2, 0:T], V[j][:, 0:2, 0:T], ALU.mult)\
                        .then_inc(p["k_sq"].sem, 1)
                for j in range(LANES):
                    v.wait_ge(*p["proj_out"].at(it, 0, j))
                    v.wait_ge(*p["sig"].at(it, 0, j))
                    v.tensor_tensor(xa[j], y[j], bank_s[j][0:T, 0:C], ALU.mult).then_inc(p["gated"].sem, 1)
                add_gated(v, p, it, lambda j: xa[j], 4, lambda j: p["gated"].at(it, 0, j))
            v.wait_ge(*end["l0f"])
            v.wait_ge(s_mask1, 16)
            v.tensor_scalar(maskb[0], maskb[0].bitcast(I32), 0.0, BIG, ALU.is_equal, ALU.mult).then_inc(s_mask1b, 1)
            v.wait_ge(s_mask1b, 1)
            with v.Fori(0, ITERS) as it:
                p = p_l1x
                norm_stats(v, p, it, 0, lambda j: x_at(it, j))
                norm_apply(v, p, it, 0, lambda j: x_at(it, j), lambda j: xn[j])
                attend_vector(v, a1, p, it)
                add_row(v, p, it, 0, row("l1_bo"))
                add_gated(v, p, it, lambda j: y[j], 1, lambda j: p["part"].at(it, 0, j))
            p = p_rt
            v.wait_ge(*end["l1x"])
            for it in range(ITERS):
                norm_stats(v, p, it, 0, lambda j: x_at(it, j))
                norm_apply(v, p, it, 0, lambda j: x_at(it, j), lambda j: xn_all[:, it * LANES + j, :])
                for j in range(LANES):
                    v.wait_ge(*p["logits"].at(it, 0, j))
                    v.tensor_reduce(rsc[:, 0, j:j + 1], bank_s[j][0:T, 0:E1], AX_X, ALU.max, negate=True)\
                        .then_inc(p["lmax"].sem, 1)
                for j in range(LANES):
                    v.wait_ge(*p["lexp"].at(it, 0, j))
                    v.reciprocal(rsc[:, 2, j:j + 1], rsc[:, 1, j:j + 1]).then_inc(p["linv"].sem, 1)
                for j in range(LANES):
                    v.wait_ge(*p["linv"].at(it, 0, j))
                    v.tensor_scalar(score[:, it * LANES + j, :], score[:, it * LANES + j, :], rsc[:, 2, j:j + 1],
                                    None, ALU.mult).then_inc(p["scored"].sem, 1)
            v.wait_ge(s_scoreT, 1)
            v.max(top16[:, 0:8], scoreT).then_inc(s_topstep, 1)
            v.wait_ge(s_topstep, 1)
            v.match_replace(scoreT2, top16[:, 0:8], scoreT, -1.0).then_inc(s_topstep, 1)
            v.max_index(topi16[:, 0:8], top16[:, 0:8], scoreT).then_inc(s_topstep, 1)
            v.wait_ge(s_topstep, 2)
            v.max(top16[:, 8:16], scoreT2).then_inc(s_topstep, 1)
            v.wait_ge(s_topstep, 4)
            v.max_index(topi16[:, 8:16], top16[:, 8:16], scoreT2).then_inc(s_topstep, 1)
            v.tensor_copy(topf[:, 0:8], topi16[:, 0:8]).then_inc(s_topstep, 1)
            v.wait_ge(s_topstep, 6)
            v.tensor_copy(topf[:, 8:CAP], topi16[:, 8:CAP]).then_inc(s_topstep, 1)
            v.wait_ge(s_idx, 1)
            for k in range(4):
                n = min(4, CAP - 4 * k)
                v.tensor_scalar(sel[:, 4 * k:4 * k + n, :], three(bank[4 + k][0:T, 0:n * P], n), iota[0:T, 0:1],
                                None, ALU.is_equal).then_inc(s_sel, 1)
            v.wait_ge(s_sel, 4)
            v.tensor_tensor(selw.rearrange("t g c -> t c g"), sel, score.rearrange("t b e -> t (b e)").unsqueeze(1).broadcast_to([T, CAP, P]),
                            ALU.mult).then_inc(s_sel, 1)
            for b in range(B):
                v.wait_ge(s_selT, b + 1)
                v.tensor_copy(selT[:, b, :, :], three(bank[b][0:T, 0:2 * T], 2)).then_inc(s_selTk, 1)
            with v.Fori(0, E1 // 2) as i:
                for s in range(2):
                    v.wait_ge(*p_ex["e_gelu"].at(i, 0, s))
                    v.tensor_tensor(hbuf[s], hbuf[s], bank[3 * s + 1][:, 0:4 * T], ALU.mult).then_inc(p_ex["e_hid"].sem, 1)
            for i in range(B // 2):
                for s in range(2):
                    v.wait_ge(*p_sh["e_gelu"].at(i, 0, s))
                    v.tensor_tensor(hbuf[s], hbuf[s], bank[3 * s + 1][:, 0:4 * T], ALU.mult).then_inc(p_sh["e_hid"].sem, 1)
                for s in range(2):
                    b = 2 * i + s
                    v.wait_ge(*p_sh["e_out"].at(i, 0, s))
                    v.scalar_tensor_tensor(X[:, b, :], bank[3 * s + 2][0:T, 0:C], gates[0:T, 5:6], X[:, b, :],
                                           ALU.mult, ALU.add).then_inc(p_sh["added"].sem, 1)
            v.wait_ge(*end["sh"])
            with v.Fori(0, ITERS) as it:
                p = p_l2x
                norm_stats(v, p, it, 0, lambda j: x_at(it, j))
                norm_apply(v, p, it, 0, lambda j: x_at(it, j), lambda j: xn[j])
                for j in range(LANES):
                    v.wait_ge(s_maskl[j], it * 16 + 16)
                    v.tensor_scalar(maskb[j], maskb[j].bitcast(I32), 0.0, BIG, ALU.is_equal, ALU.mult)\
                        .then_inc(p["mask_ready"].sem, 1)
                v.wait_ge(*p["mask_ready"].at(it, 0, LANES - 1))
                attend_vector(v, a2, p, it)
                add_row(v, p, it, 0, row("l2_bo"))
                add_gated(v, p, it, lambda j: y[j], 2, lambda j: p["part"].at(it, 0, j))
            v.wait_ge(*end["l2x"])
            for l in range(2):
                p = p_f[l]
                if l == 1:
                    v.wait_ge(*end["m0"])
                v.wait_ge(s_rows2, 16 if l == 0 else 32)
                with v.Fori(0, ITERS) as it:
                    acc = lambda j: accs[j][:, it, :]
                    n = 0
                    if l == 0:
                        norm_stats(v, p, it, 0, lambda j: x_at(it, j))
                        norm_apply(v, p, it, 0, lambda j: x_at(it, j), acc)
                        n = 1
                    norm_stats(v, p, it, n, acc, (lambda j: p["normed"].at(it, 0, j)) if l == 0 else None)
                    norm_apply_affine(v, p, it, n, 0, acc, lambda j: xn[j], row2(l, "ln1_w"), row2(l, "ln1_b"))
                    attend_vector(v, af[l], p, it)
                    add_row(v, p, it, 0, row2(l, "bo"))
                    for j in range(LANES):
                        v.wait_ge(*p["part"].at(it, 0, j))
                        v.tensor_tensor(acc(j), acc(j), y[j], ALU.add).then_inc(p["summed"].sem, 1)
                    norm_stats(v, p, it, n + 1, acc, lambda j: p["summed"].at(it, 0, j))
                    norm_apply_affine(v, p, it, n + 1, 1, acc, lambda j: xn[j], row2(l, "ln2_w"), row2(l, "ln2_b"))
                    if l == 1:
                        for j in range(LANES):
                            v.wait_ge(*p["xT_ready"].at(it, 1, j))
                            v.tensor_reduce(hmean[:, 0, j, :], xT[j], AX_X, ALU.add).then_inc(p["hmean_sum"].sem, 1)
                        for j in range(LANES):
                            v.wait_ge(*p["hmean_sum"].at(it, 0, j))
                            v.tensor_scalar(hmean[:, 1, j, :], hmean[:, 0, j, :], 1.0 / T, None, ALU.mult)\
                                .then_inc(p["hmean_ready"].sem, 1)
                    for j in range(LANES):
                        v.wait_ge(*p["g_out"].at(it, 0, j))
                        v.tensor_tensor(gsm[:, 0, j, :], bank_s[j][0:T, 0:E2], gate_b[:, l, :], ALU.add)\
                            .then_inc(p["g_val"].sem, 1)
                    for j in range(LANES):
                        wait_first(v, *p["g_val"].at(it, 0, j))
                        v.max(gsm[:, 1, j, :], gsm[:, 0, j, :]).then_inc(p["g_maxed"].sem, 1)
                    for j in range(LANES):
                        wait_first(v, *p["g_maxed"].at(it, 0, j))
                        last = v.max_index(gix[:, j, :], gsm[:, 1, j, :], gsm[:, 0, j, :])
                    last.then_inc(p["g_top"].sem, 1)
                    v.tensor_tensor(tiny[:, 0, :], gsm[:, 1, :, 1], gsm[:, 1, :, 0], ALU.subtract)\
                        .then_inc(p["g_diff"].sem, 1)
                    v.wait_ge(*p["g_top"].at(it))
                    v.tensor_copy(gsm[:, 5, :, :], gix[:, :, :]).then_inc(p["g_topf"].sem, 1)
                    v.wait_ge(*p["g_exp"].at(it))
                    v.tensor_scalar(tiny[:, 2, :], tiny[:, 1, :], 1.0, None, ALU.add).then_inc(p["g_sum"].sem, 1)
                    v.wait_ge(*p["g_sum"].at(it))
                    v.reciprocal(tiny[:, 3, :], tiny[:, 2, :]).then_inc(p["g_w1"].sem, 1)
                    v.wait_ge(*p["g_w1"].at(it))
                    v.tensor_tensor(tiny[:, 4, :], tiny[:, 3, :], tiny[:, 1, :], ALU.mult).then_inc(p["g_w2"].sem, 1)
                    v.wait_ge(*p["g_w2"].at(it))
                    v.wait_ge(*p["g_topf"].at(it))
                    for j in range(LANES):
                        for k in range(2):
                            last = v.tensor_scalar(gsm[:, 2 + k, j, :], iota8[:, :], gsm[:, 5, j, k:k + 1],
                                                   tiny[:, 3 + k, j:j + 1], ALU.is_equal, ALU.mult)
                        last.then_inc(p["g_half"].sem, 1)
                    v.wait_ge(*p["g_half"].at(it, 0, LANES - 1))
                    v.tensor_tensor(gsm[:, 4, :, :], gsm[:, 2, :, :], gsm[:, 3, :, :], ALU.add).then_inc(p["g_cw"].sem, 1)
                    v.wait_ge(*p["g_cw"].at(it))
                    v.tensor_copy(cw[:, bass.ds(it * LANES, LANES), :],
                                  tiny[:, 3:3 + TOP2, :].rearrange("t k j -> t j k"))\
                        .then_inc(p["cw_spread"].sem, LANES)
                    if l == 0:
                        for k in range(TOP2):
                            v.tensor_tensor(picks_of[:, bass.ds(it * LANES, LANES), k, :],
                                            iota8[:, :].unsqueeze(1).broadcast_to([T, LANES, E2]),
                                            gsm[:, 5, :, k:k + 1].broadcast_to([T, LANES, E2]),
                                            ALU.is_equal).then_inc(s_picks, 1)
                    else:
                        v.tensor_copy(ids[:, bass.ds(it * LANES, LANES), :], gix[:, :, 0:TOP2])\
                            .then_inc(p["ids_ready"].sem, 1)
                    for j in range(LANES):
                        v.wait_ge(*p["b2_out"].at(it, 0, j))
                        if l == 0:
                            v.wait_ge(*p["h_kept"].at(it, 0, j))
                        v.tensor_tensor(acc(j), acc(j), bank_s[j][0:T, 0:C], ALU.add).then_inc(p["acc_ready"].sem, 1)
                v.wait_ge(*p["cw_spread"].at(ITERS - 1, 0, LANES - 1))
                v.wait_ge(*end[f"f{l}"])
                if l == 1:
                    with v.Fori(0, ITERS) as it:
                        for r in range(SEQ_ITEMS):
                            j, k = r // TOP2, r % TOP2
                            v.wait_ge(*p_m[1]["e_out"].at(it, r))
                            if k:
                                v.wait_ge(*p_m[1]["added"].at(it, r - 1))
                            dst = accs[j][:, it, :]
                            v.scalar_tensor_tensor(dst, bank[4 + r % 2][0:T, 0:C],
                                                   cw[:, bass.ds(it * LANES + j, 1), k], dst, ALU.mult, ALU.add)\
                                .then_inc(p_m[1]["added"].sem, 1)
                    v.wait_ge(*end["m1"])
                    continue
                v.wait_ge(s_rmm, 2)
                v.tensor_scalar(fill, whole, bank[1][0:E2, 0:1], None, ALU.is_lt).then_inc(s_route, 1)
                v.wait_ge(s_route, 2)
                v.tensor_reduce(used, fill, AX_X, ALU.add).then_inc(s_route, 1)
                v.wait_ge(s_rmm, 4)
                n = MAX_TURNS * TOK_SLOTS
                v.tensor_tensor(held[:, 0:n, :], bank[3][0:1, 0:E2].unsqueeze(1).broadcast_to([1, n, E2]),
                                steps[:, 0:n].unsqueeze(2).broadcast_to([1, n, E2]), ALU.is_le).then_inc(s_route, 1)
                v.tensor_scalar(held[:, n:n + 1, 0:MAX_TURNS].rearrange("o c e -> o (c e)"), steps[:, n:n + MAX_TURNS],
                                bank[3][0:1, E2 - 1:E2], None, ALU.is_lt).then_inc(s_route, 1)
                v.tensor_tensor(place, bank[2][0:T, 0:P].rearrange("t (g e) -> t g e", e=E2), picks, ALU.mult)\
                    .then_inc(s_route, 1)
                v.wait_ge(s_route, 5)
                v.tensor_reduce(idf[:, 0:n], held[:, 0:n, :], AX_X, ALU.add)
                v.tensor_reduce(idf[:, n:n + 1], held[:, n, 0:MAX_TURNS], AX_X, ALU.add).then_inc(s_rid, 1)
                v.wait_ge(s_route, 6)
                v.tensor_reduce(placef, place, AX_X, ALU.add).then_inc(s_route, 1)
                v.wait_ge(s_rid, 1)
                v.tensor_scalar(tok_ids[:, :], idf[:, 0:n + 1], float(E2 - 1), None, ALU.min).then_inc(s_tid, 1)
                v.wait_ge(s_route, 7)
                v.tensor_copy(tok_slot[:, :], placef).then_inc(s_route, 1)
                v.wait_ge(s_tid, 1)
                v.wait_ge(s_raw3, 48)
                for i in range(3):
                    v.tensor_reduce(wabs[:, 0, i:i + 1], raw3[i], AX_X, ALU.add, apply_absolute_value=True)\
                        .then_inc(s_abs, 1)
                v.wait_ge(s_wsum, 1)
                v.tensor_scalar(wabs[:, 1, :], bank[5][:, 0:3], 1.0 / (C * FF), EPS, ALU.mult, ALU.max).then_inc(s_wmean, 1)
                v.wait_ge(s_wmean, 1)
                v.reciprocal(wabs[:, 2, :], wabs[:, 1, :]).then_inc(s_wmean, 1)
                turns = v.value_load(tok_ids[0:1, n:n + 1], min_val=MIN_TURNS, max_val=MAX_TURNS)
                with v.Fori(0, turns) as it:
                    p = p_m[0]

                    def keep_rows(r):
                        v.wait_ge(*p["tok_turned"].at(it, r))
                        if r >= 2:
                            v.wait_ge(*p["tok_h_out"].at(it, 2 * (r - 2) + 1))
                        v.tensor_copy(tok_xT[r % 2], three(bank[6 + r % 2][:, 0:C], 2)).then_inc(p["tok_xT"].sem, 1)

                    keep_rows(0)
                    keep_rows(1)
                    for r in range(TOK_SLOTS):
                        if r + 2 < TOK_SLOTS:
                            keep_rows(r + 2)
                        v.wait_ge(*p["tok_y_out"].at(it, r))
                        if r >= 2:
                            v.wait_ge(s_yst[r % 2], it * (8 * TOK_SLOTS) + r // 2 * 16)
                        v.tensor_copy(tok_y[r], bank[4 + r % 2][:, 0:C]).then_inc(p["tok_y_kept"].sem, 1)
                v.wait_ge(s_yg, 16 * PAIRS)
                for k in range(TOP2):
                    for j in range(LANES):
                        for i in range(ITERS):
                            if k:
                                v.wait_ge(s_tokadd, j * ITERS + i + 1)
                            b, dst = i * LANES + j, accs[j][:, i, :]
                            v.scalar_tensor_tensor(dst, tok_got[j][:, i, k, :], cw[:, b, k:k + 1], dst,
                                                   ALU.mult, ALU.add).then_inc(s_tokadd, 1)
            for b in range(B):
                dst = X[:, b, :]
                v.scalar_tensor_tensor(dst, accs[b % LANES][:, b // LANES, :], gates[0:T, 6:7], dst,
                                       ALU.mult, ALU.add).then_inc(s_gadd, 1)
            v.wait_ge(s_gadd, B)
            with v.Fori(0, ITERS) as it:
                p = p_l3x
                norm_stats(v, p, it, 0, lambda j: x_at(it, j))
                norm_apply(v, p, it, 0, lambda j: x_at(it, j), lambda j: xn[j])
                attend_vector(v, a3, p, it)
                add_gated(v, p, it, lambda j: bank_s[j][0:T, 0:C], 3, lambda j: p["proj_out"].at(it, 0, j))
            v.wait_ge(*end["l3x"])
            with v.Fori(0, ITERS) as it:
                p = p_l3f
                norm_stats(v, p, it, 0, lambda j: x_at(it, j))
                norm_apply(v, p, it, 0, lambda j: x_at(it, j), lambda j: xn[j])
                for j in range(LANES):
                    v.wait_ge(*p["normed"].at(it, 0, j))
                    v.tensor_reduce(tiny[:, 0, j:j + 1], xn[j], AX_X, ALU.max, apply_absolute_value=True)\
                        .then_inc(p["amax_ready"].sem, 1)
                v.wait_ge(*p["amax_ready"].at(it, 0, LANES - 1))
                v.tensor_scalar(tiny[:, 1, :], tiny[:, 0, :], EPS, None, ALU.max).then_inc(p["tiny_done"].sem, 1)
                v.wait_ge(*p["tiny_done"].at(it, 0))
                v.reciprocal(tiny[:, 2, :], tiny[:, 1, :]).then_inc(p["tiny_done"].sem, 1)
                v.tensor_scalar(tiny[:, 4, :], tiny[:, 1, :], 1.0 / 127.0, wabs[0:T, 1, 0:1], ALU.mult, ALU.mult)\
                    .then_inc(p["tiny_done"].sem, 1)
                v.tensor_scalar(tiny[:, 5, :], tiny[:, 1, :], 1.0 / 127.0, wabs[0:T, 1, 1:2], ALU.mult, ALU.mult)\
                    .then_inc(p["tiny_done"].sem, 1)
                v.wait_ge(*p["tiny_done"].at(it, 1))
                v.tensor_scalar(tiny[:, 3, :], tiny[:, 2, :], 127.0, None, ALU.mult).then_inc(p["tiny_done"].sem, 1)
                v.wait_ge(*p["tiny_done"].at(it, 3))
                v.tensor_tensor(tiny[:, 6, :], tiny[:, 4, :], tiny[:, 4, :], ALU.mult).then_inc(p["tiny_done"].sem, 1)
                v.wait_ge(*p["tiny_done"].at(it, 5))
                v.tensor_tensor(tiny[:, 7, :], tiny[:, 6, :], tiny[:, 5, :], ALU.mult).then_inc(p["tiny_done"].sem, 1)
                for j in range(LANES):
                    v.tensor_scalar(y[j], xn[j], tiny[:, 3, j:j + 1], ROUND, ALU.mult, ALU.add).then_inc(p["rounded"].sem, 1)
                for j in range(LANES):
                    v.wait_ge(*p["rounded"].at(it, 0, j))
                    v.tensor_scalar(qx[j], y[j], ROUND, 127.0, ALU.subtract, ALU.min).then_inc(p["q_ready"].sem, 1)
                for j in range(LANES):
                    v.wait_ge(*p["turned"].at(it, 0, j))
                    v.tensor_scalar(xqT[j], three(bank_bf[4 + j][:, 0:2 * T], 2), -128.0, None, ALU.max)\
                        .then_inc(p["xq_ready"].sem, 1)
                for h in range(2):
                    for j in range(LANES):
                        v.wait_ge(*p["g_sq"].at(it, h, j))
                        v.tensor_tensor(wide[j][0:T, h * 512:(h + 1) * 512], ga[j], bank_t[j][0:T, :], ALU.mult)\
                            .then_inc(p["h_part"].sem, 1)
                for j in range(LANES):
                    v.wait_ge(*p["h_part"].at(it, 1, j))
                    v.tensor_reduce(tiny[:, 8, j:j + 1], wide[j][0:T, :], AX_X, ALU.max, apply_absolute_value=True)\
                        .then_inc(p["amax_ready"].sem, 1)
                v.wait_ge(*p["amax_ready"].at(it, 1, LANES - 1))
                v.tensor_tensor(tiny[:, 9, :], tiny[:, 8, :], tiny[:, 7, :], ALU.mult).then_inc(p["tiny_done"].sem, 1)
                v.wait_ge(*p["tiny_done"].at(it, 7))
                v.tensor_scalar(tiny[:, 10, :], tiny[:, 9, :], EPS, None, ALU.max).then_inc(p["tiny_done"].sem, 1)
                v.wait_ge(*p["tiny_done"].at(it, 8))
                v.reciprocal(tiny[:, 11, :], tiny[:, 10, :]).then_inc(p["tiny_done"].sem, 1)
                v.tensor_scalar(tiny[:, 13, :], tiny[:, 10, :], 1.0 / 127.0, wabs[0:T, 1, 2:3], ALU.mult, ALU.mult)\
                    .then_inc(p["tiny_done"].sem, 1)
                v.wait_ge(*p["tiny_done"].at(it, 9))
                v.scalar_tensor_tensor(tiny[:, 12, :], tiny[:, 11, :], 127.0, tiny[:, 7, :], ALU.mult, ALU.mult)\
                    .then_inc(p["tiny_done"].sem, 1)
                v.wait_ge(*p["tiny_done"].at(it, 11))
                for j in range(LANES):
                    v.tensor_scalar(wide[j][0:T, :], wide[j][0:T, :], tiny[:, 12, j:j + 1], ROUND, ALU.mult, ALU.add)\
                        .then_inc(p["rounded"].sem, 1)
                for j in range(LANES):
                    v.wait_ge(*p["rounded"].at(it, 1, j))
                    v.tensor_scalar(hq[j], wide[j][0:T, :], ROUND, 127.0, ALU.subtract, ALU.min)\
                        .then_inc(p["q_ready"].sem, 1)
                for j in range(LANES):
                    v.wait_ge(*p["q2_turned"].at(it, 0, j))
                    v.tensor_scalar(hqT[j], three(bank_bf[j][:, 0:8 * T], 8), -128.0, None, ALU.max)\
                        .then_inc(p["q2T_ready"].sem, 1)
                for j in range(LANES):
                    v.wait_ge(*p["proj_out"].at(it, 0, j))
                    v.tensor_scalar(y[j], bank_t[j][0:T, 0:C], tiny[:, 13, j:j + 1], gates[0:T, 7:8], ALU.mult,
                                    ALU.mult).then_inc(p["out_scaled"].sem, 1)
                for j in range(LANES):
                    v.wait_ge(*p["out_scaled"].at(it, 0, j))
                    v.tensor_tensor(x_at(it, j), x_at(it, j), y[j], ALU.add).then_inc(p["x_added"].sem, 1)


def _lay_out(i):
    f = lambda n: np.asarray(i[n])
    tr = lambda a: np.ascontiguousarray(np.swapaxes(a, -1, -2))
    columns = lambda v: v.reshape(-1, P).T

    a = {"x": f("x"), "ctxT": np.ascontiguousarray(f("ctx_1024").transpose(2, 0, 1)),
         "mask1": f("mask_1xSxS2_ik0"), "mask2": f("mask_BxSxS2_ik1")}
    a["identity"] = np.eye(P, dtype=np.float32)
    a["iota"] = np.arange(P, dtype=np.float32).reshape(P, 1)
    a["iota8"] = np.arange(E2, dtype=np.float32)
    n = np.arange(T)
    a["before"] = (n[:, None] < n[None, :]).astype(np.float32)
    a["steps"] = np.concatenate([np.arange(MAX_TURNS * TOK_SLOTS), np.arange(MAX_TURNS) * TOK_SLOTS])\
        .astype(np.float32)[None]
    group, expert, e8 = np.arange(P) // E2, np.arange(P) % E2, np.arange(E2)
    same = expert[:, None] == expert[None, :]
    a["groups_before"] = (same & (group[:, None] < group[None, :])).astype(np.float32)
    a["of_expert"] = (expert[:, None] == e8[None, :]).astype(np.float32)
    a["chunks_before"] = np.float32(P) * (e8[:, None] < expert[None, :])
    a["chunks_upto"] = (e8[:, None] <= e8[None, :]).astype(np.float32)
    a["whole"] = np.tile(np.arange(MAX_OF, dtype=np.float32) * P, (E2, 1))
    a["zeros"] = np.zeros((P, C), np.float32)
    a["causal"] = np.where(n[None, :] > n[:, None], np.float32(BIG), np.float32(0))
    a["gates"] = np.concatenate([f("g_xattn"), f("g_ffn")])
    w, b = tr(f("L0_xattn_in_proj_w")), f("L0_xattn_in_proj_b")
    a["l0_wsv"] = np.ascontiguousarray(tr(f("L0_xattn_qkv_w"))[:, 2 * C:])
    a["l0_wso"] = tr(f("L0_xattn_sa_out_w"))
    for k, n in enumerate(("l0_wq", "l0_wk", "l0_wv")):
        a[n] = np.ascontiguousarray(w[:, k * C:(k + 1) * C])
    a["l0_wo"], a["l0_w1"], a["l0_w2"] = (tr(f("L0_xattn_" + n)) for n in ("mha_out_w", "lin1_w", "lin2_w"))
    a["l0_wr"], a["l0_wkk"], a["l0_wvv"] = (tr(f("L0_ffn_" + n)) for n in ("W_r", "W_k", "W_v"))
    a["l1_wq"], a["l1_wk"], a["l1_wv"], a["l1_wo"] = (f("L1_xattn_" + n) for n in ("Wq", "Wk", "Wv", "Wo"))
    a["l1_gate"] = tr(f("L1_ffn_gate_w"))
    a["e_wg"], a["e_wu"], a["e_wd"] = (tr(f("L1_ffn_" + n)) for n in ("Wg", "Wu", "Wd"))
    a["ws_g"], a["ws_u"], a["ws_d"] = (tr(f("L1_ffn_" + n)) for n in ("Ws_g", "Ws_u", "Ws_d"))
    a["l2_wq"] = tr(f("L2_xattn_Wq"))
    a["l2_wk"], a["l2_wv"], a["l2_wo"] = (tr(f("L2_xattn_" + n)) for n in ("Wk", "Wv", "Wo"))
    for l in range(2):
        for n in ("wq", "wk", "wv", "wo"):
            a[f"f{l}_{n}"] = f("L2_ffn_" + n)[l]
        a[f"f{l}_gate"] = f("L2_ffn_gate_w")[l]
    a["moe_gate_b"] = f("L2_ffn_gate_b")
    a["moe_w1"], a["moe_w2"] = f("L2_ffn_e_w1"), f("L2_ffn_e_w2")
    a["moe_b1"] = np.ascontiguousarray(f("L2_ffn_e_b1").reshape(2, E2 * 8, P).transpose(2, 0, 1))
    a["moe_b2"] = np.ascontiguousarray(f("L2_ffn_e_b2").transpose(1, 0, 2))
    a["l3_wq"], a["l3_wk"], a["l3_wv"], a["l3_wo"] = (f("L3_xattn_" + n) for n in ("w_q", "w_k", "w_v", "w_o"))
    for n, m in (("raw_g", "w_gate"), ("raw_u", "w_up"), ("raw_d", "w_down")):
        t = tr(f("L3_ffn_" + m))
        a[n] = np.ascontiguousarray(t.reshape(-1, P, t.shape[1]).transpose(1, 0, 2).reshape(P, -1))
    vec = {"l0_sv": f("L0_xattn_qkv_b")[2 * C:], "l0_bq": b[0:C], "l0_bk": b[C:2 * C],
           "lin1_b": f("L0_xattn_lin1_b"), "mu_r": f("L0_ffn_mu_r"), "mu_k": f("L0_ffn_mu_k"),
           "l1_bq": f("L1_xattn_bq"), "l1_bk": f("L1_xattn_bk"), "l2_bq": f("L2_xattn_bq"),
           "l2_bk": f("L2_xattn_bk")}
    for l in range(2):
        vec[f"f{l}_bq"] = f("L2_ffn_bq")[l]
        vec[f"f{l}_bk"] = f("L2_ffn_bk")[l]
    vec["head_rows"] = np.concatenate([(np.arange(P) // d == h).astype(np.float32)
                                       for d in (16, 32, 64) for h in range(P // d)])
    a["columns"] = np.ascontiguousarray(np.concatenate([columns(vec[n]) for n in COLS], 1))
    r = {"sa_b": f("L0_xattn_sa_out_b"), "ln1_g": f("L0_xattn_ln1_g"), "ln1_b": f("L0_xattn_ln1_b"),
         "l0_bv": b[2 * C:], "l0_bo": f("L0_xattn_mha_out_b"), "ln2_g": f("L0_xattn_ln2_g"),
         "ln2_b": f("L0_xattn_ln2_b"), "lin2_b": f("L0_xattn_lin2_b"), "ln3_g": f("L0_xattn_ln3_g"),
         "ln3_b": f("L0_xattn_ln3_b"), "l1_bv": np.pad(f("L1_xattn_bv"), (0, C - P)), "l1_bo": f("L1_xattn_bo"),
         "l2_bv": f("L2_xattn_bv"), "l2_bo": f("L2_xattn_bo")}
    a["rows"] = np.stack([r[n] for n in ROWS])
    a["rows2"] = np.stack([f("L2_ffn_" + n)[l] for l in range(2) for n in ROWS2])
    return a


def kernel(**inputs):
    import concourse.bacc as bacc
    from concourse.bass_utils import run_bass_kernel_spmd

    nc = bacc.Bacc("TRN2", target_bir_lowering=False, num_devices=1)
    arrays, aps = {}, {}
    for name, a in _lay_out(inputs).items():
        a = np.ascontiguousarray(a)
        arrays["in_" + name] = a
        aps[name] = nc.dram_tensor("in_" + name, a.shape, mybir.dt.from_np(a.dtype), kind="ExternalInput").ap()
    out = nc.dram_tensor("out_x", (B, T, C), F32, kind="ExternalOutput").ap()
    flamingo(nc, aps, out)
    return run_bass_kernel_spmd(nc, [arrays], core_ids=[0]).results[0]["out_x"]
```

```python
from contextlib import ExitStack

import numpy as np

import concourse.bass as bass
from concourse import mybir

F32 = mybir.dt.float32
BF16 = mybir.dt.bfloat16
I32 = mybir.dt.int32
U32 = mybir.dt.uint32
ALU = mybir.AluOpType
ACT = mybir.ActivationFunctionType
AX_X = mybir.AxisListType.X

B, T, C = 8, 112, 256
S2 = 375
P = 128
KC = C // P
LANES = 4
ITERS = B // LANES
TOP2 = 2
PAIRS = B * TOP2
SEQ_ITEMS = LANES * TOP2
SEQ_SLOTS = 4
KEY_TILES, KEY_W = 3, S2 // 3
E1, FE = 16, 512
EX_SLOTS = 4
CAP = T * 2 // E1
HALF_E = E1 // 2
E2, FF = 8, 1024
MAX_OF = -(-B * T // P)
TOK_SLOTS = 4
MAX_CHUNKS = (B * T * TOP2 + E2 * (P - 1)) // P
MIN_TURNS = -(-B * T * TOP2 // (P * TOK_SLOTS))
MAX_TURNS = -(-MAX_CHUNKS // TOK_SLOTS)
EPS = 1e-5
BIG = 1.0e30
ROUND = 1.5 * 2.0 ** 23

ROWS = ["sa_b", "ln1_g", "ln1_b", "l0_bv", "l0_bo", "ln2_g", "ln2_b", "lin2_b", "ln3_g", "ln3_b",
        "l1_bv", "l1_bo", "l2_bv", "l2_bo"]
ROWS2 = ["ln1_w", "ln1_b", "bv", "bo", "ln2_w", "ln2_b"]
COLS = {"l0_sv": 2, "l0_bq": 2, "l0_bk": 2, "lin1_b": 8, "mu_r": 2, "mu_k": 2, "l1_bq": 1, "l1_bk": 1,
        "l2_bq": 2, "l2_bk": 2, "f0_bq": 2, "f0_bk": 2, "f1_bq": 2, "f1_bk": 2,
        "head_rows": 14}


class Signal:

    def __init__(self, sem, base, times, lanes):
        self.sem, self.base, self.times, self.lanes = sem, base, times, lanes

    def at(self, it, r=0, j=0):
        return self.sem, it * (self.times * self.lanes) + (self.base + r * self.lanes + j + 1)


def phase_signals(known, make, turns, one, lanes, times):
    signals = {}
    for name, n in times.items():
        if not n:
            continue
        width = 1 if name in one else lanes
        if name not in known:
            known[name] = [make(name), 0]
        sem, base = known[name]
        signals[name] = Signal(sem, base, n, width)
        known[name][1] = base + turns * n * width
    return signals


class Attention:

    def __init__(self, tiles, heads, d, keys, key_tiles, wq, wk, wv, bq=None, bk=None, bv=None,
                 mask=None, guard=False):
        self.tiles, self.heads, self.d, self.keys, self.key_tiles = tiles, heads, d, keys, key_tiles
        self.key_w = keys // key_tiles
        self.batch = min(4, heads)
        self.masks = None if heads == 1 else {8: 0, 4: 8, 2: 12}[heads]
        self.group = 4 if key_tiles == 1 else 1
        self.groups = heads // self.group
        self.wq, self.wk, self.wv, self.bq, self.bk, self.bv = wq, wk, wv, bq, bk, bv
        self.mask, self.guard, self.scale = mask, guard, float(d) ** -0.5


def flamingo(nc, A, out):
    ctx = ExitStack()
    with ctx:
        def sb(name, shape, dt=F32):
            return ctx.enter_context(nc.sbuf_tensor(name, shape, dt))

        def make(name):
            return ctx.enter_context(nc.semaphore(name))

        known = {}

        def phase(turns, one=(), lanes=LANES, **times):
            return phase_signals(known, make, turns, one, lanes, times)

        bank = [ctx.enter_context(nc.psum_tensor(f"bank{i}", [P, 512], F32)) for i in range(8)]
        bank_s, bank_t = bank[0:4], bank[4:8]
        bank_bf = [b[:, :].bitcast(BF16) for b in bank]

        X = sb("x_state", [T, B, C])
        ident = sb("identity", [P, P])
        ident_bf = sb("identity_bf", [P, P], BF16)
        iota = sb("token_number", [P, 1])
        causal = sb("causal_mask", [T, T])
        gates = sb("tanh_gates", [P, 8])
        cols = sb("columns", [P, sum(COLS.values()) ])
        rows = sb("rows", [P, len(ROWS), C])
        minus_half = sb("minus_half", [P, LANES])
        stats = sb("bn_sums", [T, LANES, 6])
        mv = sb("mean_var", [T, LANES, 2])
        veps = sb("var_eps", [T, LANES])
        rstd = sb("rstd", [T, LANES])
        x_sums = sb("x_bn_sums", [T, LANES, 6])
        x_mv = sb("x_mean_var", [T, LANES, 2])
        x_mean = sb("x_mean", [T, B])
        x_veps = sb("x_var_eps", [T, B])
        x_rstd = sb("x_rstd", [T, B])
        rowmin = sb("rowmin", [T, LANES, 4])
        rowsum = sb("rowsum", [T, LANES, 4])
        rinv = sb("rinv", [T, LANES, 4])
        omu = sb("one_minus_mu", [P, 4])
        one_col = sb("one_column", [P, 1])
        iota8 = sb("expert_number", [T, E2])
        gate_b = sb("moe_gate_bias", [T, 2, E2])
        cw = sb("moe_weight", [T, B, TOP2])
        gsm = sb("gate_small", [T, 8, LANES, E2])
        gix = sb("gate_index", [T, LANES, E2], U32)
        ids = sb("seq_experts", [T, B, TOP2], I32)
        b1q = sb("moe_b1", [P, SEQ_SLOTS, FF // P])
        tok_slot = sb("token_slots", [T, PAIRS], U32)
        tok_ids = sb("chunk_experts", [1, MAX_TURNS * TOK_SLOTS + 1], I32)
        hmean = sb("h_mean", [P, 2, LANES, KC])
        tiny = sb("tiny", [T, 20, LANES])
        wabs = sb("weight_abs", [P, 3, 3])
        region0 = sb("region0", [P, 9728])
        region1 = sb("region1", [P, 8720])
        stream = sb("stream", [P, 8192])
        LB = 4864
        arena = sb("arena", [P, LANES * LB])

        at = {"n": 0}

        def cut(region, words, dt=F32):
            n = at["n"]
            at["n"] = n + words
            ap = region[:, n:n + words]
            return ap if dt == F32 else ap.bitcast(dt)

        def three(ap, k):
            return ap.rearrange("p (k n) -> p k n", k=k)

        w_sv, w_so = three(cut(region0, 512), 2), three(cut(region0, 512), 2)
        w_q0, w_k0, w_v0, w_o0 = (three(cut(region0, 512), 2) for _ in range(4))
        w_l1, w_l2 = three(cut(region0, 2048), 2), three(cut(region0, 2048), 8)
        w_r, w_k, w_v = (three(cut(region0, 512), 2) for _ in range(3))
        w_q1, w_k1, w_v1 = (three(cut(region0, 256), 2) for _ in range(3))
        w_o1 = three(cut(region0, 256), 1)
        assert at["n"] <= 9728
        at["n"] = 0
        w_q3, w_k3, w_v3 = (three(cut(region0, 2048), 2) for _ in range(3))
        w_o3 = three(cut(region0, 2048), 8)
        at["n"] = 0
        w_sg, w_su = three(cut(region1, 1024), 2), three(cut(region1, 1024), 2)
        w_sd = three(cut(region1, 1024), 4)
        w_gate1 = three(cut(region1, 32), 2)
        w_q2, w_k2, w_v2, w_o2 = (three(cut(region1, 512), 2) for _ in range(4))

        def f_weights():
            return [three(cut(region1, 512), 2) for _ in range(4)] + [three(cut(region1, 16), 2)]

        at["n"] = 6656
        w_f = [f_weights()]
        assert at["n"] <= 8720
        at["n"] = 0
        w_f.append(f_weights())
        raw3 = [cut(region1, 2048) for _ in range(3)]
        assert at["n"] <= 8720
        tern = [region1[:, 0:1024].bitcast(BF16), region1[:, 1024:2048].bitcast(BF16), raw3[0][:, 0:1024].bitcast(BF16)]
        w_tg, w_tu, w_td = three(tern[0], 2), three(tern[1], 2), three(tern[2], 8)
        xn, xa, y, xT, cT, qT, kT, V, E, PT, O, wide, ga, accs, qm = ([] for _ in range(15))
        off = {}
        for j in range(LANES):
            at["n"] = j * LB
            xa.append(cut(arena, 256)[0:T, :])
            qm.append(three(arena[:, at["n"]:at["n"] + 4 * T], 4))
            xn.append(cut(arena, 256)[0:T, :])
            y.append(cut(arena, 256)[0:T, :])
            xT.append(three(cut(arena, 2 * T), 2))
            qT.append(three(cut(arena, 2 * T), 2))
            kT.append(cut(arena, S2))
            V.append(three(cut(arena, 3 * P), 3))
            off["e"] = at["n"] - j * LB
            E.append(cut(arena, 4 * T))
            PT.append(cut(arena, 4 * T))
            ga.append(arena[0:T, j * LB + off["e"]:j * LB + off["e"] + 512])
            O.append(cut(arena, P)[0:T, :])
            at["n"] += at["n"] % 2
            off["c"] = at["n"] - j * LB
            cT.append(three(cut(arena, 2 * S2), 2))
            off["w"] = at["n"] - j * LB
            wide.append(cut(arena, 1024))
            accs.append(three(arena[0:T, j * LB + off["w"] + 256:j * LB + off["w"] + 256 + 2 * C], 2))
            assert at["n"] <= (j + 1) * LB, at["n"] - j * LB
        assert 2 * 2 * 4 * T <= off["e"] * 1
        maskb = [w[0:T, 512:512 + S2] for w in wide]
        OT = [three(w[:, 0:8 * T], 8) for w in wide]
        qx = [a[:, 0:128].bitcast(BF16) for a in xa]
        xqT = [three(a[:, 0, :].bitcast(BF16), 2) for a in xT]
        hq = [a[0:T, :, :].rearrange("p k s -> p (k s)")[:, 0:512].bitcast(BF16) for a in cT]
        hqT = [three(arena[:, j * LB + off["e"]:j * LB + off["e"] + 4 * T].bitcast(BF16), 8) for j in range(LANES)]
        h2w = [three(arena[:, j * LB + off["c"]:j * LB + off["c"] + 2 * KC * T], 2) for j in range(LANES)]

        n = off["c"] + 72
        hrow = [three(arena[0:T, j * LB + n:j * LB + n + 2 * C], 2) for j in range(LANES)]
        n += 2 * C
        picks = arena[0:T, n:n + P].rearrange("t (g e) -> t g e", e=E2)
        picks_of = arena[0:T, n:n + P].rearrange("t (b k e) -> t b k e", k=TOP2, e=E2)
        before = arena[0:T, LB + n:LB + n + T]
        steps = arena[0:1, LB + n + T:LB + n + T + 30]
        groups_before = arena[:, 2 * LB + n:2 * LB + n + P]
        n += 3 * LB
        chunks_before = arena[0:E2, n:n + P]
        chunks_upto, whole = arena[0:E2, n + P:n + P + E2], arena[0:E2, n + P + E2:n + P + E2 + MAX_OF]
        of_expert = arena[:, n + P + 15:n + P + 15 + E2]
        assert n + P + 15 + E2 <= 3 * LB + off["w"]
        count = arena[:, 2048:2048 + T]
        place = arena[0:T, LB + 2048:LB + 2048 + P].rearrange("t (g e) -> t g e", e=E2)
        placef = arena[0:T, 2 * LB + 2048:2 * LB + 2048 + PAIRS]
        fill, used = arena[0:E2, 3 * LB + 2048:3 * LB + 2048 + MAX_OF], arena[0:E2, 3 * LB + 2060:3 * LB + 2061]
        held = arena[0:1, 3 * LB + 2100:3 * LB + 2100 + 240].rearrange("o (c e) -> o c e", e=E2)
        idf = arena[0:1, 3 * LB + 2400:3 * LB + 2430]
        tok_hid = [arena[:, s * LB + 2048:s * LB + 2048 + 8 * P] for s in range(2)]
        tok_x = [arena[:, (2 + s) * LB + 2048:(2 + s) * LB + 2048 + C] for s in range(2)]
        tok_xT = [three(arena[:, (2 + s) * LB + 2048 + C:(2 + s) * LB + 2048 + 2 * C], 2) for s in range(2)]
        tok_y = [arena[:, (2 + s % 2) * LB + 2048 + (2 + s // 2) * C:(2 + s % 2) * LB + 2048 + (3 + s // 2) * C]
                 for s in range(TOK_SLOTS)]
        tok_got = stream[0:T, 4096:8192].rearrange("t (i j k c) -> t i j k c", i=ITERS, j=LANES, k=TOP2)

        def col(name, i=0, n=1):
            at_ = 0
            for k, v in COLS.items():
                if k == name:
                    return cols[:, at_ + i:at_ + i + n]
                at_ += v

        def row(name, n=T):
            return rows[0:n, ROWS.index(name), :]

        def row2(l, name, n=T):
            return rows[0:n, l * len(ROWS2) + ROWS2.index(name), :]

        def norm_counts(n, affine, of_x=1):
            return dict(stats_done=n - of_x, var_ready=n - of_x, veps_ready=n - of_x, rstd_ready=n - of_x, normed=n,
                        **({"scaled": affine} if affine else {}))

        def attn_counts(a, n=1):
            g = a.tiles * a.groups * n
            return dict(projected=a.tiles * n, k_out=a.tiles * n, qv_ready=a.tiles * n, k_ready=a.tiles * n, scores=g,
                        q_masked=g * a.group // a.batch if a.heads > 1 else 0, rowmin_ready=g, probs=g, probs_turned=g, probs_T=g, rinv_ready=g * (2 if a.guard else 1), heads_out=g,
                        heads_ready=g, o_turned=a.tiles * n, o_T=a.tiles * n)

        a0 = Attention(2, 4, 32, S2, KEY_TILES, w_q0, w_k0, w_v0, "l0_bq", "l0_bk", row("l0_bv", KEY_W))
        a1 = Attention(1, 1, 128, S2, KEY_TILES, w_q1, w_k1, w_v1, "l1_bq", "l1_bk", row("l1_bv", KEY_W),
                       mask=lambda j: maskb[0], guard=True)
        a2 = Attention(2, 8, 16, S2, KEY_TILES, w_q2, w_k2, w_v2, "l2_bq", "l2_bk", row("l2_bv", KEY_W),
                       mask=lambda j: maskb[j])
        af = [Attention(2, 8, 16, T, 1, w_f[l][0], w_f[l][1], w_f[l][2], f"f{l}_bq", f"f{l}_bk",
                        row2(l, "bv"), mask=lambda j: causal[:, :]) for l in range(2)]
        a3 = Attention(8, 2, 64, S2, KEY_TILES, w_q3, w_k3, w_v3)

        one = ("rstd_ready", "veps_ready")
        use = {k: n * ITERS for n, k in enumerate(("l0x", "l0f", "l1x", "rt", "l2x", "f0", "l3x", "l3f"))}
        s_xst, s_xvar, s_xveps, s_xrstd = (make(n) for n in ("x_summed", "x_var_ready", "x_veps_ready", "x_rstd_ready"))
        p_x = phase(1, x_added=1)
        p_l0x = phase(ITERS, one, **norm_counts(4, 3), turned=3, xT_ready=3, self_v=1, self_vT=1,
                      proj_out=3, part=3, summed=3, x_added=1, hid=1, hid_a=1, hid_b=1, **attn_counts(a0))
        p_l0f = phase(ITERS, one, **norm_counts(1, 0), turned=1, xT_ready=1, mixed_r=1, mixed=1,
                      rk=1, k_relu=1, k_sq=1, sig=1, proj_out=1, gated=1, x_added=1)
        p_l1x = phase(ITERS, one, **norm_counts(1, 0), turned=1, xT_ready=1, proj_out=1, part=1, x_added=1,
                      **attn_counts(a1))
        p_rt = phase(ITERS, one, **norm_counts(1, 0), turned=1, xT_ready=1, xT_spread=1, logits=1, lmax=1,
                     lexp=1, linv=1, scored=1)
        two = dict(lanes=2)
        p_ex = phase(E1 // EX_SLOTS, gu_out=1, e_gelu=1, e_hid=1, e_out=1, e_kept=1, lanes=EX_SLOTS)
        p_sh = phase(B // 2, gu_out=1, e_gelu=1, e_hid=1, e_out=1, added=1, **two)
        p_l2x = phase(ITERS, one, **norm_counts(1, 0), turned=1, xT_ready=1, proj_out=1, part=1, x_added=1,
                      mask_ready=1, **attn_counts(a2))
        p_f, p_m = [], []
        gate_steps = ("g_top", "g_topf", "g_diff", "g_exp", "g_sum", "g_w1", "g_w2", "g_cw")
        for l in range(2):
            p_f.append(phase(ITERS, one + gate_steps + ("ids_ready",), **norm_counts(3 - l, 2, 1 - l), turned=2, xT_ready=2, h_spread=l, h_kept=1 - l,
                             proj_out=1, part=1, summed=1, hmean_sum=l, hmean_ready=l, ids_ready=l, g_out=1, g_val=1,
                             g_maxed=1, g_half=1, cw_turned=1, cwT_ready=1, cw_spread=1, b2_out=1, acc_ready=1,
                             **{n: 1 for n in gate_steps}, **attn_counts(af[l])))
        p_m.append(phase(MAX_TURNS, lanes=1, tok_turned=TOK_SLOTS, tok_xT=TOK_SLOTS, tok_h_out=2 * TOK_SLOTS,
                         tok_gelu=2 * TOK_SLOTS, tok_y_out=TOK_SLOTS, tok_y_kept=TOK_SLOTS))
        p_m.append(phase(ITERS, lanes=1, gu_out=2 * SEQ_ITEMS, e_gelu=2 * SEQ_ITEMS,
                         e_out=SEQ_ITEMS, added=SEQ_ITEMS))
        p_l3x = phase(ITERS, one, **norm_counts(1, 0), turned=1, xT_ready=1, proj_out=1, x_added=1,
                      **attn_counts(a3))
        p_l3f = phase(ITERS, one + ("tiny_done",), **norm_counts(1, 0), amax_ready=3, tiny_done=13, rounded=2,
                      q_ready=2, turned=1, xq_ready=1, g_u_out=2, g_relu=2, g_sq=2, h_part=2, 
                      q2_turned=1, q2T_ready=1, proj_out=1, out_scaled=1, x_added=1)
        (s_const, s_wl0, s_wl1, s_wl3, s_rows2, s_wf1, s_raw3, s_x, s_mask1, s_gates, s_omu, s_half,
         s_mask1b, s_shift0, s_rpe, s_ract, s_topstep, s_sel, s_selTk,
         s_stored, s_rows_in, s_abs, s_wsum, s_wmean, s_tern, s_gadd, s_out) = (make(n) for n in (
             "constants_loaded", "weights_l0_loaded", "weights_l1_l2_loaded", "weights_l3_loaded",
             "rows2_loaded", "weights_f1_loaded", "raw_l3_loaded", "x_loaded", "mask1_loaded",
             "tanh_gates_ready", "one_minus_mu_ready", "constants_set", "mask1_bias_ready",
             "shift_columns_zeroed", "router_products", "router_copies", "top_step_done",
             "selection_ready", "selT_ready",
             "expert_rows_stored", "expert_rows_loaded", "weights_abs_summed", "weights_sum_out",
             "weights_mean_step", "ternary_step", "x_gated_added", "out_stored"))
        s_ctx = [make(f"context_loaded{j}") for j in range(LANES)]
        s_maskl = [make(f"mask_loaded{j}") for j in range(LANES)]
        s_ew = [make(f"expert_weights_loaded{s}") for s in range(EX_SLOTS)]
        s_tw = [make(f"token_moe_weights_loaded{s}") for s in range(TOK_SLOTS)]
        s_xr = [make(f"token_rows_loaded{s}") for s in range(2)]
        s_yst = [make(f"token_outputs_stored{s}") for s in range(2)]
        s_route, s_rmm, s_tokadd, s_scat, s_zero, s_rconst, s_tid, s_picks, s_yg, s_wo0 = (make(n) for n in (
            "routing_step", "routing_products", "token_outputs_added", "token_rows_scattered",
            "token_rows_zeroed", "routing_constants_loaded", "token_experts_ready", "pairs_picked",
            "token_outputs_gathered", "weights_l0_rest_loaded"))
        s_qw = [make(f"seq_moe_weights_loaded{s}") for s in range(SEQ_SLOTS)]

        def wait_first(eng, sem, value):
            eng.wait_ge(sem, value)
            eng.nop(nofuse=True)

        def x_stats(v, u, group, ready=None):
            for j in range(LANES):
                if ready is not None:
                    wait_first(v, *ready(j))
                v.bn_stats(x_sums[:, j, :], x_at(group, j)).then_inc(s_xst, 1)
            for j in range(LANES):
                wait_first(v, s_xst, u * LANES + (j + 1))
                v.bn_aggr(x_mv[:, j, :], x_sums[:, j, :]).then_inc(s_xvar, 1)
            turn_of = bass.ds(group * LANES, LANES)
            wait_first(v, s_xvar, u * LANES + LANES)
            v.tensor_copy(x_mean[:, turn_of], x_mv[:, :, 0])
            v.tensor_scalar(x_veps[:, turn_of], x_mv[:, :, 1], EPS, None, ALU.add).then_inc(s_xveps, 1)

        def x_rstds(g, u, group):
            turn_of = bass.ds(group * LANES, LANES)
            wait_first(g, s_xveps, u + 1)
            g.tensor_tensor(x_rstd[:, turn_of], x_veps[:, turn_of], minus_half[0:T, :], ALU.pow).then_inc(s_xrstd, 1)

        def x_norm(v, k, p, it, dst):
            wait_first(v, s_xrstd, it + (use[k] + 1))
            for j in range(LANES):
                b = it * LANES + j
                v.tensor_scalar(dst(j), x_at(it, j), x_mean[:, bass.ds(b, 1)], x_rstd[:, bass.ds(b, 1)],
                                ALU.subtract, ALU.mult).then_inc(p["normed"].sem, 1)

        def x_stats_ahead(v, k, p, it):
            x_stats(v, it + (use[k] + 1), (ITERS - 1) - it, lambda j: p["x_added"].at(it - 1, 0, j))

        def norm_stats(v, p, it, r, src, ready=None):
            for j in range(LANES):
                if ready is not None:
                    wait_first(v, *ready(j))
                v.bn_stats(stats[:, j, :], src(j)).then_inc(p["stats_done"].sem, 1)
            for j in range(LANES):
                wait_first(v, *p["stats_done"].at(it, r, j))
                v.bn_aggr(mv[:, j, :], stats[:, j, :]).then_inc(p["var_ready"].sem, 1)

        def norm_rstd(g, p, it, r):
            wait_first(g, *p["var_ready"].at(it, r, LANES - 1))
            g.tensor_scalar(veps[:, :], mv[:, :, 1], EPS, None, ALU.add).then_inc(p["veps_ready"].sem, 1)
            g.wait_ge(*p["veps_ready"].at(it, r))
            g.tensor_tensor(rstd[:, :], veps[:, :], minus_half[0:T, :], ALU.pow).then_inc(p["rstd_ready"].sem, 1)

        def norm_apply_affine(v, p, it, r, ra, src, dst, g, b):
            for j in range(LANES):
                v.wait_ge(*p["var_ready"].at(it, r, j))
                v.scalar_tensor_tensor(dst(j), src(j), mv[:, j, 0:1], g, ALU.subtract,
                                       ALU.mult).then_inc(p["scaled"].sem, 1)
            v.wait_ge(*p["rstd_ready"].at(it, r))
            for j in range(LANES):
                v.wait_ge(*p["scaled"].at(it, ra, j))
                v.scalar_tensor_tensor(dst(j), dst(j), rstd[:, j:j + 1], b, ALU.mult,
                                       ALU.add).then_inc(p["normed"].sem, 1)

        def turn(pe, p, it, r, rn, src):
            for j in range(LANES):
                pe.wait_ge(*p["normed"].at(it, rn, j))
                for c in range(KC):
                    last = pe.transpose(bank_t[j][:, c * T:(c + 1) * T], src[j][:, c * P:(c + 1) * P],
                                        ident[0:T, 0:T])
                last.then_inc(p["turned"].sem, 1)

        def keep_turned(act, p, it, r):
            for j in range(LANES):
                act.wait_ge(*p["turned"].at(it, r, j))
                act.copy(xT[j], three(bank_t[j][:, 0:2 * T], 2)).then_inc(p["xT_ready"].sem, 1)

        def matmuls(pe, dst, pairs):
            n = len(pairs)
            for i, (l, r) in enumerate(pairs):
                last = pe.matmul(dst, l, r, start=(i == 0), stop=(i == n - 1))
            return last


        def heads_at(a, j):
            return bank_t[j][0:T, 512 - a.group * a.d:512]

        def attend_tensor(pe, a, p, it, rx, keys_of, keys_ready):
            def project_k(m, j):
                k, f = keys_of(j), slice(m * P, (m + 1) * P)
                matmuls(pe, bank_s[j][:, 0:a.keys], [(a.wk[:, c, f], k[:, c, :]) for c in range(KC)])\
                    .then_inc(p["k_out"].sem, 1)

            def project_qv(m, j):
                k, f = keys_of(j), slice(m * P, (m + 1) * P)
                matmuls(pe, bank_t[j][:, 0:T], [(a.wq[:, c, f], xT[j][:, c, :]) for c in range(KC)])
                for t in range(a.key_tiles):
                    ks = slice(t * a.key_w, (t + 1) * a.key_w)
                    last = matmuls(pe, bank_t[j][0:a.key_w, T + t * P:T + (t + 1) * P],
                                   [(k[:, c, ks], a.wv[:, c, f]) for c in range(KC)])
                last.then_inc(p["projected"].sem, 1)

            def scores_of(m, g, j):
                r, heads = m * a.groups + g, [g * a.group + i for i in range(a.group)]
                if a.heads > 1 and heads[0] % a.batch == 0:
                    pe.wait_ge(*p["q_masked"].at(it, r * a.group // a.batch, j))
                for i, h in enumerate(heads):
                    last = pe.matmul(bank_s[j][0:T, i * a.keys:(i + 1) * a.keys],
                                     qT[j][:, 0, :] if a.heads == 1 else qm[j][:, h % a.batch, :],
                                     kT[j][:, 0:a.keys], start=True, stop=True)
                last.then_inc(p["scores"].sem, 1)

            def outputs_of(m, g, j):
                pe.wait_ge(*p["probs_T"].at(it, m * a.groups + g, j))
                for i in range(a.group):
                    h = g * a.group + i
                    last = matmuls(pe, heads_at(a, j)[:, i * a.d:(i + 1) * a.d],
                                   [(PT[j][0:a.key_w, (i * a.key_tiles + t) * T:(i * a.key_tiles + t + 1) * T],
                                     V[j][0:a.key_w, t, h * a.d:(h + 1) * a.d]) for t in range(a.key_tiles)])
                last.then_inc(p["heads_out"].sem, 1)

            for j in range(LANES):
                pe.wait_ge(*p["xT_ready"].at(it, rx, j))
                if keys_ready is not None:
                    pe.wait_ge(*keys_ready(it, j))
                project_k(0, j)
                project_qv(0, j)
            for m in range(a.tiles):
                for j in range(LANES):
                    pe.wait_ge(*p["qv_ready"].at(it, m, j))
                    pe.wait_ge(*p["k_ready"].at(it, m, j))
                    scores_of(m, 0, j)
                for g in range(a.groups):
                    r = m * a.groups + g
                    for j in range(LANES):
                        pe.wait_ge(*p["probs"].at(it, r, j))
                        if g:
                            pe.wait_ge(*p["heads_ready"].at(it, r - 1, j))
                        for i in range(a.group * a.key_tiles):
                            last = pe.transpose(bank_t[j][0:a.key_w, i * T:(i + 1) * T],
                                                E[j][0:T, i * a.key_w:(i + 1) * a.key_w], ident[0:T, 0:T])
                        last.then_inc(p["probs_turned"].sem, 1)
                        if g + 1 < a.groups:
                            scores_of(m, g + 1, j)
                        elif m + 1 < a.tiles:
                            project_k(m + 1, j)
                        if j:
                            outputs_of(m, g, j - 1)
                    outputs_of(m, g, LANES - 1)
                for j in range(LANES):
                    pe.wait_ge(*p["heads_ready"].at(it, (m + 1) * a.groups - 1, j))
                    pe.transpose(bank_t[j][:, 0:T], O[j], ident[0:T, 0:T]).then_inc(p["o_turned"].sem, 1)
                if m + 1 < a.tiles:
                    for j in range(LANES):
                        pe.wait_ge(*p["o_T"].at(it, m, j))
                        project_qv(m + 1, j)

        def attend_vector(v, a, p, it):
            def mask_and_min(r, j):
                wait_first(v, *p["scores"].at(it, r, j))
                if a.mask is None:
                    last = v.tensor_reduce(rowmin[:, j, 0:1], bank_s[j][0:T, 0:a.keys], AX_X, ALU.min)
                else:
                    for i in range(a.group):
                        ks = slice(i * a.keys, (i + 1) * a.keys)
                        last = nc.vector.tensor_tensor_reduce(
                            out=E[j][0:T, ks], in0=bank_s[j][0:T, ks], in1=a.mask(j), scale=1.0,
                            scalar=3.0e38, op0=ALU.add, op1=ALU.min, accum_out=rowmin[:, j, i:i + 1])
                last.then_inc(p["rowmin_ready"].sem, 1)

            def keep_heads(g, r, j):
                v.wait_ge(*p["heads_out"].at(it, r, j))
                v.wait_ge(*(p["rinv_ready"].at(it, 2 * r + 1, j) if a.guard else p["rinv_ready"].at(it, r, j)))
                dst, ps = O[j][:, g * a.group * a.d:(g + 1) * a.group * a.d], heads_at(a, j)
                if a.group == 1:
                    last = v.tensor_scalar(dst, ps, rinv[:, j, 0:1], None, ALU.mult)
                else:
                    last = v.tensor_tensor(three(dst, a.group), three(ps, a.group),
                                           rinv[:, j, 0:a.group].unsqueeze(2).broadcast_to([T, a.group, a.d]),
                                           ALU.mult)
                last.then_inc(p["heads_ready"].sem, 1)

            for m in range(a.tiles):
                for j in range(LANES):
                    v.wait_ge(*p["projected"].at(it, m, j))
                    ps = bank_t[j][:, 0:T]
                    if a.bq is None:
                        v.tensor_scalar(qT[j][:, 0, :], ps, -a.scale, None, ALU.mult)
                    else:
                        v.tensor_scalar(qT[j][:, 0, :], ps, col(a.bq, m), -a.scale, ALU.add, ALU.mult)
                    vs = three(bank_t[j][0:a.key_w, T:T + a.key_tiles * P], a.key_tiles)
                    vd = V[j][0:a.key_w, 0:a.key_tiles, :]
                    if a.bv is None:
                        last = v.tensor_copy(vd, vs)
                    else:
                        bv = a.bv[0:a.key_w, m * P:(m + 1) * P].unsqueeze(1).broadcast_to([a.key_w, a.key_tiles, P])
                        last = v.tensor_tensor(vd, vs, bv, ALU.add)
                    last.then_inc(p["qv_ready"].sem, 1)
                for j in range(LANES):
                    mask_and_min(m * a.groups, j)
                for g in range(a.groups):
                    r = m * a.groups + g
                    for j in range(LANES):
                        v.wait_ge(*p["probs"].at(it, r, j))
                        v.reciprocal(rinv[:, j, 0:a.group], rowsum[:, j, 0:a.group])\
                            .then_inc(p["rinv_ready"].sem, 1)
                        if g + 1 < a.groups:
                            mask_and_min(r + 1, j)
                        if j and not a.guard:
                            keep_heads(g, r, j - 1)
                    if a.guard:
                        for j in range(LANES):
                            v.wait_ge(*p["rinv_ready"].at(it, 2 * r, j))
                            v.scalar_tensor_tensor(rinv[:, j, 0:1], rowmin[:, j, 0:1], 0.5 * BIG, rinv[:, j, 0:1],
                                                   ALU.is_lt, ALU.mult).then_inc(p["rinv_ready"].sem, 1)
                    for j in range(0 if a.guard else LANES - 1, LANES):
                        keep_heads(g, r, j)

        def attend_scalar(act, a, p, it):
            def keep_k(m, j):
                act.wait_ge(*p["k_out"].at(it, m, j))
                if a.bk is None:
                    last = act.copy(kT[j][:, 0:a.keys], bank_s[j][:, 0:a.keys])
                else:
                    last = act.activation(kT[j][:, 0:a.keys], bank_s[j][:, 0:a.keys], ACT.Identity,
                                          bias=col(a.bk, m))
                last.then_inc(p["k_ready"].sem, 1)

            def exps(r, j):
                act.wait_ge(*p["rowmin_ready"].at(it, r, j))
                for i in range(a.group):
                    ks = slice(i * a.keys, (i + 1) * a.keys)
                    src = bank_s[j] if a.mask is None else E[j]
                    last = act.activation(E[j][0:T, ks], src[0:T, ks], ACT.Exp, bias=rowmin[:, j, i:i + 1],
                                          scale=-1.0, accum_out=rowsum[:, j, i:i + 1])
                last.then_inc(p["probs"].sem, 1)

            def keep_probs(r, j):
                n = a.group * a.key_tiles * T
                act.wait_ge(*p["probs_turned"].at(it, r, j))
                act.copy(PT[j][0:a.key_w, 0:n], bank_t[j][0:a.key_w, 0:n]).then_inc(p["probs_T"].sem, 1)

            for j in range(LANES):
                keep_k(0, j)
            for m in range(a.tiles):
                for j in range(LANES):
                    exps(m * a.groups, j)
                for g in range(a.groups):
                    r = m * a.groups + g
                    keep_probs(r, 0)
                    for j in range(LANES):
                        if j + 1 < LANES:
                            keep_probs(r, j + 1)
                        if g + 1 < a.groups:
                            exps(r + 1, j)
                        elif m + 1 < a.tiles:
                            keep_k(m + 1, j)
                for j in range(LANES):
                    act.wait_ge(*p["o_turned"].at(it, m, j))
                    act.copy(OT[j][:, m, :], bank_t[j][:, 0:T]).then_inc(p["o_T"].sem, 1)

        def attend_gpsimd(g, a, p, it):
            per = a.heads // a.batch
            for m in range(a.tiles):
                for n in range(per):
                    for j in range(LANES):
                        g.wait_ge(*p["qv_ready"].at(it, m, j))
                        if n:
                            g.wait_ge(*p["scores"].at(it, m * a.groups + n * a.batch // a.group - 1, j))
                        rows_of = col("head_rows", a.masks + n * a.batch, a.batch)
                        g.tensor_tensor(qm[j][:, 0:a.batch, :],
                                        qT[j][:, 0:1, :].broadcast_to([P, a.batch, T]),
                                        rows_of.unsqueeze(2).broadcast_to([P, a.batch, T]), ALU.mult)\
                            .then_inc(p["q_masked"].sem, 1)

        def project_out(pe, p, it, r, w, ready):
            for j in range(LANES):
                pe.wait_ge(*ready(j))
                matmuls(pe, bank_s[j][0:T, 0:C], [(OT[j][:, c, :], w[:, c, :]) for c in range(w.shape[1])]) \
                    .then_inc(p["proj_out"].sem, 1)

        def x_at(it, j):
            return X[:, it * LANES + j, :]

        def add_gated(v, p, it, src, gate, ready):
            for j in range(LANES):
                v.wait_ge(*ready(j))
                v.scalar_tensor_tensor(x_at(it, j), src(j), gates[0:T, gate:gate + 1], x_at(it, j), ALU.mult,
                                       ALU.add).then_inc(p["x_added"].sem, 1)

        def add_row(v, p, it, r, b):
            for j in range(LANES):
                v.wait_ge(*p["proj_out"].at(it, r, j))
                v.tensor_tensor(y[j], bank_s[j][0:T, 0:C], b, ALU.add).then_inc(p["part"].sem, 1)

        at["n"] = 0
        xn_all = cut(arena, B * C)[0:T, :].rearrange("t (b c) -> t b c", b=B)
        sel = cut(arena, CAP * P)[0:T, :].rearrange("t (c g) -> t c g", c=CAP)
        selw = cut(arena, CAP * P)[0:T, :].rearrange("t (g c) -> t g c", c=CAP)
        expert_rows = arena[0:T, 0:2 * B * C].rearrange("s (b h f) -> s b h f", b=B, h=2)
        xnT_all = cut(arena, KC * B * T).rearrange("p (k b t) -> p k b t", k=KC, b=B)
        taken = cut(arena, KC * E1 * B * CAP).rearrange("p (k e n) -> p k e n", k=KC, e=E1)
        selT = cut(arena, B * 2 * T)[0:T, :].rearrange("s (b h t) -> s b h t", b=B, h=2)
        eo = cut(arena, E1 * C)[0:T, :].rearrange("s (e c) -> s e c", e=E1)
        hbuf = [cut(arena, 4 * T) for _ in range(2)]
        score = cut(arena, B * E1)[0:T, :].rearrange("t (b e) -> t b e", b=B)
        scoreT, scoreT2 = cut(arena, T), cut(arena, T)
        top16, topi16, topf = cut(arena, 16), cut(arena, 16, U32), cut(arena, CAP)
        rsc = cut(arena, 4 * LANES)[0:T, :].rearrange("t (n j) -> t n j", n=4)
        assert at["n"] <= LANES * LB, at["n"]
        at["n"] = 6144
        rxT = [three(cut(stream, KC * T), KC) for _ in range(LANES)]
        scratch = nc.dram_tensor("expert_out", (E1, B, CAP, C), F32, kind="Internal").ap()

        tok_rows = nc.dram_tensor("token_rows", ((MAX_TURNS * TOK_SLOTS + 2) * P, C), F32, kind="Internal").ap()
        tok_outs = nc.dram_tensor("token_outputs", (MAX_TURNS * TOK_SLOTS * P, C), F32, kind="Internal").ap()

        def expert_slot(s):
            n, region = s % 2 * 3072, stream if s < 2 else region0
            return (three(region[:, n:n + 1024], 2), three(region[:, n + 1024:n + 2048], 2),
                    three(region[:, n + 2048:n + 3072], 4))

        def moe_slot(s):
            if s < 2:
                return (three(stream[:, s * 4096:s * 4096 + 2048], 2),
                        three(stream[:, s * 4096 + 2048:s * 4096 + 4096], 8))
            n = (s - 2) * 2 * LB
            return three(arena[:, n:n + 2048], 2), three(arena[:, n + LB:n + LB + 2048], 8)

        def seq_hid(s):
            return arena[:, s * LB + 2048:s * LB + 2048 + 8 * T]

        ctx_turn = {"l0": 0, "l1": 1, "l2": 2, "l3": 3}

        def ctx_ready(which):
            return lambda it, j: (s_ctx[j], it * 16 + (ctx_turn[which] * ITERS * 16 + 16))

        end = {k: (v.sem, v.base + n) for k, (v, n) in {
            "l0x": (p_l0x["x_added"], B), "l0f": (p_l0f["x_added"], B), "l1x": (p_l1x["x_added"], B),
            "sh": (p_sh["added"], B), "l2x": (p_l2x["x_added"], B), "l3x": (p_l3x["x_added"], B),
            "l3f": (p_l3f["x_added"], B), "f0": (p_f[0]["acc_ready"], B), "f1": (p_f[1]["acc_ready"], B),
            "m1": (p_m[1]["added"], ITERS * SEQ_ITEMS)}.items()}

        block = ctx.enter_context(nc.Block())

        @block.sync
        def _(sp):
            def load(dst, src, s):
                sp.dma_start(dst, src).then_inc(s, 16)

            def weight(dst, name, s):
                load(dst, A[name].rearrange("(k p) n -> p k n", p=P), s)

            def context(which, it, j, before=None):
                if before is not None:
                    sp.wait_ge(*before)
                load(cT[j], A["ctxT"][:, it * LANES + j, :].rearrange("(k p) s -> p k s", p=P), s_ctx[j])

            load(X[:, :, :], A["x"].rearrange("b t c -> t b c"), s_x)
            load(ident[:, :], A["identity"], s_x)
            load(cols[:, :], A["columns"], s_x)
            load(gates[:, :], A["gates"].partition_broadcast(P), s_x)
            for dst, name in ((w_sv, "l0_wsv"), (w_so, "l0_wso")):
                weight(dst, name, s_wl0)
            load(rows[:, :, :], A["rows"].partition_broadcast(P), s_const)
            for dst, name in ((w_q0, "l0_wq"), (w_k0, "l0_wk"), (w_v0, "l0_wv")):
                weight(dst, name, s_wl0)
            for j in range(LANES):
                context("l0", 0, j)
            load(causal[:, :], A["causal"], s_const)
            load(iota[:, :], A["iota"], s_const)
            load(iota8[:, :], A["iota8"].partition_broadcast(T), s_const)
            load(gate_b[:, :, :], A["moe_gate_b"].partition_broadcast(T), s_const)
            for dst, name in ((w_o0, "l0_wo"), (w_l1, "l0_w1"), (w_l2, "l0_w2"), (w_r, "l0_wr"),
                              (w_k, "l0_wkk"), (w_v, "l0_wvv"), (w_q1, "l1_wq"), (w_k1, "l1_wk"),
                              (w_v1, "l1_wv"), (w_o1, "l1_wo")):
                weight(dst, name, s_wo0)
            for dst, name in ((w_sg, "ws_g"), (w_su, "ws_u"), (w_sd, "ws_d"), (w_gate1, "l1_gate"),
                              (w_q2, "l2_wq"), (w_k2, "l2_wk"), (w_v2, "l2_wv"), (w_o2, "l2_wo"),
                              (w_f[0][0], "f0_wq"), (w_f[0][1], "f0_wk"), (w_f[0][2], "f0_wv"),
                              (w_f[0][3], "f0_wo"), (w_f[0][4], "f0_gate")):
                weight(dst, name, s_wl1)

            load(tok_rows.rearrange("(c p) f -> c p f", p=P),
                 A["zeros"].unsqueeze(0).broadcast_to([MAX_TURNS * TOK_SLOTS + 2, P, C]), s_zero)
            n = MIN_TURNS * TOK_SLOTS
            load(tok_outs[n * P:, :].rearrange("(c p) f -> c p f", p=P),
                 A["zeros"].unsqueeze(0).broadcast_to([MAX_TURNS * TOK_SLOTS - n, P, C]), s_zero)

            def expert(e, s):
                wg, wu, wd = expert_slot(s)
                load(wg, A["e_wg"][e].rearrange("(k p) n -> p k n", p=P), s_ew[s])
                load(wu, A["e_wu"][e].rearrange("(k p) n -> p k n", p=P), s_ew[s])
                load(wd, A["e_wd"][e].rearrange("(k p) n -> p k n", p=P), s_ew[s])

            for s in range(2):
                expert(s, s)
            for j in range(LANES):
                context("l0", 1, j, p_l0x["projected"].at(0, a0.tiles - 1, j))
            sp.wait_ge(*end["l0x"])
            load(maskb[0].bitcast(I32), A["mask1"][0], s_mask1)
            sp.wait_ge(*end["l0f"])
            for j in range(LANES):
                context("l1", 0, j)
            for j in range(LANES):
                context("l1", 1, j, p_l1x["projected"].at(0, a1.tiles - 1, j))
            sp.wait_ge(*end["l1x"])
            load(rows[:, 0:2 * len(ROWS2), :], A["rows2"].partition_broadcast(P), s_rows2)
            for e in range(2, EX_SLOTS):
                expert(e, e)
            with sp.Fori(1, E1 // EX_SLOTS) as i:
                for s in range(EX_SLOTS):
                    sp.wait_ge(*p_ex["e_out"].at(i - 1, 0, s))
                    expert(i * EX_SLOTS + s, s)
            sp.wait_ge(s_stored, 16 * E1)
            sp.wait_ge(s_selTk, B)
            for e in range(E1):
                h, i = e // HALF_E, e % HALF_E
                load(expert_rows[i * CAP:(i + 1) * CAP, :, h, :], scratch[e].rearrange("b c f -> c b f"), s_rows_in)

            def chosen(l, s, sem, e):
                w1, w2 = moe_slot(s)
                load(w1, A["moe_w1"][l, bass.ds(e, 1)].rearrange("o (k p) n -> p (o k) n", p=P), sem)
                load(w2, A["moe_w2"][l, bass.ds(e, 1)].rearrange("o (k p) n -> p (o k) n", p=P), sem)
                load(b1q[:, s, :], A["moe_b1"][:, l, bass.ds(e * E2, E2)], sem)

            sp.wait_ge(*end["sh"])
            for it in range(ITERS):
                for j in range(LANES):
                    context("l2", it, j, p_l2x["projected"].at(0, a2.tiles - 1, j) if it else None)
                    if it:
                        sp.wait_ge(*p_l2x["rowmin_ready"].at(0, a2.tiles * a2.groups - 1, j))
                    load(maskb[j].bitcast(I32), A["mask2"][it * LANES + j], s_maskl[j])
            sp.wait_ge(*end["l2x"])
            load(rows[0:E2, 12:14, :], A["moe_b2"], s_rows2)
            load(raw3[0], A["raw_g"], s_raw3)
            load(raw3[1], A["raw_u"], s_raw3)
            for dst, name in ((w_q3, "l3_wq"), (w_k3, "l3_wk"), (w_v3, "l3_wv"), (w_o3, "l3_wo")):
                weight(dst, name, s_wl3)
            for dst, name in ((w_f[1][0], "f1_wq"), (w_f[1][1], "f1_wk"), (w_f[1][2], "f1_wv"),
                              (w_f[1][3], "f1_wo"), (w_f[1][4], "f1_gate")):
                weight(dst, name, s_wf1)
            for dst, name in ((before, "before"), (steps, "steps"), (groups_before, "groups_before"),
                              (chunks_before, "chunks_before"), (chunks_upto, "chunks_upto"), (whole, "whole"),
                              (of_expert, "of_expert")):
                load(dst, A[name], s_rconst)
            sp.wait_ge(*end["f0"])
            def chunk_expert(it, r):
                e = sp.value_load(tok_ids[0:1, bass.ds(it * TOK_SLOTS + r, 1)], min_val=0, max_val=E2 - 1)
                chosen(0, r, s_tw[r], e)

            sp.wait_ge(s_tid, 2)
            turns = sp.value_load(tok_ids[0:1, MAX_TURNS * TOK_SLOTS:MAX_TURNS * TOK_SLOTS + 1], min_val=MIN_TURNS,
                                  max_val=MAX_TURNS)
            chunk_expert(0, 0)
            sp.wait_ge(s_scat, 16 * PAIRS)
            for r in range(1, TOK_SLOTS):
                chunk_expert(0, r)
                sp.wait_ge(s_tw[r], 48)
            load(raw3[2], A["raw_d"], s_raw3)
            with sp.Fori(1, turns) as it:
                for r in range(TOK_SLOTS):
                    sp.wait_ge(*p_m[0]["tok_y_out"].at(it - 1, r))
                    chunk_expert(it, r)

            def seq_expert(it, r):
                e = sp.value_load(ids[0:1, bass.ds(it * LANES + r // TOP2, 1), r % TOP2], min_val=0, max_val=E2 - 1)
                chosen(1, r % SEQ_SLOTS, s_qw[r % SEQ_SLOTS], e)

            for it in range(ITERS):
                sp.wait_ge(*p_f[1]["ids_ready"].at(it))
                for r in range(SEQ_ITEMS):
                    n = it * SEQ_ITEMS + r
                    if n == 1:
                        sp.wait_ge(s_tokadd, PAIRS)
                    if n == 2:
                        sp.wait_ge(*end["f1"])
                    if n >= SEQ_SLOTS:
                        sp.wait_ge(*p_m[1]["e_out"].at(0, n - SEQ_SLOTS))
                    if 2 <= n < SEQ_SLOTS:
                        sp.wait_ge(s_qw[n - 1], 48)
                    seq_expert(it, r)
            sp.wait_ge(*end["m1"])
            for it in range(ITERS):
                for j in range(LANES):
                    context("l3", it, j, p_l3x["projected"].at(0, a3.tiles - 1, j) if it else None)
            for it in range(ITERS):
                for j in range(LANES):
                    sp.wait_ge(*p_l3f["x_added"].at(it, 0, j))
                    b = it * LANES + j
                    load(out[b], X[:, b, :], s_out)
            sp.wait_ge(s_out, 16 * B)

        @block.gpsimd
        def _(g):
            g.memset(minus_half[:, :], -0.5).then_inc(s_half, 1)
            g.memset(one_col[:, :], 1.0).then_inc(s_half, 1)
            g.wait_ge(s_half, 2)

            def chain(p, before, a=None, after=0, name=None):
                with g.Fori(0, ITERS) as it:
                    if name is not None:
                        x_rstds(g, it + (use[name] + 1), (ITERS - 1) - it)
                    for r in range(before):
                        norm_rstd(g, p, it, r)
                    if a is not None:
                        attend_gpsimd(g, a, p, it)
                    for r in range(before, before + after):
                        norm_rstd(g, p, it, r)

            x_rstds(g, use["l0x"], 0)
            chain(p_l0x, 1, a0, 2, "l0x")
            chain(p_l0f, 0, name="l0f")
            chain(p_l1x, 0, name="l1x")
            x_rstds(g, use["rt"] + 1, 1)
            x_rstds(g, use["l2x"], 0)
            chain(p_l2x, 0, a2, name="l2x")
            x_rstds(g, use["f0"] + 1, 1)
            p = p_f[0]
            with g.Fori(0, ITERS) as it:
                norm_rstd(g, p, it, 0)
                attend_gpsimd(g, af[0], p, it)
                norm_rstd(g, p, it, 1)
                for j in range(LANES):
                    g.wait_ge(*p["normed"].at(it, 2, j))
                    g.tensor_copy(hrow[j][:, it, :], xn[j]).then_inc(p["h_kept"].sem, 1)
            g.wait_ge(s_zero, 32)
            g.wait_ge(s_route, 8)
            g.wait_ge(*p["h_kept"].at(ITERS - 1, 0, LANES - 1))
            for b in range(B):
                for k in range(TOP2):
                    n = b * TOP2 + k
                    g.indirect_dma_start(tok_rows, bass.IndirectOffsetOnAxis(ap=tok_slot[:, n:n + 1], axis=0),
                                         hrow[b % LANES][:, b // LANES, :], None).then_inc(s_scat, 16)
            g.wait_ge(s_scat, 16 * PAIRS)
            g.wait_ge(s_tid, 2)
            turns = g.value_load(tok_ids[0:1, MAX_TURNS * TOK_SLOTS:MAX_TURNS * TOK_SLOTS + 1], min_val=MIN_TURNS,
                                 max_val=MAX_TURNS)

            def chunk_rows(it, r):
                g.dma_start(tok_x[r % 2], tok_rows[bass.ds((it * TOK_SLOTS + r) * P, P), :]).then_inc(s_xr[r % 2], 16)

            for r in range(2):
                chunk_rows(0, r)
            with g.Fori(0, turns) as it:
                p = p_m[0]
                for r in range(TOK_SLOTS):
                    wait_first(g, *p["tok_turned"].at(it, r))
                    chunk_rows(it, r + 2)
                    for n in ([r - 1] if r else []) + ([r] if r == TOK_SLOTS - 1 else []):
                        wait_first(g, *p["tok_y_kept"].at(it, n))
                        g.dma_start(tok_outs[bass.ds((it * TOK_SLOTS + n) * P, P), :], tok_y[n])\
                            .then_inc(s_yst[n % 2], 16)
            for s in range(2):
                wait_first(g, s_xr[s], turns * (8 * TOK_SLOTS) + 16)
                wait_first(g, s_yst[s], turns * (8 * TOK_SLOTS))
            for i in range(ITERS):
                for j in range(LANES):
                    for k in range(TOP2):
                        n = (i * LANES + j) * TOP2 + k
                        g.indirect_dma_start(tok_got[:, i, j, k, :], None, tok_outs,
                                             bass.IndirectOffsetOnAxis(ap=tok_slot[:, n:n + 1], axis=0))\
                            .then_inc(s_yg, 16)
                if i + 1 < ITERS:
                    g.wait_ge(s_yg, 16 * SEQ_ITEMS * (i + 1))
            chain(p_f[1], 1, af[1], 1)
            g.wait_ge(s_wmean, 2)
            g.wait_ge(*end["f1"])
            for i in range(3):
                g.tensor_scalar(raw3[i], raw3[i], wabs[:, 2, i:i + 1], ROUND, ALU.mult, ALU.add).then_inc(s_tern, 1)
            for i in range(3):
                g.wait_ge(s_tern, i + 1)
                g.tensor_scalar(raw3[i], raw3[i], -ROUND, 1.0, ALU.add, ALU.min).then_inc(s_tern, 1)
            for i in range(3):
                g.wait_ge(s_tern, 3 + i + 1)
                if i == 2:
                    g.wait_ge(s_tern, 7)
                g.tensor_scalar(tern[i], raw3[i], -1.0, None, ALU.max).then_inc(s_tern, 1)
            x_rstds(g, use["l3x"], 0)
            chain(p_l3x, 0, a3, name="l3x")
            x_rstds(g, use["l3f"] + 1, 1)

        @block.scalar
        def _(act):
            act.wait_ge(s_x, 16 * 4)
            act.activation(gates[:, :], gates[:, :], ACT.Tanh).then_inc(s_gates, 1)

            with act.Fori(0, ITERS) as it:
                p = p_l0x
                keep_turned(act, p, it, 0)
                for j in range(LANES):
                    act.wait_ge(*p["self_v"].at(it, 0, j))
                    for m in range(KC):
                        last = act.activation(qT[j][:, m, :], bank_s[j][:, m * T:(m + 1) * T], ACT.Identity,
                                              bias=col("l0_sv", m))
                    last.then_inc(p["self_vT"].sem, 1)
                keep_turned(act, p, it, 1)
                attend_scalar(act, a0, p, it)
                keep_turned(act, p, it, 2)
                for j in range(LANES):
                    act.wait_ge(*p["hid"].at(it, 0, j))
                    for m in range(0, 4):
                        last = act.activation(OT[j][:, m, :], bank_s[j][:, m * T:(m + 1) * T], ACT.Relu,
                                              bias=col("lin1_b", m))
                    last.then_inc(p["hid_a"].sem, 1)
            with act.Fori(0, ITERS) as it:
                p = p_l0f
                for j in range(LANES):
                    act.wait_ge(*p["turned"].at(it, 0, j))
                    act.copy(cT[j][:, :, 1:T + 1], three(bank_t[j][:, 0:2 * T], 2)).then_inc(p["xT_ready"].sem, 1)
                for j in range(LANES):
                    act.wait_ge(*p["rk"].at(it, 0, j))
                    act.activation(V[j][:, 0:2, 0:T], three(bank_t[j][:, 0:2 * T], 2), ACT.Relu)\
                        .then_inc(p["k_relu"].sem, 1)
                    act.activation(y[j], bank_s[j][0:T, 0:C], ACT.Sigmoid).then_inc(p["sig"].sem, 1)
            with act.Fori(0, ITERS) as it:
                keep_turned(act, p_l1x, it, 0)
                attend_scalar(act, a1, p_l1x, it)
            p = p_rt
            for it in range(ITERS):
                for j in range(LANES):
                    act.wait_ge(*p["turned"].at(it, 0, j))
                    act.copy(rxT[j], three(bank_t[j][:, 0:2 * T], 2)).then_inc(p["xT_ready"].sem, 1)
                for j in range(LANES):
                    b = it * LANES + j
                    act.copy(xnT_all[:, :, b, :], three(bank_t[j][:, 0:2 * T], 2)).then_inc(p["xT_spread"].sem, 1)
                for j in range(LANES):
                    act.wait_ge(*p["lmax"].at(it, 0, j))
                    act.activation(score[:, it * LANES + j, :], bank_s[j][0:T, 0:E1], ACT.Exp,
                                   bias=rsc[:, 0, j:j + 1], accum_out=rsc[:, 1, j:j + 1]).then_inc(p["lexp"].sem, 1)
            act.wait_ge(s_rpe, 1)
            act.copy(scoreT, bank[0][:, 0:T]).then_inc(s_ract, 1)
            for b in range(B):
                act.wait_ge(s_rpe, 2 + b + 1)
                for k in range(KC):
                    last = act.copy(taken[:, k, :, b * CAP:(b + 1) * CAP],
                                    bank[b][:, k * CAP * E1:(k + 1) * CAP * E1].rearrange("p (c e) -> p e c", c=CAP))
                last.then_inc(s_ract, 1)
            with act.Fori(0, E1 // EX_SLOTS) as i:
                for n in range(EX_SLOTS + 1):
                    if n < EX_SLOTS:
                        if n >= 2:
                            act.wait_ge(*p_ex["e_out"].at(i, 0, n - 2))
                        act.wait_ge(*p_ex["gu_out"].at(i, 0, n))
                        act.activation(hbuf[n % 2], bank[n % 2 * 3][:, 0:4 * T], ACT.Gelu)\
                            .then_inc(p_ex["e_gelu"].sem, 1)
                    if n == 0:
                        continue
                    s = n - 1
                    act.wait_ge(*p_ex["e_out"].at(i, 0, s))
                    act.copy(eo[:, i * EX_SLOTS + s, :], bank[s % 2 * 3 + 2][0:T, 0:C]).then_inc(p_ex["e_kept"].sem, 1)
                    act.wait_ge(*p_ex["e_kept"].at(i, 0, s))
                    act.dma_start(scratch[i * EX_SLOTS + s].rearrange("b c f -> (b c) f"), eo[:, i * EX_SLOTS + s, :])\
                        .then_inc(s_stored, 16)
            for b in range(B):
                act.wait_ge(*p_sh["gu_out"].at(b // 2, 0, b % 2))
                act.activation(hbuf[b % 2], bank[3 * (b % 2)][:, 0:4 * T], ACT.Gelu).then_inc(p_sh["e_gelu"].sem, 1)
            with act.Fori(0, ITERS) as it:
                keep_turned(act, p_l2x, it, 0)
                attend_scalar(act, a2, p_l2x, it)
            for l in range(2):
                p = p_f[l]
                with act.Fori(0, ITERS) as it:
                    keep_turned(act, p, it, 0)
                    attend_scalar(act, af[l], p, it)
                    keep_turned(act, p, it, 1)
                    if l == 1:
                        for j in range(LANES):
                            act.copy(h2w[j][:, it, :], bank_t[j][:, 0:2 * T]).then_inc(p["h_spread"].sem, 1)
                    act.wait_ge(*p["g_diff"].at(it))
                    act.activation(tiny[:, 1, :], tiny[:, 0, :], ACT.Exp).then_inc(p["g_exp"].sem, 1)
                    for j in range(LANES):
                        act.wait_ge(*p["cw_turned"].at(it, 0, j))
                        act.copy(E[j][0:E2, 0:T], bank_t[j][0:E2, 0:T]).then_inc(p["cwT_ready"].sem, 1)
                if l == 1:
                    with act.Fori(0, ITERS) as it:
                        for r in range(SEQ_ITEMS):
                            if r >= 2:
                                act.wait_ge(*p_m[1]["e_out"].at(it, r - 2))
                            for m in range(8):
                                if m % 4 == 0:
                                    act.wait_ge(*p_m[1]["gu_out"].at(it, 2 * r + m // 4))
                                last = act.activation(seq_hid(r % 2)[:, m * T:(m + 1) * T],
                                                      bank[r % 2 * 2 + m // 4][:, m % 4 * T:(m % 4 + 1) * T],
                                                      ACT.Gelu, bias=b1q[:, r % SEQ_SLOTS, m:m + 1])
                                if m % 4 == 3:
                                    last.then_inc(p_m[1]["e_gelu"].sem, 1)
                    continue
                act.wait_ge(s_rmm, 1)
                act.copy(count, bank[0][:, 0:T]).then_inc(s_route, 1)
                act.wait_ge(s_tid, 2)
                turns = act.value_load(tok_ids[0:1, MAX_TURNS * TOK_SLOTS:MAX_TURNS * TOK_SLOTS + 1], min_val=MIN_TURNS,
                                       max_val=MAX_TURNS)
                with act.Fori(0, turns) as it:
                    for r in range(TOK_SLOTS):
                        if r >= 2:
                            act.wait_ge(*p_m[0]["tok_y_out"].at(it, r - 2))
                        for m in range(8):
                            if m % 4 == 0:
                                act.wait_ge(*p_m[0]["tok_h_out"].at(it, 2 * r + m // 4))
                            last = act.activation(tok_hid[r % 2][:, m * P:(m + 1) * P],
                                                  bank[r % 2 * 2 + m // 4][:, m % 4 * P:(m % 4 + 1) * P],
                                                  ACT.Gelu, bias=b1q[:, r, m:m + 1])
                            if m % 4 == 3:
                                last.then_inc(p_m[0]["tok_gelu"].sem, 1)
            with act.Fori(0, ITERS) as it:
                keep_turned(act, p_l3x, it, 0)
                attend_scalar(act, a3, p_l3x, it)
            with act.Fori(0, ITERS) as it:
                p = p_l3f
                for h in range(2):
                    for j in range(LANES):
                        act.wait_ge(*p["g_u_out"].at(it, h, j))
                        if h == 1:
                            act.wait_ge(*p["h_part"].at(it, 0, j))
                        act.activation(ga[j], bank_s[j][0:T, :], ACT.Relu).then_inc(p["g_relu"].sem, 1)
                    for j in range(LANES):
                        act.wait_ge(*p["g_relu"].at(it, h, j))
                        act.activation(ga[j], ga[j], ACT.Square).then_inc(p["g_sq"].sem, 1)

        @block.tensor
        def _(pe):
            pe.wait_ge(s_x, 16 * 4)
            pe.wait_ge(s_wl0, 16 * 5)
            with pe.Fori(0, ITERS) as it:
                p = p_l0x
                turn(pe, p, it, 0, 0, xn)
                for j in range(LANES):
                    pe.wait_ge(*p["xT_ready"].at(it, 0, j))
                    for m in range(KC):
                        last = matmuls(pe, bank_s[j][:, m * T:(m + 1) * T],
                                       [(w_sv[:, c, m * P:(m + 1) * P], xT[j][:, c, :]) for c in range(KC)])
                    last.then_inc(p["self_v"].sem, 1)
                for j in range(LANES):
                    pe.wait_ge(*p["self_vT"].at(it, 0, j))
                    matmuls(pe, bank_s[j][0:T, 0:C], [(qT[j][:, c, :], w_so[:, c, :]) for c in range(KC)])\
                        .then_inc(p["proj_out"].sem, 1)
                turn(pe, p, it, 1, 1, xa)
                attend_tensor(pe, a0, p, it, 1, lambda j: cT[j], ctx_ready("l0"))
                pe.wait_ge(s_wo0, 16 * 10)
                project_out(pe, p, it, 1, w_o0, lambda j: p["o_T"].at(it, a0.tiles - 1, j))
                turn(pe, p, it, 2, 2, xn)
                for j in range(LANES):
                    pe.wait_ge(*p["xT_ready"].at(it, 2, j))
                    for m in range(8):
                        dst = (bank_s if m < 4 else bank_t)[j]
                        last = matmuls(pe, dst[:, m % 4 * T:(m % 4 + 1) * T],
                                       [(w_l1[:, c, m * P:(m + 1) * P], xT[j][:, c, :]) for c in range(KC)])
                    last.then_inc(p["hid"].sem, 1)
                pe.wait_ge(*p["hid_b"].at(it, 0, LANES - 1))
                project_out(pe, p, it, 2, w_l2, lambda j: p["hid_a"].at(it, 0, j))
            with pe.Fori(0, ITERS) as it:
                p = p_l0f
                turn(pe, p, it, 0, 0, xn)
                for j in range(LANES):
                    pe.wait_ge(*p["mixed"].at(it, 0, j))
                    mr, mk = qT[j], three(PT[j][:, 0:2 * T], 2)
                    matmuls(pe, bank_s[j][0:T, 0:C], [(mr[:, c, :], w_r[:, c, :]) for c in range(KC)])
                    for m in range(KC):
                        last = matmuls(pe, bank_t[j][:, m * T:(m + 1) * T],
                                       [(w_k[:, c, m * P:(m + 1) * P], mk[:, c, :]) for c in range(KC)])
                    last.then_inc(p["rk"].sem, 1)
                pe.wait_ge(*p["sig"].at(it, 0, LANES - 1))
                project_out(pe, p, it, 0, w_v, lambda j: p["k_sq"].at(it, 0, j))
            with pe.Fori(0, ITERS) as it:
                p = p_l1x
                turn(pe, p, it, 0, 0, xn)
                attend_tensor(pe, a1, p, it, 0, lambda j: cT[j], ctx_ready("l1"))
                project_out(pe, p, it, 0, w_o1, lambda j: p["o_T"].at(it, a1.tiles - 1, j))
            pe.wait_ge(s_wl1, 16 * 13)
            p = p_rt
            for it in range(ITERS):
                for j in range(LANES):
                    pe.wait_ge(*p["normed"].at(it, 0, j))
                    for c in range(KC):
                        last = pe.transpose(bank_t[j][:, c * T:(c + 1) * T],
                                            xn_all[:, it * LANES + j, c * P:(c + 1) * P], ident[0:T, 0:T])
                    last.then_inc(p["turned"].sem, 1)
                for j in range(LANES):
                    pe.wait_ge(*p["xT_ready"].at(it, 0, j))
                    matmuls(pe, bank_s[j][0:T, 0:E1], [(rxT[j][:, c, :], w_gate1[:, c, :]) for c in range(KC)])\
                        .then_inc(p["logits"].sem, 1)
                pe.wait_ge(*p["xT_spread"].at(it, 0, LANES - 1))
                pe.wait_ge(*p["lexp"].at(it, 0, LANES - 1))
            pe.wait_ge(*p["scored"].at(ITERS - 1, 0, LANES - 1))
            pe.transpose(bank[0][:, 0:T], score.rearrange("t b e -> t (b e)"), ident[0:T, 0:T]).then_inc(s_rpe, 1)
            pe.wait_ge(s_topstep, 7)
            for c in range(CAP):
                last = pe.matmul(bank[4 + c // 4][0:T, c % 4 * P:(c % 4 + 1) * P],
                                 topf[:, c:c + 1].broadcast_to([P, T]), ident[:, :], start=True, stop=True)
            last.then_inc(s_rpe, 1)
            for b in range(B):
                if b == 0:
                    pe.wait_ge(s_sel, 4)
                for k in range(KC):
                    last = pe.matmul(bank[b][:, k * CAP * E1:(k + 1) * CAP * E1], xn_all[:, b, k * P:(k + 1) * P],
                                     sel[:, :, b * E1:(b + 1) * E1], start=True, stop=True)
                last.then_inc(s_rpe, 1)
            pe.wait_ge(s_sel, 5)
            for b in range(B):
                pe.wait_ge(s_ract, 1 + b + 1)
                for h in range(2):
                    g0 = b * E1 + h * HALF_E
                    last = pe.transpose(bank[b][0:T, h * T:(h + 1) * T],
                                        selw[:, g0:g0 + HALF_E, :].rearrange("t e c -> t (e c)"), ident[0:T, 0:T])
                last.then_inc(s_rpe, 1)

            def gate_up(s, wg, wu, rhs, sig):
                for dst, w in ((bank[3 * s], wg), (bank[3 * s + 1], wu)):
                    for m in range(4):
                        last = matmuls(pe, dst[:, m * T:(m + 1) * T],
                                       [(w[:, c, m * P:(m + 1) * P], rhs(c)) for c in range(KC)])
                last.then_inc(sig.sem, 1)

            pe.wait_ge(s_selTk, B)
            with pe.Fori(0, E1 // EX_SLOTS) as i:
                for n in range(EX_SLOTS + 1):
                    if n < EX_SLOTS:
                        pe.wait_ge(s_ew[n], i * 48 + 48)
                        if n >= 2:
                            pe.wait_ge(*p_ex["e_hid"].at(i, 0, n - 2))
                        wg, wu, wd = expert_slot(n)
                        gate_up(n % 2, wg, wu, lambda c: taken[:, c, i * EX_SLOTS + n, :], p_ex["gu_out"])
                    if n == 0:
                        continue
                    s = n - 1
                    wg, wu, wd = expert_slot(s)
                    if s >= 2:
                        pe.wait_ge(*p_ex["e_kept"].at(i, 0, s - 2))
                    pe.wait_ge(*p_ex["e_hid"].at(i, 0, s))
                    matmuls(pe, bank[s % 2 * 3 + 2][0:T, 0:C],
                            [(hbuf[s % 2][:, m * T:(m + 1) * T], wd[:, m, :]) for m in range(4)])\
                        .then_inc(p_ex["e_out"].sem, 1)
                pe.wait_ge(*p_ex["e_kept"].at(i, 0, EX_SLOTS - 1))
            for i in range(B // 2):
                for s in range(2):
                    b = 2 * i + s
                    gate_up(s, w_sg, w_su, lambda c: xnT_all[:, c, b, :], p_sh["gu_out"])
                for s in range(2):
                    b = 2 * i + s
                    if b == 0:
                        pe.wait_ge(s_rows_in, 16 * E1)
                    pe.wait_ge(*p_sh["e_hid"].at(i, 0, s))
                    matmuls(pe, bank[3 * s + 2][0:T, 0:C],
                            [(hbuf[s][:, m * T:(m + 1) * T], w_sd[:, m, :]) for m in range(4)]
                            + [(selT[:, b, h, :], expert_rows[:, b, h, :]) for h in range(2)])\
                        .then_inc(p_sh["e_out"].sem, 1)
                pe.wait_ge(*p_sh["added"].at(i, 0, 1))
            with pe.Fori(0, ITERS) as it:
                p = p_l2x
                turn(pe, p, it, 0, 0, xn)
                attend_tensor(pe, a2, p, it, 0, lambda j: cT[j], ctx_ready("l2"))
                project_out(pe, p, it, 0, w_o2, lambda j: p["o_T"].at(it, a2.tiles - 1, j))
            for l in range(2):
                p = p_f[l]
                if l == 1:
                    pe.wait_ge(s_wf1, 80)
                with pe.Fori(0, ITERS) as it:
                    turn(pe, p, it, 0, 1 - l, xn)
                    attend_tensor(pe, af[l], p, it, 0, lambda j: xT[j], None)
                    project_out(pe, p, it, 0, w_f[l][3], lambda j: p["o_T"].at(it, af[l].tiles - 1, j))
                    turn(pe, p, it, 1, 2 - l, xn)
                    for j in range(LANES):
                        pe.wait_ge(*(p["xT_ready"].at(it, 1, j) if l == 0 else p["hmean_ready"].at(it, 0, j)))
                        lhs = [xT[j][:, c, :] if l == 0 else hmean[:, 1, j, c:c + 1].broadcast_to([P, T])
                               for c in range(KC)]
                        matmuls(pe, bank_s[j][0:T, 0:E2], [(lhs[c], w_f[l][4][:, c, :]) for c in range(KC)])\
                            .then_inc(p["g_out"].sem, 1)
                    for j in range(LANES):
                        pe.wait_ge(*p["g_cw"].at(it))
                        if l == 1:
                            pe.wait_ge(*p["h_spread"].at(it, 0, j))
                        pe.transpose(bank_t[j][0:E2, 0:T], gsm[:, 4, j, :], ident[0:T, 0:T]).then_inc(p["cw_turned"].sem, 1)
                    for j in range(LANES):
                        if j == 0:
                            pe.wait_ge(s_rows2, 32)
                        pe.wait_ge(*p["cwT_ready"].at(it, 0, j))
                        matmuls(pe, bank_s[j][0:T, 0:C], [(E[j][0:E2, 0:T], rows[0:E2, 12 + l, :])])\
                            .then_inc(p["b2_out"].sem, 1)
                pe.wait_ge(*end[f"f{l}"])

                if l == 1:
                    p = p_m[1]

                    def pair_hidden(it, r):
                        w1, _ = moe_slot(r % SEQ_SLOTS)
                        pe.wait_ge(s_qw[r % SEQ_SLOTS], it * (48 * SEQ_ITEMS // SEQ_SLOTS)
                                   + 48 * (r // SEQ_SLOTS + 1))
                        for half in range(2):
                            if r >= 2:
                                pe.wait_ge(*p["e_gelu"].at(it, 2 * (r - 2) + half))
                            for m in range(4 * half, 4 * half + 4):
                                last = matmuls(pe, bank[r % 2 * 2 + half][:, m % 4 * T:(m % 4 + 1) * T],
                                               [(w1[:, c, m * P:(m + 1) * P],
                                                 h2w[r // TOP2][:, bass.ds(it, 1), c * T:(c + 1) * T])
                                                for c in range(KC)])
                            last.then_inc(p["gu_out"].sem, 1)

                    def pair_outputs(it, r):
                        _, w2 = moe_slot(r % SEQ_SLOTS)
                        if r >= 2:
                            pe.wait_ge(*p["added"].at(it, r - 2))
                        pe.wait_ge(*p["e_gelu"].at(it, 2 * r + 1))
                        matmuls(pe, bank[4 + r % 2][0:T, 0:C],
                                [(seq_hid(r % 2)[:, m * T:(m + 1) * T], w2[:, m, :]) for m in range(8)])\
                            .then_inc(p["e_out"].sem, 1)

                    with pe.Fori(0, ITERS) as it:
                        pair_hidden(it, 0)
                        for r in range(SEQ_ITEMS):
                            if r + 1 < SEQ_ITEMS:
                                pair_hidden(it, r + 1)
                            pair_outputs(it, r)
                        pe.wait_ge(*p["added"].at(it, SEQ_ITEMS - 1))
                    continue

                p = p_m[0]
                picked = picks.rearrange("t g e -> t (g e)")
                pe.wait_ge(s_picks, ITERS * TOP2)
                pe.matmul(bank[0][:, 0:T], picked, one_col[0:T, 0:1].broadcast_to([T, T]), start=True,
                          stop=True).then_inc(s_rmm, 1)
                pe.wait_ge(s_route, 1)
                pe.wait_ge(s_rconst, 16 * 7)
                pe.matmul(bank[1][0:E2, 0:T], of_expert, count, start=True, stop=True).then_inc(s_rmm, 1)
                pe.wait_ge(s_route, 3)
                pe.matmul(bank[2][0:T, 0:P], before, picked, start=True, stop=False)
                pe.matmul(bank[2][0:T, 0:P], count, groups_before, start=False, stop=False)
                pe.matmul(bank[2][0:T, 0:P], used.broadcast_to([E2, T]), chunks_before, start=False,
                          stop=True).then_inc(s_rmm, 1)
                pe.matmul(bank[3][0:T, 0:E2], used.broadcast_to([E2, T]), chunks_upto, start=True,
                          stop=True).then_inc(s_rmm, 1)

                def turn_rows(it, r):
                    pe.wait_ge(s_xr[r % 2], it * (8 * TOK_SLOTS) + (r // 2 + 1) * 16)
                    for c in range(KC):
                        last = pe.transpose(bank[6 + r % 2][:, c * P:(c + 1) * P], tok_x[r % 2][:, c * P:(c + 1) * P],
                                            ident[:, :])
                    last.then_inc(p["tok_turned"].sem, 1)

                def chunk_hidden(it, r):
                    w1, _ = moe_slot(r)
                    pe.wait_ge(s_tw[r], it * 48 + 48)
                    pe.wait_ge(*p["tok_xT"].at(it, r))
                    for half in range(2):
                        if r >= 2:
                            pe.wait_ge(*p["tok_gelu"].at(it, 2 * (r - 2) + half))
                        for m in range(4 * half, 4 * half + 4):
                            last = matmuls(pe, bank[r % 2 * 2 + half][:, m % 4 * P:(m % 4 + 1) * P],
                                           [(w1[:, c, m * P:(m + 1) * P], tok_xT[r % 2][:, c, :])
                                            for c in range(KC)])
                        last.then_inc(p["tok_h_out"].sem, 1)

                def chunk_outputs(it, r):
                    _, w2 = moe_slot(r)
                    if r >= 2:
                        pe.wait_ge(*p["tok_y_kept"].at(it, r - 2))
                    pe.wait_ge(*p["tok_gelu"].at(it, 2 * r + 1))
                    matmuls(pe, bank[4 + r % 2][:, 0:C],
                            [(tok_hid[r % 2][:, m * P:(m + 1) * P], w2[:, m, :]) for m in range(8)])\
                        .then_inc(p["tok_y_out"].sem, 1)

                pe.wait_ge(s_tid, 2)
                turns = pe.value_load(tok_ids[0:1, MAX_TURNS * TOK_SLOTS:MAX_TURNS * TOK_SLOTS + 1], min_val=MIN_TURNS,
                                      max_val=MAX_TURNS)
                with pe.Fori(0, turns) as it:
                    turn_rows(it, 0)
                    turn_rows(it, 1)
                    chunk_hidden(it, 0)
                    for r in range(TOK_SLOTS):
                        if r + 1 < TOK_SLOTS:
                            chunk_hidden(it, r + 1)
                        if r + 2 < TOK_SLOTS:
                            turn_rows(it, r + 2)
                        chunk_outputs(it, r)
                    pe.wait_ge(*p["tok_y_kept"].at(it, TOK_SLOTS - 1))
                pe.wait_ge(s_abs, 3)
                pe.wait_ge(s_half, 2)
                pe.matmul(bank[5][:, 0:3], one_col[:, 0:1].broadcast_to([P, P]), wabs[:, 0, :], start=True,
                          stop=True).then_inc(s_wsum, 1)
                pe.wait_ge(s_wmean, 1)
            pe.wait_ge(s_wl3, 64)
            with pe.Fori(0, ITERS) as it:
                p = p_l3x
                turn(pe, p, it, 0, 0, xn)
                attend_tensor(pe, a3, p, it, 0, lambda j: cT[j], ctx_ready("l3"))
                project_out(pe, p, it, 0, w_o3, lambda j: p["o_T"].at(it, a3.tiles - 1, j))
            pe.wait_ge(s_tern, 9)
            with pe.Fori(0, ITERS) as it:
                p = p_l3f
                for j in range(LANES):
                    pe.wait_ge(*p["q_ready"].at(it, 0, j))
                    for c in range(KC):
                        last = pe.transpose(bank_bf[4 + j][:, c * T:(c + 1) * T],
                                            qx[j][:, c * P:(c + 1) * P], ident_bf[0:T, 0:T])
                    last.then_inc(p["turned"].sem, 1)
                for h in range(2):
                    for j in range(LANES):
                        if h == 0:
                            pe.wait_ge(*p["xq_ready"].at(it, 0, j))
                        else:
                            pe.wait_ge(*p["h_part"].at(it, 0, j))
                        for dst, w in ((bank_s[j], w_tg), (bank_t[j], w_tu)):
                            last = matmuls(pe, dst[0:T, :], [(xqT[j][:, c, :], w[:, c, h * 512:(h + 1) * 512])
                                                             for c in range(KC)])
                        last.then_inc(p["g_u_out"].sem, 1)
                for j in range(LANES):
                    pe.wait_ge(*p["q_ready"].at(it, 1, j))
                    for c in range(8):
                        last = pe.transpose(bank_bf[j][:, c * T:(c + 1) * T], hq[j][:, c * P:(c + 1) * P],
                                            ident_bf[0:T, 0:T])
                    last.then_inc(p["q2_turned"].sem, 1)
                for j in range(LANES):
                    pe.wait_ge(*p["q2T_ready"].at(it, 0, j))
                    matmuls(pe, bank_t[j][0:T, 0:C], [(hqT[j][:, c, :], w_td[:, c, :]) for c in range(8)])\
                        .then_inc(p["proj_out"].sem, 1)

        @block.vector
        def _(v):
            v.wait_ge(s_x, 16 * 4)
            v.tensor_copy(ident_bf[:, :], ident[:, :]).then_inc(p_x["x_added"].sem, LANES)
            v.tensor_scalar(omu[:, :], col("mu_r", 0, 4), -1.0, 1.0, ALU.mult, ALU.add).then_inc(s_omu, 1)
            v.wait_ge(s_gates, 1)
            x_stats(v, use["l0x"], 0)
            with v.Fori(0, ITERS) as it:
                p = p_l0x
                x_norm(v, "l0x", p, it, lambda j: xn[j])
                x_stats_ahead(v, "l0x", p, it)
                v.wait_ge(s_const, 16 * 5)
                add_row(v, p, it, 0, row("sa_b"))
                for j in range(LANES):
                    v.wait_ge(*p["part"].at(it, 0, j))
                    v.tensor_tensor(y[j], y[j], xn[j], ALU.add).then_inc(p["summed"].sem, 1)
                norm_stats(v, p, it, 0, lambda j: y[j], lambda j: p["summed"].at(it, 0, j))
                norm_apply_affine(v, p, it, 0, 0, lambda j: y[j], lambda j: xa[j], row("ln1_g"), row("ln1_b"))
                attend_vector(v, a0, p, it)
                add_row(v, p, it, 1, row("l0_bo"))
                for j in range(LANES):
                    v.wait_ge(*p["part"].at(it, 1, j))
                    v.tensor_tensor(y[j], y[j], xa[j], ALU.add).then_inc(p["summed"].sem, 1)
                norm_stats(v, p, it, 1, lambda j: y[j], lambda j: p["summed"].at(it, 1, j))
                norm_apply_affine(v, p, it, 1, 1, lambda j: y[j], lambda j: xn[j], row("ln2_g"), row("ln2_b"))
                for j in range(LANES):
                    v.wait_ge(*p["hid"].at(it, 0, j))
                    for m in range(4, 8):
                        last = v.tensor_scalar(OT[j][:, m, :], bank_t[j][:, (m - 4) * T:(m - 3) * T],
                                               col("lin1_b", m), 0.0, ALU.add, ALU.max)
                    last.then_inc(p["hid_b"].sem, 1)
                add_row(v, p, it, 2, row("lin2_b"))
                for j in range(LANES):
                    v.wait_ge(*p["part"].at(it, 2, j))
                    v.tensor_tensor(y[j], y[j], xn[j], ALU.add).then_inc(p["summed"].sem, 1)
                norm_stats(v, p, it, 2, lambda j: y[j], lambda j: p["summed"].at(it, 2, j))
                norm_apply_affine(v, p, it, 2, 2, lambda j: y[j], lambda j: xa[j], row("ln3_g"), row("ln3_b"))
                add_gated(v, p, it, lambda j: xa[j], 0, lambda j: p["normed"].at(it, 3, j))
            v.wait_ge(*end["l0x"])
            for j in range(LANES):
                v.memset(cT[j][:, :, 0:1], 0.0).then_inc(s_shift0, 1)
            v.wait_ge(s_shift0, LANES)
            v.wait_ge(s_omu, 1)
            with v.Fori(0, ITERS) as it:
                p = p_l0f
                x_norm(v, "l0f", p, it, lambda j: xn[j])
                x_stats_ahead(v, "l0f", p, it)
                for j in range(LANES):
                    v.wait_ge(*p["xT_ready"].at(it, 0, j))
                    for i in range(4):
                        last = v.tensor_scalar(E[j][:, i * T:(i + 1) * T], cT[j][:, i % 2, 0:T], omu[:, i:i + 1],
                                               None, ALU.mult)
                    last.then_inc(p["mixed_r"].sem, 1)
                for j in range(LANES):
                    v.wait_ge(*p["mixed_r"].at(it, 0, j))
                    for i in range(4):
                        dst = qT[j][:, i, :] if i < 2 else PT[j][:, (i - 2) * T:(i - 1) * T]
                        last = v.scalar_tensor_tensor(dst, cT[j][:, i % 2, 1:T + 1], col("mu_r", i),
                                                      E[j][:, i * T:(i + 1) * T], ALU.mult, ALU.add)
                    last.then_inc(p["mixed"].sem, 1)
                for j in range(LANES):
                    v.wait_ge(*p["k_relu"].at(it, 0, j))
                    v.tensor_tensor(OT[j][:, 0:2, :], V[j][:, 0:2, 0:T], V[j][:, 0:2, 0:T], ALU.mult)\
                        .then_inc(p["k_sq"].sem, 1)
                for j in range(LANES):
                    v.wait_ge(*p["proj_out"].at(it, 0, j))
                    v.wait_ge(*p["sig"].at(it, 0, j))
                    v.tensor_tensor(xa[j], y[j], bank_s[j][0:T, 0:C], ALU.mult).then_inc(p["gated"].sem, 1)
                add_gated(v, p, it, lambda j: xa[j], 4, lambda j: p["gated"].at(it, 0, j))
            v.wait_ge(*end["l0f"])
            v.wait_ge(s_mask1, 16)
            v.tensor_scalar(maskb[0], maskb[0].bitcast(I32), 0.0, BIG, ALU.is_equal, ALU.mult).then_inc(s_mask1b, 1)
            v.wait_ge(s_mask1b, 1)
            with v.Fori(0, ITERS) as it:
                p = p_l1x
                x_norm(v, "l1x", p, it, lambda j: xn[j])
                x_stats_ahead(v, "l1x", p, it)
                attend_vector(v, a1, p, it)
                add_row(v, p, it, 0, row("l1_bo"))
                add_gated(v, p, it, lambda j: y[j], 1, lambda j: p["part"].at(it, 0, j))
            p = p_rt
            v.wait_ge(*end["l1x"])
            for it in range(ITERS):
                x_norm(v, "rt", p, it, lambda j: xn_all[:, it * LANES + j, :])
                if it == 0:
                    x_stats(v, use["rt"] + 1, 1)
                for j in range(LANES):
                    v.wait_ge(*p["logits"].at(it, 0, j))
                    v.tensor_reduce(rsc[:, 0, j:j + 1], bank_s[j][0:T, 0:E1], AX_X, ALU.max, negate=True)\
                        .then_inc(p["lmax"].sem, 1)
                for j in range(LANES):
                    v.wait_ge(*p["lexp"].at(it, 0, j))
                    v.reciprocal(rsc[:, 2, j:j + 1], rsc[:, 1, j:j + 1]).then_inc(p["linv"].sem, 1)
                for j in range(LANES):
                    v.wait_ge(*p["linv"].at(it, 0, j))
                    v.tensor_scalar(score[:, it * LANES + j, :], score[:, it * LANES + j, :], rsc[:, 2, j:j + 1],
                                    None, ALU.mult).then_inc(p["scored"].sem, 1)
            v.wait_ge(s_ract, 1)
            v.max(top16[:, 0:8], scoreT).then_inc(s_topstep, 1)
            v.wait_ge(s_topstep, 1)
            v.match_replace(scoreT2, top16[:, 0:8], scoreT, -1.0).then_inc(s_topstep, 1)
            v.max_index(topi16[:, 0:8], top16[:, 0:8], scoreT).then_inc(s_topstep, 1)
            v.wait_ge(s_topstep, 2)
            v.max(top16[:, 8:16], scoreT2).then_inc(s_topstep, 1)
            v.wait_ge(s_topstep, 4)
            v.max_index(topi16[:, 8:16], top16[:, 8:16], scoreT2).then_inc(s_topstep, 1)
            v.tensor_copy(topf[:, 0:8], topi16[:, 0:8]).then_inc(s_topstep, 1)
            v.wait_ge(s_topstep, 6)
            v.tensor_copy(topf[:, 8:CAP], topi16[:, 8:CAP]).then_inc(s_topstep, 1)
            v.wait_ge(s_rpe, 2)
            for k in range(4):
                n = min(4, CAP - 4 * k)
                v.tensor_scalar(sel[:, 4 * k:4 * k + n, :], three(bank[4 + k][0:T, 0:n * P], n), iota[0:T, 0:1],
                                None, ALU.is_equal).then_inc(s_sel, 1)
            v.wait_ge(s_sel, 4)
            v.tensor_tensor(selw.rearrange("t g c -> t c g"), sel, score.rearrange("t b e -> t (b e)").unsqueeze(1).broadcast_to([T, CAP, P]),
                            ALU.mult).then_inc(s_sel, 1)
            for b in range(B):
                v.wait_ge(s_rpe, 2 + B + b + 1)
                v.tensor_copy(selT[:, b, :, :], three(bank[b][0:T, 0:2 * T], 2)).then_inc(s_selTk, 1)
            with v.Fori(0, E1 // EX_SLOTS) as i:
                for s in range(EX_SLOTS):
                    v.wait_ge(*p_ex["e_gelu"].at(i, 0, s))
                    v.tensor_tensor(hbuf[s % 2], hbuf[s % 2], bank[s % 2 * 3 + 1][:, 0:4 * T], ALU.mult).then_inc(p_ex["e_hid"].sem, 1)
            for i in range(B // 2):
                for s in range(2):
                    v.wait_ge(*p_sh["e_gelu"].at(i, 0, s))
                    v.tensor_tensor(hbuf[s], hbuf[s], bank[3 * s + 1][:, 0:4 * T], ALU.mult).then_inc(p_sh["e_hid"].sem, 1)
                for s in range(2):
                    b = 2 * i + s
                    v.wait_ge(*p_sh["e_out"].at(i, 0, s))
                    v.scalar_tensor_tensor(X[:, b, :], bank[3 * s + 2][0:T, 0:C], gates[0:T, 5:6], X[:, b, :],
                                           ALU.mult, ALU.add).then_inc(p_sh["added"].sem, 1)
                if i == 1:
                    x_stats(v, use["l2x"], 0, lambda j: p_sh["added"].at(j // 2, 0, j % 2))
            v.wait_ge(*end["sh"])
            with v.Fori(0, ITERS) as it:
                p = p_l2x
                x_norm(v, "l2x", p, it, lambda j: xn[j])
                x_stats_ahead(v, "l2x", p, it)
                for j in range(LANES):
                    v.wait_ge(s_maskl[j], it * 16 + 16)
                    v.tensor_scalar(maskb[j], maskb[j].bitcast(I32), 0.0, BIG, ALU.is_equal, ALU.mult)\
                        .then_inc(p["mask_ready"].sem, 1)
                v.wait_ge(*p["mask_ready"].at(it, 0, LANES - 1))
                attend_vector(v, a2, p, it)
                add_row(v, p, it, 0, row("l2_bo"))
                add_gated(v, p, it, lambda j: y[j], 2, lambda j: p["part"].at(it, 0, j))
            v.wait_ge(*end["l2x"])
            x_stats(v, use["f0"] + 1, 1)
            for l in range(2):
                p = p_f[l]
                v.wait_ge(s_rows2, 16 if l == 0 else 32)
                with v.Fori(0, ITERS) as it:
                    acc = lambda j: accs[j][:, it, :]
                    if l == 0:
                        x_norm(v, "f0", p, it, acc)
                    else:
                        v.wait_ge(s_yg, it * (16 * SEQ_ITEMS) + 16 * SEQ_ITEMS)
                        for k in range(TOP2):
                            for j in range(LANES):
                                if k:
                                    v.wait_ge(s_tokadd, it * SEQ_ITEMS + (j + 1))
                                v.scalar_tensor_tensor(acc(j), tok_got[:, it, j, k, :],
                                                       cw[:, bass.ds(it * LANES + j, 1), k], acc(j), ALU.mult,
                                                       ALU.add).then_inc(s_tokadd, 1)
                    norm_stats(v, p, it, 0, acc, (lambda j: p["normed"].at(it, 0, j)) if l == 0 else
                               lambda j: (s_tokadd, it * SEQ_ITEMS + (LANES + j + 1)))
                    norm_apply_affine(v, p, it, 0, 0, acc, lambda j: xn[j], row2(l, "ln1_w"), row2(l, "ln1_b"))
                    attend_vector(v, af[l], p, it)
                    add_row(v, p, it, 0, row2(l, "bo"))
                    for j in range(LANES):
                        v.wait_ge(*p["part"].at(it, 0, j))
                        v.tensor_tensor(acc(j), acc(j), y[j], ALU.add).then_inc(p["summed"].sem, 1)
                    norm_stats(v, p, it, 1, acc, lambda j: p["summed"].at(it, 0, j))
                    norm_apply_affine(v, p, it, 1, 1, acc, lambda j: xn[j], row2(l, "ln2_w"), row2(l, "ln2_b"))
                    if l == 1:
                        for j in range(LANES):
                            v.wait_ge(*p["xT_ready"].at(it, 1, j))
                            v.tensor_reduce(hmean[:, 0, j, :], xT[j], AX_X, ALU.add).then_inc(p["hmean_sum"].sem, 1)
                        for j in range(LANES):
                            v.wait_ge(*p["hmean_sum"].at(it, 0, j))
                            v.tensor_scalar(hmean[:, 1, j, :], hmean[:, 0, j, :], 1.0 / T, None, ALU.mult)\
                                .then_inc(p["hmean_ready"].sem, 1)
                    for j in range(LANES):
                        v.wait_ge(*p["g_out"].at(it, 0, j))
                        v.tensor_tensor(gsm[:, 0, j, :], bank_s[j][0:T, 0:E2], gate_b[:, l, :], ALU.add)\
                            .then_inc(p["g_val"].sem, 1)
                    for j in range(LANES):
                        wait_first(v, *p["g_val"].at(it, 0, j))
                        v.max(gsm[:, 1, j, :], gsm[:, 0, j, :]).then_inc(p["g_maxed"].sem, 1)
                    for j in range(LANES):
                        wait_first(v, *p["g_maxed"].at(it, 0, j))
                        last = v.max_index(gix[:, j, :], gsm[:, 1, j, :], gsm[:, 0, j, :])
                    last.then_inc(p["g_top"].sem, 1)
                    v.tensor_tensor(tiny[:, 0, :], gsm[:, 1, :, 1], gsm[:, 1, :, 0], ALU.subtract)\
                        .then_inc(p["g_diff"].sem, 1)
                    v.wait_ge(*p["g_top"].at(it))
                    v.tensor_copy(gsm[:, 5, :, :], gix[:, :, :]).then_inc(p["g_topf"].sem, 1)
                    v.wait_ge(*p["g_exp"].at(it))
                    v.tensor_scalar(tiny[:, 2, :], tiny[:, 1, :], 1.0, None, ALU.add).then_inc(p["g_sum"].sem, 1)
                    v.wait_ge(*p["g_sum"].at(it))
                    v.reciprocal(tiny[:, 3, :], tiny[:, 2, :]).then_inc(p["g_w1"].sem, 1)
                    v.wait_ge(*p["g_w1"].at(it))
                    v.tensor_tensor(tiny[:, 4, :], tiny[:, 3, :], tiny[:, 1, :], ALU.mult).then_inc(p["g_w2"].sem, 1)
                    v.wait_ge(*p["g_w2"].at(it))
                    v.wait_ge(*p["g_topf"].at(it))
                    for j in range(LANES):
                        for k in range(2):
                            last = v.tensor_scalar(gsm[:, 2 + k, j, :], iota8[:, :], gsm[:, 5, j, k:k + 1],
                                                   tiny[:, 3 + k, j:j + 1], ALU.is_equal, ALU.mult)
                        last.then_inc(p["g_half"].sem, 1)
                    v.wait_ge(*p["g_half"].at(it, 0, LANES - 1))
                    v.tensor_tensor(gsm[:, 4, :, :], gsm[:, 2, :, :], gsm[:, 3, :, :], ALU.add).then_inc(p["g_cw"].sem, 1)
                    v.wait_ge(*p["g_cw"].at(it))
                    v.tensor_copy(cw[:, bass.ds(it * LANES, LANES), :],
                                  tiny[:, 3:3 + TOP2, :].rearrange("t k j -> t j k"))\
                        .then_inc(p["cw_spread"].sem, LANES)
                    if l == 0:
                        for k in range(TOP2):
                            v.tensor_tensor(picks_of[:, bass.ds(it * LANES, LANES), k, :],
                                            iota8[:, :].unsqueeze(1).broadcast_to([T, LANES, E2]),
                                            gsm[:, 5, :, k:k + 1].broadcast_to([T, LANES, E2]),
                                            ALU.is_equal).then_inc(s_picks, 1)
                    else:
                        v.tensor_copy(ids[:, bass.ds(it * LANES, LANES), :], gix[:, :, 0:TOP2])\
                            .then_inc(p["ids_ready"].sem, 1)
                    for j in range(LANES):
                        v.wait_ge(*p["b2_out"].at(it, 0, j))
                        if l == 0:
                            v.wait_ge(*p["h_kept"].at(it, 0, j))
                        v.tensor_tensor(acc(j), acc(j), bank_s[j][0:T, 0:C], ALU.add).then_inc(p["acc_ready"].sem, 1)
                v.wait_ge(*p["cw_spread"].at(ITERS - 1, 0, LANES - 1))
                v.wait_ge(*end[f"f{l}"])
                if l == 1:
                    with v.Fori(0, ITERS) as it:
                        for r in range(SEQ_ITEMS):
                            j, k = r // TOP2, r % TOP2
                            v.wait_ge(*p_m[1]["e_out"].at(it, r))
                            if k:
                                v.wait_ge(*p_m[1]["added"].at(it, r - 1))
                            dst = accs[j][:, it, :]
                            v.scalar_tensor_tensor(dst, bank[4 + r % 2][0:T, 0:C],
                                                   cw[:, bass.ds(it * LANES + j, 1), k], dst, ALU.mult, ALU.add)\
                                .then_inc(p_m[1]["added"].sem, 1)
                    v.wait_ge(*end["m1"])
                    continue
                v.wait_ge(s_rmm, 2)
                v.tensor_scalar(fill, whole, bank[1][0:E2, 0:1], None, ALU.is_lt).then_inc(s_route, 1)
                v.wait_ge(s_route, 2)
                v.tensor_reduce(used, fill, AX_X, ALU.add).then_inc(s_route, 1)
                v.wait_ge(s_rmm, 4)
                n = MAX_TURNS * TOK_SLOTS
                v.tensor_tensor(held[:, 0:n, :], bank[3][0:1, 0:E2].unsqueeze(1).broadcast_to([1, n, E2]),
                                steps[:, 0:n].unsqueeze(2).broadcast_to([1, n, E2]), ALU.is_le).then_inc(s_route, 1)
                v.tensor_scalar(held[:, n:n + 1, 0:MAX_TURNS].rearrange("o c e -> o (c e)"), steps[:, n:n + MAX_TURNS],
                                bank[3][0:1, E2 - 1:E2], None, ALU.is_lt).then_inc(s_route, 1)
                v.tensor_tensor(place, bank[2][0:T, 0:P].rearrange("t (g e) -> t g e", e=E2), picks, ALU.mult)\
                    .then_inc(s_route, 1)
                v.wait_ge(s_route, 5)
                v.tensor_reduce(idf[:, 0:n], held[:, 0:n, :], AX_X, ALU.add)
                v.tensor_reduce(idf[:, n:n + 1], held[:, n, 0:MAX_TURNS], AX_X, ALU.add).then_inc(s_tid, 1)
                v.wait_ge(s_route, 6)
                v.tensor_reduce(placef, place, AX_X, ALU.add).then_inc(s_route, 1)
                v.wait_ge(s_tid, 1)
                v.tensor_scalar(tok_ids[:, :], idf[:, 0:n + 1], float(E2 - 1), None, ALU.min).then_inc(s_tid, 1)
                v.wait_ge(s_route, 7)
                v.tensor_copy(tok_slot[:, :], placef).then_inc(s_route, 1)
                v.wait_ge(s_tid, 2)
                turns = v.value_load(tok_ids[0:1, n:n + 1], min_val=MIN_TURNS, max_val=MAX_TURNS)
                with v.Fori(0, turns) as it:
                    p = p_m[0]

                    def keep_rows(r):
                        v.wait_ge(*p["tok_turned"].at(it, r))
                        if r >= 2:
                            v.wait_ge(*p["tok_h_out"].at(it, 2 * (r - 2) + 1))
                        v.tensor_copy(tok_xT[r % 2], three(bank[6 + r % 2][:, 0:C], 2)).then_inc(p["tok_xT"].sem, 1)

                    keep_rows(0)
                    keep_rows(1)
                    for r in range(TOK_SLOTS):
                        if r + 2 < TOK_SLOTS:
                            keep_rows(r + 2)
                        v.wait_ge(*p["tok_y_out"].at(it, r))
                        if r >= 2:
                            v.wait_ge(s_yst[r % 2], it * (8 * TOK_SLOTS) + r // 2 * 16)
                        v.tensor_copy(tok_y[r], bank[4 + r % 2][:, 0:C]).then_inc(p["tok_y_kept"].sem, 1)
                v.wait_ge(s_raw3, 48)
                for i in range(3):
                    v.tensor_reduce(wabs[:, 0, i:i + 1], raw3[i], AX_X, ALU.add, apply_absolute_value=True)\
                        .then_inc(s_abs, 1)
                v.wait_ge(s_wsum, 1)
                v.tensor_scalar(wabs[:, 1, :], bank[5][:, 0:3], 1.0 / (C * FF), EPS, ALU.mult, ALU.max).then_inc(s_wmean, 1)
                v.wait_ge(s_wmean, 1)
                v.reciprocal(wabs[:, 2, :], wabs[:, 1, :]).then_inc(s_wmean, 1)
            for b in range(B):
                dst = X[:, b, :]
                v.scalar_tensor_tensor(dst, accs[b % LANES][:, b // LANES, :], gates[0:T, 6:7], dst,
                                       ALU.mult, ALU.add).then_inc(s_gadd, 1)
                if b == LANES - 1:
                    x_stats(v, use["l3x"], 0, lambda j: (s_gadd, j + 1))
            v.wait_ge(s_gadd, B)
            with v.Fori(0, ITERS) as it:
                p = p_l3x
                x_norm(v, "l3x", p, it, lambda j: xn[j])
                x_stats_ahead(v, "l3x", p, it)
                attend_vector(v, a3, p, it)
                add_gated(v, p, it, lambda j: bank_s[j][0:T, 0:C], 3, lambda j: p["proj_out"].at(it, 0, j))
            v.wait_ge(*end["l3x"])
            x_stats(v, use["l3f"] + 1, 1)
            with v.Fori(0, ITERS) as it:
                p = p_l3f
                x_norm(v, "l3f", p, it, lambda j: xn[j])
                for j in range(LANES):
                    v.wait_ge(*p["normed"].at(it, 0, j))
                    v.tensor_reduce(tiny[:, 0, j:j + 1], xn[j], AX_X, ALU.max, apply_absolute_value=True)\
                        .then_inc(p["amax_ready"].sem, 1)
                v.wait_ge(*p["amax_ready"].at(it, 0, LANES - 1))
                v.tensor_scalar(tiny[:, 1, :], tiny[:, 0, :], EPS, None, ALU.max).then_inc(p["tiny_done"].sem, 1)
                v.wait_ge(*p["tiny_done"].at(it, 0))
                v.reciprocal(tiny[:, 2, :], tiny[:, 1, :]).then_inc(p["tiny_done"].sem, 1)
                v.tensor_scalar(tiny[:, 4, :], tiny[:, 1, :], 1.0 / 127.0, wabs[0:T, 1, 0:1], ALU.mult, ALU.mult)\
                    .then_inc(p["tiny_done"].sem, 1)
                v.tensor_scalar(tiny[:, 5, :], tiny[:, 1, :], 1.0 / 127.0, wabs[0:T, 1, 1:2], ALU.mult, ALU.mult)\
                    .then_inc(p["tiny_done"].sem, 1)
                v.wait_ge(*p["tiny_done"].at(it, 1))
                v.tensor_scalar(tiny[:, 3, :], tiny[:, 2, :], 127.0, None, ALU.mult).then_inc(p["tiny_done"].sem, 1)
                v.wait_ge(*p["tiny_done"].at(it, 3))
                v.tensor_tensor(tiny[:, 6, :], tiny[:, 4, :], tiny[:, 4, :], ALU.mult).then_inc(p["tiny_done"].sem, 1)
                v.wait_ge(*p["tiny_done"].at(it, 5))
                v.tensor_tensor(tiny[:, 7, :], tiny[:, 6, :], tiny[:, 5, :], ALU.mult).then_inc(p["tiny_done"].sem, 1)
                for j in range(LANES):
                    v.tensor_scalar(y[j], xn[j], tiny[:, 3, j:j + 1], ROUND, ALU.mult, ALU.add).then_inc(p["rounded"].sem, 1)
                for j in range(LANES):
                    v.wait_ge(*p["rounded"].at(it, 0, j))
                    v.tensor_scalar(qx[j], y[j], ROUND, 127.0, ALU.subtract, ALU.min).then_inc(p["q_ready"].sem, 1)
                for j in range(LANES):
                    v.wait_ge(*p["turned"].at(it, 0, j))
                    v.tensor_scalar(xqT[j], three(bank_bf[4 + j][:, 0:2 * T], 2), -128.0, None, ALU.max)\
                        .then_inc(p["xq_ready"].sem, 1)
                for h in range(2):
                    for j in range(LANES):
                        v.wait_ge(*p["g_sq"].at(it, h, j))
                        v.tensor_tensor(wide[j][0:T, h * 512:(h + 1) * 512], ga[j], bank_t[j][0:T, :], ALU.mult)\
                            .then_inc(p["h_part"].sem, 1)
                    for j in range(LANES):
                        v.wait_ge(*p["h_part"].at(it, h, j))
                        v.tensor_reduce(tiny[:, 8 + 6 * h, j:j + 1], wide[j][0:T, h * 512:(h + 1) * 512], AX_X, ALU.max,
                                        apply_absolute_value=True).then_inc(p["amax_ready"].sem, 1)
                v.wait_ge(*p["amax_ready"].at(it, 2, LANES - 1))
                v.tensor_tensor(tiny[:, 15, :], tiny[:, 8, :], tiny[:, 14, :], ALU.max).then_inc(p["tiny_done"].sem, 1)
                v.wait_ge(*p["tiny_done"].at(it, 7))
                v.tensor_tensor(tiny[:, 9, :], tiny[:, 15, :], tiny[:, 7, :], ALU.mult).then_inc(p["tiny_done"].sem, 1)
                v.wait_ge(*p["tiny_done"].at(it, 8))
                v.tensor_scalar(tiny[:, 10, :], tiny[:, 9, :], EPS, None, ALU.max).then_inc(p["tiny_done"].sem, 1)
                v.wait_ge(*p["tiny_done"].at(it, 9))
                v.reciprocal(tiny[:, 11, :], tiny[:, 10, :]).then_inc(p["tiny_done"].sem, 1)
                v.tensor_scalar(tiny[:, 13, :], tiny[:, 10, :], 1.0 / 127.0, wabs[0:T, 1, 2:3], ALU.mult, ALU.mult)\
                    .then_inc(p["tiny_done"].sem, 1)
                v.wait_ge(*p["tiny_done"].at(it, 10))
                v.scalar_tensor_tensor(tiny[:, 12, :], tiny[:, 11, :], 127.0, tiny[:, 7, :], ALU.mult, ALU.mult)\
                    .then_inc(p["tiny_done"].sem, 1)
                v.wait_ge(*p["tiny_done"].at(it, 12))
                for j in range(LANES):
                    v.tensor_scalar(wide[j][0:T, :], wide[j][0:T, :], tiny[:, 12, j:j + 1], ROUND, ALU.mult, ALU.add)\
                        .then_inc(p["rounded"].sem, 1)
                for j in range(LANES):
                    v.wait_ge(*p["rounded"].at(it, 1, j))
                    v.tensor_scalar(hq[j], wide[j][0:T, :], ROUND, 127.0, ALU.subtract, ALU.min)\
                        .then_inc(p["q_ready"].sem, 1)
                for j in range(LANES):
                    v.wait_ge(*p["q2_turned"].at(it, 0, j))
                    v.tensor_scalar(hqT[j], three(bank_bf[j][:, 0:8 * T], 8), -128.0, None, ALU.max)\
                        .then_inc(p["q2T_ready"].sem, 1)
                for j in range(LANES):
                    v.wait_ge(*p["proj_out"].at(it, 0, j))
                    v.tensor_scalar(y[j], bank_t[j][0:T, 0:C], tiny[:, 13, j:j + 1], gates[0:T, 7:8], ALU.mult,
                                    ALU.mult).then_inc(p["out_scaled"].sem, 1)
                for j in range(LANES):
                    v.wait_ge(*p["out_scaled"].at(it, 0, j))
                    v.tensor_tensor(x_at(it, j), x_at(it, j), y[j], ALU.add).then_inc(p["x_added"].sem, 1)


def _lay_out(i):
    f = lambda n: np.asarray(i[n])
    tr = lambda a: np.ascontiguousarray(np.swapaxes(a, -1, -2))
    columns = lambda v: v.reshape(-1, P).T

    a = {"x": f("x"), "ctxT": np.ascontiguousarray(f("ctx_1024").transpose(2, 0, 1)),
         "mask1": f("mask_1xSxS2_ik0"), "mask2": f("mask_BxSxS2_ik1")}
    a["identity"] = np.eye(P, dtype=np.float32)
    a["iota"] = np.arange(P, dtype=np.float32).reshape(P, 1)
    a["iota8"] = np.arange(E2, dtype=np.float32)
    n = np.arange(T)
    a["before"] = (n[:, None] < n[None, :]).astype(np.float32)
    a["steps"] = np.concatenate([np.arange(MAX_TURNS * TOK_SLOTS), np.arange(MAX_TURNS) * TOK_SLOTS])\
        .astype(np.float32)[None]
    group, expert, e8 = np.arange(P) // E2, np.arange(P) % E2, np.arange(E2)
    same = expert[:, None] == expert[None, :]
    a["groups_before"] = (same & (group[:, None] < group[None, :])).astype(np.float32)
    a["of_expert"] = (expert[:, None] == e8[None, :]).astype(np.float32)
    a["chunks_before"] = np.float32(P) * (e8[:, None] < expert[None, :])
    a["chunks_upto"] = (e8[:, None] <= e8[None, :]).astype(np.float32)
    a["whole"] = np.tile(np.arange(MAX_OF, dtype=np.float32) * P, (E2, 1))
    a["zeros"] = np.zeros((P, C), np.float32)
    a["causal"] = np.where(n[None, :] > n[:, None], np.float32(BIG), np.float32(0))
    a["gates"] = np.concatenate([f("g_xattn"), f("g_ffn")])
    w, b = tr(f("L0_xattn_in_proj_w")), f("L0_xattn_in_proj_b")
    a["l0_wsv"] = np.ascontiguousarray(tr(f("L0_xattn_qkv_w"))[:, 2 * C:])
    a["l0_wso"] = tr(f("L0_xattn_sa_out_w"))
    for k, n in enumerate(("l0_wq", "l0_wk", "l0_wv")):
        a[n] = np.ascontiguousarray(w[:, k * C:(k + 1) * C])
    a["l0_wo"], a["l0_w1"], a["l0_w2"] = (tr(f("L0_xattn_" + n)) for n in ("mha_out_w", "lin1_w", "lin2_w"))
    a["l0_wr"], a["l0_wkk"], a["l0_wvv"] = (tr(f("L0_ffn_" + n)) for n in ("W_r", "W_k", "W_v"))
    a["l1_wq"], a["l1_wk"], a["l1_wv"], a["l1_wo"] = (f("L1_xattn_" + n) for n in ("Wq", "Wk", "Wv", "Wo"))
    a["l1_gate"] = tr(f("L1_ffn_gate_w"))
    a["e_wg"], a["e_wu"], a["e_wd"] = (tr(f("L1_ffn_" + n)) for n in ("Wg", "Wu", "Wd"))
    a["ws_g"], a["ws_u"], a["ws_d"] = (tr(f("L1_ffn_" + n)) for n in ("Ws_g", "Ws_u", "Ws_d"))
    a["l2_wq"] = tr(f("L2_xattn_Wq"))
    a["l2_wk"], a["l2_wv"], a["l2_wo"] = (tr(f("L2_xattn_" + n)) for n in ("Wk", "Wv", "Wo"))
    for l in range(2):
        for n in ("wq", "wk", "wv", "wo"):
            a[f"f{l}_{n}"] = f("L2_ffn_" + n)[l]
        a[f"f{l}_gate"] = f("L2_ffn_gate_w")[l]
    a["moe_gate_b"] = f("L2_ffn_gate_b")
    a["moe_w1"], a["moe_w2"] = f("L2_ffn_e_w1"), f("L2_ffn_e_w2")
    a["moe_b1"] = np.ascontiguousarray(f("L2_ffn_e_b1").reshape(2, E2 * 8, P).transpose(2, 0, 1))
    a["moe_b2"] = np.ascontiguousarray(f("L2_ffn_e_b2").transpose(1, 0, 2))
    a["l3_wq"], a["l3_wk"], a["l3_wv"], a["l3_wo"] = (f("L3_xattn_" + n) for n in ("w_q", "w_k", "w_v", "w_o"))
    for n, m in (("raw_g", "w_gate"), ("raw_u", "w_up"), ("raw_d", "w_down")):
        t = tr(f("L3_ffn_" + m))
        a[n] = np.ascontiguousarray(t.reshape(-1, P, t.shape[1]).transpose(1, 0, 2).reshape(P, -1))
    vec = {"l0_sv": f("L0_xattn_qkv_b")[2 * C:], "l0_bq": b[0:C], "l0_bk": b[C:2 * C],
           "lin1_b": f("L0_xattn_lin1_b"), "mu_r": f("L0_ffn_mu_r"), "mu_k": f("L0_ffn_mu_k"),
           "l1_bq": f("L1_xattn_bq"), "l1_bk": f("L1_xattn_bk"), "l2_bq": f("L2_xattn_bq"),
           "l2_bk": f("L2_xattn_bk")}
    for l in range(2):
        vec[f"f{l}_bq"] = f("L2_ffn_bq")[l]
        vec[f"f{l}_bk"] = f("L2_ffn_bk")[l]
    vec["head_rows"] = np.concatenate([(np.arange(P) // d == h).astype(np.float32)
                                       for d in (16, 32, 64) for h in range(P // d)])
    a["columns"] = np.ascontiguousarray(np.concatenate([columns(vec[n]) for n in COLS], 1))
    r = {"sa_b": f("L0_xattn_sa_out_b"), "ln1_g": f("L0_xattn_ln1_g"), "ln1_b": f("L0_xattn_ln1_b"),
         "l0_bv": b[2 * C:], "l0_bo": f("L0_xattn_mha_out_b"), "ln2_g": f("L0_xattn_ln2_g"),
         "ln2_b": f("L0_xattn_ln2_b"), "lin2_b": f("L0_xattn_lin2_b"), "ln3_g": f("L0_xattn_ln3_g"),
         "ln3_b": f("L0_xattn_ln3_b"), "l1_bv": np.pad(f("L1_xattn_bv"), (0, C - P)), "l1_bo": f("L1_xattn_bo"),
         "l2_bv": f("L2_xattn_bv"), "l2_bo": f("L2_xattn_bo")}
    a["rows"] = np.stack([r[n] for n in ROWS])
    a["rows2"] = np.stack([f("L2_ffn_" + n)[l] for l in range(2) for n in ROWS2])
    return a


def kernel(**inputs):
    import concourse.bacc as bacc
    from concourse.bass_utils import run_bass_kernel_spmd

    nc = bacc.Bacc("TRN2", target_bir_lowering=False, num_devices=1)
    arrays, aps = {}, {}
    for name, a in _lay_out(inputs).items():
        a = np.ascontiguousarray(a)
        arrays["in_" + name] = a
        aps[name] = nc.dram_tensor("in_" + name, a.shape, mybir.dt.from_np(a.dtype), kind="ExternalInput").ap()
    out = nc.dram_tensor("out_x", (B, T, C), F32, kind="ExternalOutput").ap()
    flamingo(nc, aps, out)
    return run_bass_kernel_spmd(nc, [arrays], core_ids=[0]).results[0]["out_x"]
```
